# Optimizing a Trainium2 kernel written in Bass

```python
import numpy as np
import jax
import jax.numpy as jnp

def _softmax(x, axis=-1):
    return jax.nn.softmax(x, axis=axis)

def _gelu(x):
    return jax.nn.gelu(x, approximate=True)

def _silu(x):
    return jax.nn.silu(x)

def _sigmoid(x):
    return jax.nn.sigmoid(x)

def _layernorm(x, axis=-1, eps=1e-05):
    m = jnp.mean(x, axis=axis, keepdims=True)
    v = jnp.var(x, axis=axis, keepdims=True)
    return (x - m) / jnp.sqrt(v + eps)

def _scatter_add(tgt, idx, src, axis=0):
    return tgt.at[idx].add(src)

def _segment_sum(src, seg, n):
    return jax.ops.segment_sum(src, seg, n)
kernel_name = 'mk_seq_preln_d2_jaxref_r8_23ad2f'

def setup_inputs(seed: int=0):
    np.random.seed(seed)
    _w = jnp.asarray

    def _L0_attn_setup():
        import jax, jax.numpy as jnp
        import numpy as np
        WS = 64
        LB = 1
        LF = 1
        H = 16
        NC = LB + LF + 1

        def _collect(a, pad_value):
            nw = a.shape[1]
            pads = [(0, 0), (LB, LF)] + [(0, 0)] * (a.ndim - 2)
            ap = jnp.pad(a, pads, constant_values=pad_value)
            idx = jnp.arange(nw)[:, None] + jnp.arange(NC)[None, :]
            g = ap[:, idx]
            return g.reshape(g.shape[0], nw, NC * a.shape[2], *a.shape[3:])
        key = jax.random.key(seed)
        ks = jax.random.split(key, 9)
        B, S, E = (1, 512, 128)
        x = jax.random.normal(ks[0], (B, S, E), dtype=jnp.float32)
        std = 0.02
        wq = std * jax.random.normal(ks[1], (E, E), dtype=jnp.float32)
        wk = std * jax.random.normal(ks[2], (E, E), dtype=jnp.float32)
        wv = std * jax.random.normal(ks[3], (E, E), dtype=jnp.float32)
        wo = std * jax.random.normal(ks[4], (E, E), dtype=jnp.float32)
        bq = std * jax.random.normal(ks[5], (E,), dtype=jnp.float32)
        bk = std * jax.random.normal(ks[6], (E,), dtype=jnp.float32)
        bv = std * jax.random.normal(ks[7], (E,), dtype=jnp.float32)
        bo = std * jax.random.normal(ks[8], (E,), dtype=jnp.float32)
        return {'x': x, 'wq': wq, 'bq': bq, 'wk': wk, 'bk': bk, 'wv': wv, 'bv': bv, 'wo': wo, 'bo': bo}
    _L0_attn_in = _L0_attn_setup()

    def _L0_ffn_setup():
        import jax, jax.numpy as jnp
        import numpy as np
        EPS = 1e-05

        def _layernorm(x, w, b):
            mu = jnp.mean(x, axis=-1, keepdims=True)
            var = jnp.mean((x - mu) ** 2, axis=-1, keepdims=True)
            return (x - mu) * jax.lax.rsqrt(var + EPS) * w + b

        def _rope_tables(T, D, base=10000.0):
            inv_freq = 1.0 / base ** (jnp.arange(0, D, 2, dtype=jnp.float32) / D)
            t = jnp.arange(T, dtype=jnp.float32)
            freqs = jnp.einsum('i,j->ij', t, inv_freq)
            emb = jnp.concatenate([freqs, freqs], axis=-1)
            return (jnp.cos(emb), jnp.sin(emb))

        def _rotate_half(x):
            x1, x2 = (x[..., :x.shape[-1] // 2], x[..., x.shape[-1] // 2:])
            return jnp.concatenate([-x2, x1], axis=-1)

        def _attn(x, ln_w, ln_b, conv_w, attn_w, proj_w, n_head):
            B, T, C = x.shape
            D = C // n_head
            h = _layernorm(x, ln_w, ln_b)
            hc = jnp.transpose(h, (0, 2, 1))
            hc = jnp.pad(hc, ((0, 0), (0, 0), (2, 0)))
            hc = jax.lax.conv_general_dilated(hc, conv_w, window_strides=(1,), padding='VALID', dimension_numbers=('NCH', 'OIH', 'NCH'), feature_group_count=C)
            h = jnp.transpose(hc, (0, 2, 1))
            qkv = h @ attn_w
            q, k, v = jnp.split(qkv, 3, axis=-1)
            q = q.reshape(B, T, n_head, D)
            k = k.reshape(B, T, n_head, D)
            v = v.reshape(B, T, n_head, D)
            cos, sin = _rope_tables(T, D)
            cos = cos[None, :, None, :]
            sin = sin[None, :, None, :]
            q = q * cos + _rotate_half(q) * sin
            k = k * cos + _rotate_half(k) * sin
            scores = jnp.einsum('bqhd,bkhd->bhqk', q, k) / jnp.sqrt(jnp.float32(D))
            causal = jnp.tril(jnp.ones((T, T), dtype=bool))
            scores = jnp.where(causal, scores, jnp.float32(-1e+30))
            p = jax.nn.softmax(scores, axis=-1)
            y = jnp.einsum('bhqk,bkhd->bqhd', p, v).reshape(B, T, C)
            return y @ proj_w

        def _moe(x, ln_w, ln_b, router_w, expert_wv, expert_proj):
            h = _layernorm(x, ln_w, ln_b)
            logits = h @ router_w
            expert_idx = jnp.argmax(logits, axis=-1)
            E = router_w.shape[-1]
            out = jnp.zeros_like(x)
            for e in range(E):
                gv = h @ expert_wv[e]
                gate_raw, value = jnp.split(gv, 2, axis=-1)
                y = gate_raw * jax.nn.sigmoid(gate_raw) * value @ expert_proj[e]
                out = out + jnp.where((expert_idx == e)[..., None], y, 0.0)
            return out
        C, H, E, B, T = (128, 16, 4, 4, 128)
        Dff = 4 * C
        key = jax.random.key(seed)
        ks = jax.random.split(key, 8)
        s = 0.02
        return {'x': jax.random.normal(ks[0], (B, T, C), dtype=jnp.float32), 'ln1_w': jnp.ones((C,), jnp.float32), 'ln1_b': jnp.zeros((C,), jnp.float32), 'ln2_w': jnp.ones((C,), jnp.float32), 'ln2_b': jnp.zeros((C,), jnp.float32), 'conv_w': jax.random.normal(ks[1], (C, 1, 3), dtype=jnp.float32) * 0.1, 'attn_w': jax.random.normal(ks[2], (C, 3 * C), dtype=jnp.float32) * s, 'proj_w': jax.random.normal(ks[3], (C, C), dtype=jnp.float32) * s, 'router_w': jax.random.normal(ks[4], (C, E), dtype=jnp.float32) * s, 'expert_wv': jax.random.normal(ks[5], (E, C, 2 * Dff), dtype=jnp.float32) * s, 'expert_proj': jax.random.normal(ks[6], (E, Dff, C), dtype=jnp.float32) * s}
    _L0_ffn_in = _L0_ffn_setup()

    def _L1_attn_setup():
        import jax, jax.numpy as jnp
        import numpy as np
        import math
        D_MODEL = 128
        N_HEADS = 16
        BASE = 1250
        B, T = (8, 128)

        def hope_bias(pos_independent, T, d_model, n_heads, base):
            dim = d_model // 2
            pos = np.arange(dim, dtype=np.float64)
            freqs_np = 1.0 / base ** (pos / dim)
            active = int(np.sum(freqs_np * 2 * math.pi * T >= 1.0))
            active = min(active, dim - d_model // 4)
            freqs = jnp.asarray(freqs_np[:active], dtype=jnp.float32)
            d = jnp.arange(-(T - 1), T, dtype=jnp.float32)
            theta = d[:, None] * freqs[None, :]
            pv_high = jnp.cos(theta) + jnp.sin(theta)
            latter = dim - active
            pv_const = pos_independent[:latter].sum(axis=-1)
            pv = jnp.concatenate([pv_high, jnp.broadcast_to(pv_const[None, :], (2 * T - 1, latter))], axis=1)
            pairs_per_head = dim // n_heads
            per_head = pv.reshape(2 * T - 1, n_heads, pairs_per_head).sum(axis=-1)
            idx = jnp.arange(T)[:, None] - jnp.arange(T)[None, :] + (T - 1)
            return per_head[idx]
        key = jax.random.key(seed)
        ks = jax.random.split(key, 6)
        d = D_MODEL
        return {'x': jax.random.normal(ks[0], (B, T, d), dtype=jnp.float32), 'w_qkv': jax.random.normal(ks[1], (3 * d, d), dtype=jnp.float32) * 0.02, 'b_qkv': jnp.zeros((3 * d,), dtype=jnp.float32), 'w_proj': jax.random.normal(ks[2], (d, d), dtype=jnp.float32) * 0.02, 'b_proj': jnp.zeros((d,), dtype=jnp.float32), 'pos_independent': jax.random.normal(ks[3], (d // 4, 2), dtype=jnp.float32)}
    _L1_attn_in = _L1_attn_setup()

    def _L1_ffn_setup():
        import jax, jax.numpy as jnp
        import numpy as np
        DIM = 128
        NUM_EXPERTS = 8
        EXPERT_DIM = 384
        B, S = (1, 256)
        key = jax.random.key(seed)
        ks = jax.random.split(key, 7)
        sd = 0.02
        x = jax.random.normal(ks[0], (B, S, DIM), dtype=jnp.float32)
        Wr = jax.random.normal(ks[1], (DIM, NUM_EXPERTS), dtype=jnp.float32) * sd
        br = jnp.zeros((NUM_EXPERTS,), dtype=jnp.float32)
        W1 = jax.random.normal(ks[2], (NUM_EXPERTS, DIM, EXPERT_DIM), dtype=jnp.float32) * sd
        b1 = jnp.zeros((NUM_EXPERTS, EXPERT_DIM), dtype=jnp.float32)
        W2 = jax.random.normal(ks[3], (NUM_EXPERTS, EXPERT_DIM, DIM), dtype=jnp.float32) * sd
        b2 = jnp.zeros((NUM_EXPERTS, DIM), dtype=jnp.float32)
        return {'x': x, 'Wr': Wr, 'br': br, 'W1': W1, 'b1': b1, 'W2': W2, 'b2': b2}
    _L1_ffn_in = _L1_ffn_setup()
    _d = {'L0_attn_x': _L0_attn_in['x'], 'L0_attn_wq': _L0_attn_in['wq'], 'L0_attn_bq': _L0_attn_in['bq'], 'L0_attn_wk': _L0_attn_in['wk'], 'L0_attn_bk': _L0_attn_in['bk'], 'L0_attn_wv': _L0_attn_in['wv'], 'L0_attn_bv': _L0_attn_in['bv'], 'L0_attn_wo': _L0_attn_in['wo'], 'L0_attn_bo': _L0_attn_in['bo'], 'L0_ffn_ln1_w': _L0_ffn_in['ln1_w'], 'L0_ffn_ln1_b': _L0_ffn_in['ln1_b'], 'L0_ffn_ln2_w': _L0_ffn_in['ln2_w'], 'L0_ffn_ln2_b': _L0_ffn_in['ln2_b'], 'L0_ffn_conv_w': _L0_ffn_in['conv_w'], 'L0_ffn_attn_w': _L0_ffn_in['attn_w'], 'L0_ffn_proj_w': _L0_ffn_in['proj_w'], 'L0_ffn_router_w': _L0_ffn_in['router_w'], 'L0_ffn_expert_wv': _L0_ffn_in['expert_wv'], 'L0_ffn_expert_proj': _L0_ffn_in['expert_proj'], 'L1_attn_w_qkv': _L1_attn_in['w_qkv'], 'L1_attn_b_qkv': _L1_attn_in['b_qkv'], 'L1_attn_w_proj': _L1_attn_in['w_proj'], 'L1_attn_b_proj': _L1_attn_in['b_proj'], 'L1_attn_pos_independent': _L1_attn_in['pos_independent'], 'L1_ffn_Wr': _L1_ffn_in['Wr'], 'L1_ffn_br': _L1_ffn_in['br'], 'L1_ffn_W1': _L1_ffn_in['W1'], 'L1_ffn_b1': _L1_ffn_in['b1'], 'L1_ffn_W2': _L1_ffn_in['W2'], 'L1_ffn_b2': _L1_ffn_in['b2']}
    _x0 = _d['L0_attn_x']
    _d['L0_attn_x'] = jax.random.normal(jax.random.fold_in(jax.random.key(seed), 1), (16, 256, 128), dtype=_x0.dtype)
    del _x0
    return _d

def reference(L0_attn_x, L0_attn_wq, L0_attn_bq, L0_attn_wk, L0_attn_bk, L0_attn_wv, L0_attn_bv, L0_attn_wo, L0_attn_bo, L0_ffn_ln1_w, L0_ffn_ln1_b, L0_ffn_ln2_w, L0_ffn_ln2_b, L0_ffn_conv_w, L0_ffn_attn_w, L0_ffn_proj_w, L0_ffn_router_w, L0_ffn_expert_wv, L0_ffn_expert_proj, L1_attn_w_qkv, L1_attn_b_qkv, L1_attn_w_proj, L1_attn_b_proj, L1_attn_pos_independent, L1_ffn_Wr, L1_ffn_br, L1_ffn_W1, L1_ffn_b1, L1_ffn_W2, L1_ffn_b2):

    def _L0_attn_ref(x, wq, bq, wk, bk, wv, bv, wo, bo):
        import jax, jax.numpy as jnp
        import numpy as np
        WS = 64
        LB = 1
        LF = 1
        H = 16
        NC = LB + LF + 1

        def _collect(a, pad_value):
            nw = a.shape[1]
            pads = [(0, 0), (LB, LF)] + [(0, 0)] * (a.ndim - 2)
            ap = jnp.pad(a, pads, constant_values=pad_value)
            idx = jnp.arange(nw)[:, None] + jnp.arange(NC)[None, :]
            g = ap[:, idx]
            return g.reshape(g.shape[0], nw, NC * a.shape[2], *a.shape[3:])
        B, S, E = x.shape
        hd = E // H
        nw = S // WS

        def proj(w, b):
            y = x @ w.T + b
            return y.reshape(B, S, H, hd).transpose(0, 2, 1, 3).reshape(B * H, S, hd)
        q = proj(wq, bq)
        k = proj(wk, bk)
        v = proj(wv, bv)
        qb = q.reshape(B * H, nw, WS, hd)
        kb = _collect(k.reshape(B * H, nw, WS, hd), -1.0)
        vb = _collect(v.reshape(B * H, nw, WS, hd), -1.0)
        t = jnp.arange(S, dtype=jnp.int32).reshape(1, nw, WS)
        ct = _collect(t, -1)
        scores = jnp.einsum('bwqd,bwkd->bwqk', qb, kb)
        qi = t.reshape(1, nw, WS, 1)
        ctb = ct[:, :, None, :]
        over = ((ctb > qi + WS * LF) | (ctb < qi - WS * LB)) & (ctb != -1)
        scores = jnp.where(over, -jnp.inf, scores)
        attn = jax.nn.softmax(scores, axis=-1)
        out = jnp.einsum('bwqk,bwkd->bwqd', attn, vb)
        out = out.reshape(B, H, S, hd).transpose(0, 2, 1, 3).reshape(B, S, E)
        return out @ wo.T + bo

    def _L0_ffn_ref(x, ln1_w, ln1_b, ln2_w, ln2_b, conv_w, attn_w, proj_w, router_w, expert_wv, expert_proj):
        import jax, jax.numpy as jnp
        import numpy as np
        EPS = 1e-05

        def _layernorm(x, w, b):
            mu = jnp.mean(x, axis=-1, keepdims=True)
            var = jnp.mean((x - mu) ** 2, axis=-1, keepdims=True)
            return (x - mu) * jax.lax.rsqrt(var + EPS) * w + b

        def _rope_tables(T, D, base=10000.0):
            inv_freq = 1.0 / base ** (jnp.arange(0, D, 2, dtype=jnp.float32) / D)
            t = jnp.arange(T, dtype=jnp.float32)
            freqs = jnp.einsum('i,j->ij', t, inv_freq)
            emb = jnp.concatenate([freqs, freqs], axis=-1)
            return (jnp.cos(emb), jnp.sin(emb))

        def _rotate_half(x):
            x1, x2 = (x[..., :x.shape[-1] // 2], x[..., x.shape[-1] // 2:])
            return jnp.concatenate([-x2, x1], axis=-1)

        def _attn(x, ln_w, ln_b, conv_w, attn_w, proj_w, n_head):
            B, T, C = x.shape
            D = C // n_head
            h = _layernorm(x, ln_w, ln_b)
            hc = jnp.transpose(h, (0, 2, 1))
            hc = jnp.pad(hc, ((0, 0), (0, 0), (2, 0)))
            hc = jax.lax.conv_general_dilated(hc, conv_w, window_strides=(1,), padding='VALID', dimension_numbers=('NCH', 'OIH', 'NCH'), feature_group_count=C)
            h = jnp.transpose(hc, (0, 2, 1))
            qkv = h @ attn_w
            q, k, v = jnp.split(qkv, 3, axis=-1)
            q = q.reshape(B, T, n_head, D)
            k = k.reshape(B, T, n_head, D)
            v = v.reshape(B, T, n_head, D)
            cos, sin = _rope_tables(T, D)
            cos = cos[None, :, None, :]
            sin = sin[None, :, None, :]
            q = q * cos + _rotate_half(q) * sin
            k = k * cos + _rotate_half(k) * sin
            scores = jnp.einsum('bqhd,bkhd->bhqk', q, k) / jnp.sqrt(jnp.float32(D))
            causal = jnp.tril(jnp.ones((T, T), dtype=bool))
            scores = jnp.where(causal, scores, jnp.float32(-1e+30))
            p = jax.nn.softmax(scores, axis=-1)
            y = jnp.einsum('bhqk,bkhd->bqhd', p, v).reshape(B, T, C)
            return y @ proj_w

        def _moe(x, ln_w, ln_b, router_w, expert_wv, expert_proj):
            h = _layernorm(x, ln_w, ln_b)
            logits = h @ router_w
            expert_idx = jnp.argmax(logits, axis=-1)
            E = router_w.shape[-1]
            out = jnp.zeros_like(x)
            for e in range(E):
                gv = h @ expert_wv[e]
                gate_raw, value = jnp.split(gv, 2, axis=-1)
                y = gate_raw * jax.nn.sigmoid(gate_raw) * value @ expert_proj[e]
                out = out + jnp.where((expert_idx == e)[..., None], y, 0.0)
            return out
        n_head = 16
        x = x + _attn(x, ln1_w, ln1_b, conv_w, attn_w, proj_w, n_head)
        x = x + _moe(x, ln2_w, ln2_b, router_w, expert_wv, expert_proj)
        return x

    def _L1_attn_ref(x, w_qkv, b_qkv, w_proj, b_proj, pos_independent):
        import jax, jax.numpy as jnp
        import numpy as np
        import math
        D_MODEL = 128
        N_HEADS = 16
        BASE = 1250
        B, T = (8, 128)

        def hope_bias(pos_independent, T, d_model, n_heads, base):
            dim = d_model // 2
            pos = np.arange(dim, dtype=np.float64)
            freqs_np = 1.0 / base ** (pos / dim)
            active = int(np.sum(freqs_np * 2 * math.pi * T >= 1.0))
            active = min(active, dim - d_model // 4)
            freqs = jnp.asarray(freqs_np[:active], dtype=jnp.float32)
            d = jnp.arange(-(T - 1), T, dtype=jnp.float32)
            theta = d[:, None] * freqs[None, :]
            pv_high = jnp.cos(theta) + jnp.sin(theta)
            latter = dim - active
            pv_const = pos_independent[:latter].sum(axis=-1)
            pv = jnp.concatenate([pv_high, jnp.broadcast_to(pv_const[None, :], (2 * T - 1, latter))], axis=1)
            pairs_per_head = dim // n_heads
            per_head = pv.reshape(2 * T - 1, n_heads, pairs_per_head).sum(axis=-1)
            idx = jnp.arange(T)[:, None] - jnp.arange(T)[None, :] + (T - 1)
            return per_head[idx]
        Bm, Tm, C = x.shape
        H = N_HEADS
        hd = C // H
        qkv = x @ w_qkv.T + b_qkv
        qkv = qkv.reshape(Bm, Tm, 3, H, hd).transpose(2, 0, 3, 1, 4)
        q, k, v = (qkv[0], qkv[1], qkv[2])
        att = jnp.einsum('bhqd,bhkd->bhqk', q, k) / jnp.sqrt(jnp.float32(hd))
        bias = hope_bias(pos_independent, Tm, C, H, BASE)
        att = att + bias.transpose(2, 0, 1)[None]
        causal = jnp.tril(jnp.ones((Tm, Tm), dtype=bool))
        att = jnp.where(causal[None, None], att, -jnp.inf)
        att = jax.nn.softmax(att, axis=-1)
        out = jnp.einsum('bhqk,bhkd->bhqd', att, v)
        out = out.transpose(0, 2, 1, 3).reshape(Bm, Tm, C)
        return out @ w_proj.T + b_proj

    def _L1_ffn_ref(x, Wr, br, W1, b1, W2, b2):
        import jax, jax.numpy as jnp
        import numpy as np
        DIM = 128
        NUM_EXPERTS = 8
        EXPERT_DIM = 384
        B, S = (1, 256)
        router_logits = x @ Wr + br
        expert_idx = jnp.argmax(router_logits, axis=-1)
        onehot = jax.nn.one_hot(expert_idx, NUM_EXPERTS, dtype=x.dtype)
        h = jax.nn.gelu(jnp.einsum('bsd,edh->bseh', x, W1) + b1, approximate=False)
        y = jnp.einsum('bseh,ehd->bsed', h, W2) + b2
        out = jnp.einsum('bsed,bse->bsd', y, onehot)
        return out
    x = L0_attn_x
    x = x + _L0_attn_ref(_layernorm(x, axis=-1), L0_attn_wq, L0_attn_bq, L0_attn_wk, L0_attn_bk, L0_attn_wv, L0_attn_bv, L0_attn_wo, L0_attn_bo)
    x = x + _L0_ffn_ref(_layernorm(x, axis=-1), L0_ffn_ln1_w, L0_ffn_ln1_b, L0_ffn_ln2_w, L0_ffn_ln2_b, L0_ffn_conv_w, L0_ffn_attn_w, L0_ffn_proj_w, L0_ffn_router_w, L0_ffn_expert_wv, L0_ffn_expert_proj)
    x = x + _L1_attn_ref(_layernorm(x, axis=-1), L1_attn_w_qkv, L1_attn_b_qkv, L1_attn_w_proj, L1_attn_b_proj, L1_attn_pos_independent)
    x = x + _L1_ffn_ref(_layernorm(x, axis=-1), L1_ffn_Wr, L1_ffn_br, L1_ffn_W1, L1_ffn_b1, L1_ffn_W2, L1_ffn_b2)
    return x

_drawn_inputs = setup_inputs


def setup_inputs(seed=0):
    import zlib

    import numpy as np

    out = dict(_drawn_inputs(seed))
    spreads = {'L0_ffn_ln1_w': (1.0, 0.6),
     'L0_ffn_ln1_b': (0.0, 0.8),
     'L0_ffn_ln2_w': (1.0, 0.6),
     'L0_ffn_ln2_b': (0.0, 0.8),
     'L1_attn_b_qkv': (0.0, 1.737),
     'L1_attn_b_proj': (0.0, 0.8),
     'L1_ffn_br': (0.0, 0.8),
     'L1_ffn_b1': (0.0, 2.0),
     'L1_ffn_b2': (0.0, 0.8)}
    factors = {'L0_attn_bq': 8.0,
     'L0_attn_wk': 8.0,
     'L0_attn_bk': 8.0,
     'L0_attn_wv': 8.0,
     'L0_attn_bv': 8.0,
     'L0_ffn_conv_w': 8.0,
     'L0_ffn_attn_w': 8.0,
     'L0_ffn_proj_w': 8.0,
     'L0_ffn_router_w': 8.0,
     'L0_ffn_expert_wv': 7.004,
     'L0_ffn_expert_proj': 7.205,
     'L1_attn_w_qkv': 7.21,
     'L1_attn_w_proj': 3.227,
     'L1_attn_pos_independent': 64.0,
     'L1_ffn_Wr': 5.257,
     'L1_ffn_W1': 8.0,
     'L1_ffn_W2': 5.416}
    for name, (base, spread) in spreads.items():
        noise = np.random.default_rng([zlib.crc32(name.encode()), seed]).standard_normal(out[name].shape)
        drawn = base * np.exp(spread * noise) if base else spread * noise
        out[name] = jnp.asarray(drawn.astype(out[name].dtype))
    for name, factor in factors.items():
        out[name] = (out[name] * factor).astype(out[name].dtype)
    return out
```

```python
import concourse.bass as bass
from concourse import mybir
from contextlib import ExitStack

NSEQ, SEQ, C, P = 16, 256, 128, 128
H, D = 16, 8
NT = NSEQ * SEQ // P
TPS = SEQ // P
WS = 64
BAND = 3 * WS
PARTS = 3
PAIRS = [(0, 0), (0, 1), (0, 2), (1, 0), (1, 1), (2, 0)]
ROWS = len(PAIRS) * D
ROW_BIAS = ROWS
ROW_MAX = (ROWS, ROWS, 2 * ROWS)
HPS = 2
NSTEP = H // HPS
GROUPS = H // 4
SW = 2 * SEQ + 2 * P
NBUF = 4
E0, F0 = 4, 512
E1, F1 = 8, 384
NTILE0 = NT + E0
NTILE1 = NT + E1
EPS = 1e-5
OFF_LOAD, OFF_PROJ, OFF_SPREAD, OFF_SCORE, OFF_MAX, OFF_ATT, OFF_OUT, OFF_ROUTE, OFF_LOGIT = 5, 4, 3, 2, 1, 0, -1, -2, -3
ATTN0, ATTN1, ATTN2 = range(3)

CF = {}
CB = {}


def _columns():
    at = 0
    for name, n in (("ident", P), ("cosq", SEQ), ("cosk", SEQ), ("sinq", SEQ), ("sink", SEQ), ("heads", H),
                    ("padfar", TPS), ("pad64", TPS), ("ones", P), ("eid", 8), ("start", 64)):
        CF[name] = (at, at + n)
        at += n
    CF["all"] = at
    at = 0
    for name, n in (("ident", P), ("band", 2 * BAND), ("causal_q", P), ("causal_k", P), ("before", P), ("ones", P)):
        CB[name] = (at, at + n)
        at += n
    CB["all"] = at


_columns()


class Unit:

    def __init__(self, rep, it):
        self.layer, self.rep, self.n = rep // NSEQ, rep, rep + NBUF * it
        self.s = self.n - NSEQ * self.layer
        self.b, self.it = rep % NBUF, it


class Slot:

    def __init__(self, rep, it, first, last):
        self.rep, self.it, self.first, self.last = rep, it, first, last

    def unit(self, off, layers=(0, 1, 2)):
        r = self.rep + off
        if not self.first <= r < self.last or r // NSEQ not in layers:
            return None
        return Unit(r, self.it)

    def before(self):
        return Slot(self.rep - 1, self.it, self.first, self.last)


def build(nc, t, out):
    f32, bf16, i32, u32 = mybir.dt.float32, mybir.dt.bfloat16, mybir.dt.int32, mybir.dt.uint32
    ALU, ACT, AX = mybir.AluOpType, mybir.ActivationFunctionType, mybir.AxisListType
    ctx = ExitStack()
    with ctx:
        def sb(name, shape, dt=f32):
            return ctx.enter_context(nc.sbuf_tensor(name, shape, dt))

        def pb(name, shape):
            return ctx.enter_context(nc.psum_tensor(name, shape, f32))

        def sem(name):
            return ctx.enter_context(nc.semaphore(name))

        def dram(name, shape):
            return nc.dram_tensor(name, shape, f32, kind="Internal").ap()

        x1_d = dram("x1_d", (NSEQ * SEQ, C))
        y_d = dram("y_d", (NSEQ * SEQ, C))
        xz_d = dram("xz_d", (NSEQ * SEQ, C))
        x2_d = dram("x2_d", (NSEQ * SEQ, C))
        x3_d = dram("x3_d", (NSEQ * SEQ, C))
        hs_d = [dram("hs0_d", (NTILE0 * P, C)), dram("hs1_d", (NTILE1 * P, C))]
        ys_d = [dram("ys0_d", (NTILE0 * P, C)), dram("ys1_d", (NTILE1 * P, C))]

        cf = sb("cf", [P, CF["all"]])
        cb = sb("cb", [P, CB["all"]], bf16)
        Fc = lambda name: cf[:, CF[name][0]:CF[name][1]]
        Bc = lambda name: cb[:, CB[name][0]:CB[name][1]]
        wt = sb("wt", [P, 14, C])
        WQ, WK, WV, WO, WRQ, WRK = range(6)
        WSET = {0: (0, 1, 2, 3, None, None), 1: (4, 5, 6, 7, 8, 9), 2: (10, 11, 12, 13, None, None)}
        W = lambda layer, which: wt[:, WSET[layer][which], :]
        cols = sb("cols", [P, 9])
        BQ0, BK0, LN1W, LN1B, BQ2, BK2, BQ2S = range(7)
        convw = sb("convw", [P, 3])
        rows = sb("rows", [P, 6, C])
        BV0, BO0, LN2W, LN2B, BV2, BO2 = range(6)
        wr = sb("wr", [P, E0 + E1])
        br = sb("br", [P, E1])
        wm = sb("wm", [P, 2 * E1 * F1])
        up = [wm[:, 0:E0 * 2 * F0], wm[:, 0:E1 * F1]]
        dn = [wm[:, E0 * 2 * F0:E0 * 3 * F0], wm[:, E1 * F1:2 * E1 * F1]]
        posr = sb("posr", [1, 8, 8])
        posc = sb("posc", [1, 3, 8])
        poscp = sb("poscp", [1, PARTS, 8], bf16)

        xin = sb("xin", [P, NBUF, TPS, C])
        stat = sb("stat", [P, NBUF, TPS, 6])
        mv = sb("mv", [P, NBUF, TPS, 2])
        rstd = sb("rstd", [P, NBUF, TPS, 2])
        xn = sb("xn", [P, NBUF, TPS, C])
        stat2 = sb("stat2", [P, NBUF, TPS, 6])
        mv2 = sb("mv2", [P, NBUF, TPS, 2])
        rstd2 = sb("rstd2", [P, NBUF, TPS, 2])
        xn2 = sb("xn2", [P, 2, TPS, C])
        xT = sb("xT", [P, 2, SEQ])
        cT = sb("cT", [P, 2, SEQ])
        tap = sb("tap", [P, 2, SEQ])
        qkf = sb("qkf", [P, 2, SEQ])
        qks = sb("qks", [P, 2, SEQ])
        parts = sb("parts", [P, PARTS, 2, SEQ], bf16)
        arena = sb("arena", [P, 2 * NBUF * H * SEQ // 2])
        QK = [arena[:, i * H * SEQ // 2:(i + 1) * H * SEQ // 2].bitcast(bf16).rearrange("p (h t) -> p h t", h=H)
              for i in range(2 * NBUF)]
        QA, KA = QK[0:NBUF], QK[NBUF:]
        vv = sb("vv", [P, NBUF, TPS, H, 32])
        nred = sb("nred", [P, 2, NSTEP, 6])
        nmax = sb("nmax", [P, 2, TPS, H])
        mres = sb("mres", [P, 2, TPS, H])
        mparts = sb("mparts", [P, TPS, P // H, H], bf16)
        mT = sb("mT", [PARTS * H, SEQ], bf16)
        spad = sb("spad", [P, NBUF, TPS, H])
        epad = sb("epad", [P, NBUF, TPS, H])
        earg = sb("earg", [P, 2, TPS, H])
        pr = sb("pr", [P, 4, SW])
        poscb = pr[0:1, :, :].rearrange("o a b -> o (a b)").bitcast(bf16).rearrange(
            "o (a h t) -> o a h t", a=PARTS, h=8)
        oT = sb("oT", [P, GROUPS, SEQ])
        rden = sb("rden", [P, 2, TPS, 2, 4])
        den = sb("den", [P, 2, TPS, 2, 4])
        on = sb("on", [P, 2, TPS, H, D])
        onT = sb("onT", [P, SEQ])
        xres = sb("xres", [P, 2, TPS, C])
        yres = sb("yres", [P, 2, TPS, C])
        zb = sb("zb", [P, 2, TPS, C])
        xzb = sb("xzb", [P, 2, TPS, C])
        stat3 = sb("stat3", [P, 2, TPS, 6])
        mv3 = sb("mv3", [P, 2, TPS, 2])
        rstd3 = sb("rstd3", [P, 2, TPS, 2])
        hn = sb("hn", [P, 2, TPS, C])
        pnum = sb("pnum", [P, TPS, 8, D])
        hT = sb("hT", [P, SEQ])
        half = sb("half", [P, TPS])
        nil = sb("nil", [P, TPS])
        eps = sb("eps", [P, TPS])
        rstdv = sb("rstdv", [P, NBUF, TPS, 2])
        rstd2v = sb("rstd2v", [P, NBUF, TPS, 2])
        rstd3v = sb("rstd3v", [P, 2, TPS, 2])
        lg = [sb("lg0", [P, NT, E0]), sb("lg1", [P, NT, E1])]
        h2 = sb("h2", [P, NT, C])

        def piece(n):
            a = piece.at
            piece.at += n
            return arena[:, a:a + n]
        piece.at = 0
        xg = piece(NT * C).rearrange("p (t c) -> p t c", t=NT)
        b1r, b2r = piece(E1 * F1), piece(E1 * C)
        xf = piece(2 * C).rearrange("p (b c) -> p b c", b=2)
        xfT = piece(2 * C).rearrange("p (b c) -> p b c", b=2)
        gate = piece(2 * F0).rearrange("p (b c) -> p b c", b=2)
        mixact = piece(2 * F0).rearrange("p (b c) -> p b c", b=2)
        actT = piece(2 * F0).rearrange("p (b c) -> p b c", b=2)
        yt = piece(2 * C).rearrange("p (b c) -> p b c", b=2)
        top = sb("top", [P, NT])
        eq = sb("eq", [P, NT, E1])
        eqi = sb("eqi", [P, NT, E1])
        pick = sb("pick", [P, NT])
        oh = sb("oh", [P, NT, E1], bf16)
        cnt = sb("cnt", [P, E1], bf16)
        padi = sb("padi", [P, E1], i32)
        padi2 = sb("padi2", [P, E1], i32)
        padf = sb("padf", [P, E1])
        base = sb("base", [P, E1 + 1])
        rk = sb("rk", [P, NT, E1])
        rk2 = sb("rk2", [P, NT, E1])
        destf = sb("destf", [P, NT])
        dest = [sb("dest0", [P, NT], u32), sb("dest1", [P, NT], u32)]
        ge = sb("ge", [1, NTILE1, E1])
        tef = sb("tef", [1, NTILE1])
        tei = [sb("te0", [1, NTILE0], i32), sb("te1", [1, NTILE1], i32)]

        psS = pb("psS", [P, 1024])
        psT = [pb("psT0", [P, 1024]), pb("psT1", [P, 1024])]
        psO = pb("psO", [P, 512])
        psM = pb("psM", [P, 512])

        S = {n: sem("s_" + n) for n in (
            "const half pos wload dn1load zero setup posb posd trig hs0 krow "
            "stats mvs veps rstds lnout lnout2 stats2 mvs2 veps2 rstds2 "
            "xt xtev tap0 tap1 tap2 tap3 conv qk qkev rot rotev ropeadd sp spev "
            "hi resid mid lo v vev sready red nmax mhi mres mmid mlo mt mtev "
            "tready exp earg epad epad64 pv oev ott den rden norm pnum ob obev op rbias zout "
            "xz stats3 mvs3 veps3 rstds3 hout hw hfin hT hTev lg lgev ").split()}
        M = {n: [sem(f"m{i}_{n}") for i in range(2)] for n in (
            "dve rank dest scat ht htev up act prod at atev yev "
            "xres add ostore te bias actg".split())}
        MD = {n: [[sem(f"m{i}{j}_{n}") for j in range(k)] for i in range(2)] for n, k in
              (("gath", 2), ("store", 2), ("fin", NT // 4))}

        def at(per, u, c, first=0):
            return per * (u.n - first) + c

        def wait(eng, name, value):
            if isinstance(value, int) and value <= 0:
                return
            eng.wait_ge(S[name], value)

        D_ = {n: [sem(f"d{i}_{n}") for i in range(2)] for n in
              "xin resdma yresdma xstore hstore ystore rep mrow".split()}
        NREP = 2 * len(PAIRS)

        def moved(eng, name, u, back=0, first=0, n=1):
            r = u.rep - back
            if r >= first:
                eng.wait_ge(D_[name][r % 2], 16 * n * ((r - first) // 2 + 1 + NBUF // 2 * u.it))

        TEN_M = [("v", OFF_SPREAD, (0, 1, 2), "vev", 1, 0), ("lg", OFF_LOGIT, (1, 2), "lgev", 1, NSEQ),
                 ("qk", OFF_PROJ, (0, 1, 2), "qkev", 2, 0), ("sp", OFF_PROJ, (0,), "spev", 1, 0),
                 ("rot", OFF_PROJ, (1,), "rotev", 1, NSEQ), ("mt", OFF_MAX, (0, 1, 2), "mtev", 1, 0),
                 ("hT", OFF_ROUTE, (1, 2), "hTev", 1, NSEQ), ("xt", OFF_LOAD, (0, 1, 2), "xtev", 1, 0)]
        TEN_O = [("pv3", OFF_OUT, (0, 1, 2), "oev", 4, 4), ("ott0", OFF_OUT, (0, 1, 2), "norm", 2, 1),
                 ("pv0", OFF_ATT, (0, 1, 2), "oev", 4, 1), ("ott1", OFF_OUT, (0, 1, 2), "norm", 2, 2),
                 ("pv1", OFF_ATT, (0, 1, 2), "oev", 4, 2), ("ob", OFF_OUT, (0, 1, 2), "obev", 1, 1),
                 ("pv2", OFF_ATT, (0, 1, 2), "oev", 4, 3), ("op", OFF_OUT, (0, 1, 2), "zout", 1, 1)]

        def wait_bank(eng, table, slot, name):
            i = [x[0] for x in table].index(name)
            sl = slot
            for _ in range(3 * len(table)):
                i -= 1
                if i < 0:
                    i, sl = len(table) - 1, sl.before()
                _, off, layers, done, per, c = table[i]
                u = sl.unit(off, layers)
                if u:
                    if table is TEN_M:
                        wait(eng, done, at(per, u, per, c))
                    else:
                        wait(eng, done, at(per, u, c))
                    return

        def slots(eng, step, first, last):
            k = first - OFF_LOAD
            while k < last - OFF_LOGIT:
                inner = k % NSEQ
                if k >= first and inner == 3:
                    with eng.Fori(0, (NSEQ - 4 - 4) // NBUF) as i:
                        for j in range(NBUF):
                            step(Slot(k + j, i, first, last))
                    k += NSEQ - 4 - 4
                else:
                    step(Slot(k, 0, first, last))
                    k += 1

        def tok(d, s, n=TPS):
            return d.rearrange("(s t p) c -> s p t c", t=TPS, p=P)[bass.ds(s, 1), :, :, :].rearrange(
                "s p t c -> p (s t) c")

        wm_parts = [
            (cf[:, :], t["cf"]), (cb[:, :], t["cb"]),
            (wt[:, :, :], t["wt"]), (cols[:, 0:6], t["cols"]), (convw[:, :], t["convw"]),
            (rows[:, :, :], t["rows"].partition_broadcast(P)),
            (wr[:, :], t["wr"]), (br[:, :], t["br"].partition_broadcast(P)),
        ]
        late_parts = [
            (up[0].rearrange("p (e n) -> p e n", e=E0), t["up0"].rearrange("e p n -> p e n")),
            (dn[0].rearrange("p (e k n) -> p e k n", e=E0, n=C), t["dn0"].rearrange("e (k p) n -> p e k n", p=P)),
            (posr[:, :, :], t["pos"]),
        ]
        NCONST, NLATE = 16 * len(wm_parts), 16 * len(late_parts)
        mix1_parts = [
            (up[1].rearrange("p (e n) -> p e n", e=E1), t["up1"].rearrange("e p n -> p e n")),
            (dn[1].rearrange("p (e k n) -> p e k n", e=E1, n=C), t["dn1"].rearrange("e (k p) n -> p e k n", p=P)),
        ]
        bias_parts = [(b1r, t["b1"].partition_broadcast(P)), (b2r, t["b2"].partition_broadcast(P))]

        block = ctx.enter_context(nc.Block())

        @block.sync
        def _(sp):
            for dst, src in wm_parts:
                sp.dma_start(dst, src).then_inc(S["const"], 16)

            def step(sl):
                ul, up, um = sl.unit(OFF_LOAD), sl.unit(OFF_SPREAD), sl.unit(OFF_MAX)
                uo, ur = sl.unit(OFF_OUT), sl.unit(OFF_ROUTE)
                if ul:
                    wait(sp, "lnout", at(2, ul, -2))
                    if ul.layer == 1:
                        moved(sp, "xstore", ul, NSEQ)
                    src = (t["x"], x1_d, x2_d)[ul.layer]
                    sp.dma_start(xin[:, ul.b, :, :], tok(src, ul.s)).then_inc(D_["xin"][ul.b % 2], 16)
                if up:
                    wait(sp, "hi", at(1, up, 1))
                    wait(sp, "tready", at(NSTEP, up, NSTEP - NSTEP * NBUF))
                    for n, made in enumerate((None, "mid", "lo")):
                        if made:
                            wait(sp, made, at(1, up, 1))
                        for w, buf in enumerate((QA, KA)):
                            for j, pair in enumerate(PAIRS):
                                if pair[w] == n:
                                    sp.dma_start(buf[up.b][D * j:D * j + D, :, :],
                                                 parts[:, n, w, :]).then_inc(D_["rep"][up.b % 2], 16)
                if uo:
                    if uo.rep >= NSEQ + 2 and uo.layer == 1:
                        wait(sp, "xz", at(1, uo, -1, NSEQ))
                    else:
                        wait(sp, "zout", at(1, uo, -1))
                    src = (t["x"], x1_d, x2_d)[uo.layer]
                    sp.dma_start(xres[:, uo.b % 2, :, :], tok(src, uo.s)).then_inc(D_["resdma"][uo.b % 2], 16)
                    if uo.layer == 1:
                        moved(sp, "ystore", uo, 0, NSEQ)
                        sp.dma_start(yres[:, uo.b % 2, :, :], tok(y_d, uo.s)).then_inc(D_["yresdma"][uo.b % 2], 16)
                if ur:
                    if ur.layer == 1:
                        wait(sp, "xz", at(1, ur, 1, NSEQ))
                        sp.dma_start(tok(xz_d, ur.s), xzb[:, ur.b % 2, :, :]).then_inc(D_["xstore"][ur.b % 2], 16)
                    else:
                        wait(sp, "zout", at(1, ur, 1))
                        sp.dma_start(tok((x1_d, None, x3_d)[ur.layer], ur.s),
                                     zb[:, ur.b % 2, :, :]).then_inc(D_["xstore"][ur.b % 2], 16)
                if ur and ur.layer >= 1:
                    wait(sp, "hfin", at(1, ur, 1, NSEQ))
                    sp.dma_start(h2[:, bass.ds(ur.s * TPS, TPS), :], hn[:, ur.b % 2, :, :]).then_inc(D_["hstore"][ur.b % 2], 16)
                if um:
                    wait(sp, "mtev", at(1, um, 1))
                    sp.dma_start(QA[um.b][ROW_MAX[um.layer]:ROW_MAX[um.layer] + PARTS, :, :], mT[:, :]).then_inc(D_["mrow"][um.b % 2], 16)
                if ul and ul.layer == 1:
                    wait(sp, "lnout", at(2, ul, 2))
                    sp.dma_start(tok(y_d, ul.s), xn[:, ul.b, :, :]).then_inc(D_["ystore"][ul.b % 2], 16)

            def mix(i):
                ntl, E = (NTILE0, NTILE1)[i], (E0, E1)[i]

                def load(j, it):
                    jx = j + 2 * it
                    if j >= 2:
                        sp.wait_ge(M["ht"][i], jx - 1)
                    sp.dma_start(xf[:, j % 2, :], hs_d[i].rearrange("(j p) c -> j p c", p=P)[
                        bass.ds(jx, 1), :, :].rearrange("j p c -> p (j c)")).then_inc(MD["gath"][i][j % 2], 16)

                def store(j, it):
                    jx = j + 2 * it
                    sp.wait_ge(M["yev"][i], jx + 1)
                    sp.dma_start(ys_d[i].rearrange("(j p) c -> j p c", p=P)[
                        bass.ds(jx, 1), :, :].rearrange("j p c -> p (j c)"), yt[:, j % 2, :]).then_inc(MD["store"][i][j % 2], 16)

                sp.wait_ge(S["tready"], NSTEP * NSEQ * (2, 3)[i])
                if i == 1:
                    for dst, src in bias_parts:
                        sp.dma_start(dst, src).then_inc(M["bias"][i], 16)
                for q in range(2):
                    sp.wait_ge(D_["xstore"][q], 8 * NSEQ * (2, 3)[i])
                src = (xz_d, x3_d)[i]
                sp.dma_start(xg, src.rearrange("(t p) c -> p t c", p=P)).then_inc(M["xres"][i], 16)
                sp.wait_ge(M["scat"][i], 16 * NT)
                load(0, 0)
                load(1, 0)
                with sp.Fori(0, (ntl - 2) // 2) as it:
                    for j in range(2):
                        load(j + 2, it)
                        store(j, it)
                store(ntl - 2, 0)
                store(ntl - 1, 0)
                dst = (x2_d, out)[i]
                for q in range(NT // 4):
                    sp.wait_ge(M["add"][i], q + 1)
                    sp.dma_start(dst.rearrange("(t p) c -> p t c", p=P)[:, 4 * q:4 * q + 4, :],
                                 xg[:, 4 * q:4 * q + 4, :]).then_inc(M["ostore"][i], 16)
                sp.wait_ge(M["ostore"][i], 16 * (NT // 4))

            sp.wait_ge(S["zero"], 1)
            for i, n in enumerate((NTILE0, NTILE1)):
                z = hs_d[i].rearrange("(t p) c -> p t c", p=P)
                sp.dma_start(z[:, 0:NT, :], h2[:, :, :]).then_inc(S["hs0"], 16)
                sp.dma_start(z[:, NT:n, :], h2[:, 0:n - NT, :]).then_inc(S["hs0"], 16)
            for dst, src in late_parts:
                sp.dma_start(dst, src).then_inc(S["wload"], 16)
            sp.wait_ge(S["hs0"], 64)
            for i in range(NBUF):
                sp.dma_start(KA[i][ROW_MAX[0]:ROW_MAX[0] + PARTS, :, :], t["onesb"]).then_inc(S["krow"], 16)
            slots(sp, step, 0, 2 * NSEQ)
            mix(0)
            for i in range(NBUF):
                sp.dma_start(QA[i][ROW_BIAS:ROW_MAX[2], :, :], t["trig"][0]).then_inc(S["trig"], 16)
                sp.dma_start(KA[i][ROW_BIAS:ROW_MAX[2], :, :], t["trig"][1]).then_inc(S["trig"], 16)
                sp.dma_start(KA[i][ROW_MAX[2]:ROW_MAX[2] + PARTS, :, :], t["onesb"]).then_inc(S["krow"], 16)
            sp.wait_ge(S["trig"], 16 * 2 * NBUF)
            sp.wait_ge(S["posb"], 1)
            for i in range(NBUF):
                sp.dma_start(KA[i][ROW_BIAS:ROW_BIAS + PARTS, 8:H, :], poscb).then_inc(S["posd"], 16)
            sp.wait_ge(S["posd"], 16 * NBUF)
            for dst, src in mix1_parts:
                sp.dma_start(dst, src).then_inc(S["dn1load"], 16)
            slots(sp, step, 2 * NSEQ, 3 * NSEQ)
            mix(1)
            for name, n in (("xstore", 3), ("hstore", 2), ("ystore", 1)):
                for q in range(2):
                    sp.wait_ge(D_[name][q], 8 * n * NSEQ)

        @block.tensor
        def _(pe):
            mm = pe.matmul

            def score(sl, g):
                u = sl.unit(OFF_SCORE)
                if not u:
                    return
                if g == 0:
                    if u.layer == 2:
                        pe.wait_ge(S["posd"], 16 * NBUF)
                    moved(pe, "rep", u, n=NREP)
                wait(pe, "red", at(NSTEP, u, g))
                q, k = QA[u.b], KA[u.b]
                n = ROW_MAX[u.layer]
                for qt in (1, 0):
                    o = psS[:, 512 * (1 - qt):512 * (2 - qt)] if u.layer else psS[:, 512 * qt:512 * qt + 512]
                    keys = (64 * qt, BAND) if u.layer == 0 else (0, P * (qt + 1))
                    for hh in range(HPS):
                        h = HPS * g + hh
                        mm(o[:, hh * keys[1]:(hh + 1) * keys[1]], q[0:n, h, P * qt:P * qt + P],
                           k[0:n, h, keys[0]:keys[0] + keys[1]], start=(hh == 0), stop=False, skip_group_check=True)
                    o2 = o[:, 0:HPS * keys[1]].rearrange("p (h k) -> p h k", h=HPS)
                    if u.layer == 0:
                        mask = Bc("band")[:, BAND * qt:BAND * qt + BAND]
                    else:
                        mask = Bc("causal_q")
                        o2 = o2[:, :, P * qt:P * qt + P]
                    w = mask.shape[-1]
                    last = mm(o2, Bc("ident"), mask.unsqueeze(1).to_broadcast([P, HPS, w]), start=False, stop=True,
                              skip_group_check=True)
                last.then_inc(S["sready"], 1)

            def scoreT(sl, g):
                u = sl.unit(OFF_ATT)
                if not u:
                    return
                if g == 0:
                    pe.wait_ge(S["krow"], 16 * NBUF * (1 + (u.layer == 2)))
                    moved(pe, "mrow", u)
                wait(pe, "exp", at(NSTEP, u, g - 1))
                n = ROW_MAX[u.layer] + PARTS
                q, k = QA[u.b][0:n], KA[u.b][0:n]
                for kt in range(2):
                    o = psT[g % 2][:, 512 * kt:512 * kt + 512]
                    q0, qn = (64 * kt, BAND) if u.layer == 0 else (P * kt, SEQ - P * kt)
                    for hh in range(HPS):
                        h = HPS * g + hh
                        mm(o[:, hh * qn:hh * qn + qn], k[:, h, P * kt:P * kt + P], q[:, h, q0:q0 + qn],
                           start=(hh == 0), stop=False, skip_group_check=True)
                    o2 = o[:, 0:HPS * qn].rearrange("p (h k) -> p h k", h=HPS)
                    if u.layer == 0:
                        mask = Bc("band")[:, BAND * kt:BAND * kt + BAND]
                    else:
                        mask = Bc("causal_k")
                        o2 = o2[:, :, 0:P]
                    w = mask.shape[-1]
                    last = mm(o2, Bc("ident"), mask.unsqueeze(1).to_broadcast([P, HPS, w]), start=False, stop=True,
                              skip_group_check=True)
                last.then_inc(S["tready"], 1)

            def pv(sl, name, gg):
                u = sl.unit(OFF_OUT if name == "pv3" else OFF_ATT)
                if not u:
                    return
                wait_bank(pe, TEN_O, sl, name)
                wait(pe, "exp", at(NSTEP, u, 2 * gg + 2))
                if gg == 0:
                    wait(pe, "vev", at(1, u, 1))
                for kt in range(2):
                    q0, qn = (64 * kt, BAND) if u.layer == 0 else (P * kt, SEQ - P * kt)
                    off = 0 if kt == 0 else HPS * (BAND if u.layer == 0 else SEQ)
                    for j in range(4):
                        h = 4 * gg + j
                        a = off + (h % 2) * qn
                        last = mm(psO[32 * j:32 * j + 32, q0:q0 + qn], vv[:, u.b, kt, h, :],
                                  pr[:, (h // 2) % 4, a:a + qn], start=(kt == 0), stop=(kt == 1),
                                  skip_group_check=True)
                last.then_inc(S["pv"], 1)

            def ott(sl, x):
                u = sl.unit(OFF_OUT)
                if not u:
                    return
                wait_bank(pe, TEN_O, sl, f"ott{x}")
                wait(pe, "oev", at(4, u, 2 * x + 2))
                for qt in range(TPS):
                    for y in range(2):
                        a = (2 * qt + y) * P
                        last = pe.transpose(psO[:, a:a + P], oT[:, 2 * x + y, P * qt:P * qt + P], Fc("ident"))
                last.then_inc(S["ott"], 1)

            def ob(sl):
                u = sl.unit(OFF_OUT)
                if not u:
                    return
                wait_bank(pe, TEN_O, sl, "ob")
                wait(pe, "norm", at(2, u, 2))
                for qt in range(TPS):
                    last = pe.transpose(psO[:, P * qt:P * qt + P],
                                        on[:, u.b % 2, qt, :, :].rearrange("p h d -> p (h d)"), Fc("ident"))
                last.then_inc(S["ob"], 1)

            def outproj(sl):
                u = sl.unit(OFF_OUT)
                if not u:
                    return
                wait(pe, "obev", at(1, u, 1))
                wait_bank(pe, TEN_O, sl, "op")
                for qt in range(TPS):
                    last = mm(psO[:, P * qt:P * qt + P], onT[:, P * qt:P * qt + P], W(u.layer, WO),
                              start=True, stop=True)
                last.then_inc(S["op"], 1)

            def xt(sl):
                u = sl.unit(OFF_LOAD)
                if not u:
                    return
                wait_bank(pe, TEN_M, sl, "xt")
                if u.layer == 1:
                    wait(pe, "lnout2", at(2, u, 2, NSEQ))
                else:
                    wait(pe, "lnout", at(2, u, 2))
                for i in range(TPS):
                    src = xn2[:, u.b % 2, i, :] if u.layer == 1 else xn[:, u.b, i, :]
                    last = pe.transpose(psM[:, P * i:P * i + P], src, Fc("ident"))
                last.then_inc(S["xt"], 1)

            def x_of(u):
                return cT[:, u.b % 2, :] if u.layer == 1 else xT[:, u.b % 2, :]

            def project(sl, name):
                u = sl.unit(OFF_SPREAD if name == "v" else OFF_PROJ, (1,) if name == "rot" else (0, 1, 2))
                if not u:
                    return
                if name == "qk":
                    if u.layer == 1:
                        wait(pe, "conv", at(1, u, 1, NSEQ))
                    else:
                        wait(pe, "xtev", at(1, u, 1))
                wait_bank(pe, TEN_M, sl, name)
                x = x_of(u)
                if name == "v":
                    for i in range(TPS):
                        last = mm(psM[:, P * i:P * i + P], x[:, P * i:P * i + P], W(u.layer, WV), start=True, stop=True)
                else:
                    for i, w in enumerate((WQ, WK) if name == "qk" else (WRQ, WRK)):
                        last = mm(psM[:, SEQ * i:SEQ * i + SEQ], W(u.layer, w), x, start=True, stop=True)
                last.then_inc(S[name], 1)

            def sumq(sl):
                u = sl.unit(OFF_PROJ, (0,))
                if not u:
                    return
                wait_bank(pe, TEN_M, sl, "sp")
                wait(pe, "qkev", at(2, u, 2))
                for i in range(TPS):
                    last = mm(psM[:, H * i:H * i + H], qkf[:, 0, P * i:P * i + P], Fc("heads"), start=True, stop=True)
                last.then_inc(S["sp"], 1)

            def mt(sl):
                u = sl.unit(OFF_MAX)
                if not u:
                    return
                wait_bank(pe, TEN_M, sl, "mt")
                wait(pe, "mlo", at(1, u, 1))
                for i in range(TPS):
                    last = pe.transpose(psM[:, :].bitcast(bf16)[:, P * i:P * i + P],
                                        mparts[:, i, :, :].rearrange("p a h -> p (a h)"), Bc("ident"))
                last.then_inc(S["mt"], 1)

            def route(sl, name):
                u = sl.unit(OFF_ROUTE if name == "hT" else OFF_LOGIT, (1, 2))
                if not u:
                    return
                wait_bank(pe, TEN_M, sl, name)
                if name == "hT":
                    wait(pe, "hfin", at(1, u, 1, NSEQ))
                    for i in range(TPS):
                        last = pe.transpose(psM[:, P * i:P * i + P], hn[:, u.b % 2, i, :], Fc("ident"))
                    last.then_inc(S["hT"], 1)
                else:
                    wait(pe, "hTev", at(1, u, 1, NSEQ))
                    w = wr[:, 0:E0] if u.layer == 1 else wr[:, E0:E0 + E1]
                    n = w.shape[-1]
                    for i in range(TPS):
                        last = mm(psM[:, n * i:n * i + n], hT[:, P * i:P * i + P], w, start=True, stop=True)
                    last.then_inc(S["lg"], 1)

            def step(sl):
                score(sl, 0)
                scoreT(sl, 0)
                pv(sl, "pv3", 3)
                project(sl, "v")
                score(sl, 1)
                scoreT(sl, 1)
                ott(sl, 0)
                route(sl, "lg")
                score(sl, 2)
                scoreT(sl, 2)
                pv(sl, "pv0", 0)
                project(sl, "qk")
                score(sl, 3)
                scoreT(sl, 3)
                ott(sl, 1)
                sumq(sl)
                project(sl, "rot")
                score(sl, 4)
                scoreT(sl, 4)
                pv(sl, "pv1", 1)
                mt(sl)
                score(sl, 5)
                scoreT(sl, 5)
                ob(sl)
                score(sl, 6)
                scoreT(sl, 6)
                pv(sl, "pv2", 2)
                route(sl, "hT")
                score(sl, 7)
                scoreT(sl, 7)
                outproj(sl)
                xt(sl)

            def mix(i):
                ntl, E, F = ((NTILE0, E0, F0), (NTILE1, E1, F1))[i]
                m = {k: v[i] for k, v in M.items()}
                pe.wait_ge(m["dve"], 6)
                mm(psT[1][:, 0:E], Bc("ones"), cnt[:, 0:E], start=True, stop=True)
                rank = psT[0][:, 0:NT * E].rearrange("p (t e) -> p t e", e=E)
                mm(rank, Bc("before"), oh[:, :, 0:E], start=True, stop=False, skip_group_check=True)
                for tt in range(NT - 1):
                    last = mm(rank[:, tt + 1:NT, :], Bc("ones"),
                              oh[:, tt:tt + 1, 0:E].to_broadcast([P, NT - 1 - tt, E]),
                              start=False, stop=(tt == NT - 2), skip_group_check=True)
                last.then_inc(m["rank"], 1)
                pe.wait_ge(m["te"], 1)
                if i == 0:
                    pe.wait_ge(S["wload"], NLATE)
                else:
                    pe.wait_ge(S["dn1load"], 32)
                nk = F // P

                def turn(j, it):
                    jx = j + 2 * it
                    pe.wait_ge(MD["gath"][i][j % 2], 16 * (j // 2 + it + 1))
                    if j >= 1:
                        pe.wait_ge(m["htev"], jx)
                    pe.transpose(psM[:, 0:P], xf[:, j % 2, :], Fc("ident")).then_inc(m["ht"], 1)

                def upward(j, it):
                    jx = j + 2 * it
                    e = pe.value_load(tei[i][0:1, bass.ds(jx, 1)], min_val=0, max_val=E - 1)
                    pe.wait_ge(m["htev"], jx + 1)
                    if j >= 2:
                        pe.wait_ge(m["act"], jx - 1)
                    for n in range(2 if i == 0 else 1):
                        w = F0 if i == 0 else F1
                        last = mm(psT[j % 2][:, 512 * n:512 * n + w], xfT[:, j % 2, :],
                                  up[i][:, bass.ds(e * (2 * F0 if i == 0 else F1) + n * F0, w)], start=True, stop=True)
                    last.then_inc(m["up"], 1)

                def turn_act(j, it):
                    jx = j + 2 * it
                    pe.wait_ge(m["act"], jx + 1)
                    if j >= 2:
                        pe.wait_ge(m["atev"], jx - 1)
                    for n in range(nk):
                        last = pe.transpose(psS[:, 512 * (j % 2) + P * n:512 * (j % 2) + P * n + P],
                                            mixact[:, j % 2, P * n:P * n + P], Fc("ident"))
                    last.then_inc(m["at"], 1)

                def downward(j, it):
                    jx = j + 2 * it
                    e = pe.value_load(tei[i][0:1, bass.ds(jx, 1)], min_val=0, max_val=E - 1)
                    pe.wait_ge(m["atev"], jx + 1)
                    if j >= 1:
                        pe.wait_ge(m["yev"], jx)
                    for n in range(nk):
                        last = mm(psO[:, 0:C], actT[:, j % 2, P * n:P * n + P],
                                  dn[i][:, bass.ds(e * F + n * C, C)], start=(n == 0), stop=(n == nk - 1))
                    last.then_inc(m["prod"], 1)

                turn(0, 0)
                turn(1, 0)
                upward(0, 0)


                def tile(j, it):
                    jx = j + 2 * it
                    if j + 1 < ntl:
                        turn(j + 1, it)
                    turn_act(j - 1, it)
                    upward(j, it)
                    downward(j - 1, it)

                tile(1, 0)
                with pe.Fori(0, (ntl - 4) // 2) as it:
                    for j in range(2):
                        tile(2 + j, it)
                tile(ntl - 2, 0)
                tile(ntl - 1, 0)
                turn_act(ntl - 1, 0)
                downward(ntl - 1, 0)

            pe.wait_ge(S["const"], NCONST)
            slots(pe, step, 0, 2 * NSEQ)
            mix(0)
            slots(pe, step, 2 * NSEQ, 3 * NSEQ)
            mix(1)

        @block.scalar
        def _(act_e):
            act = act_e
            actv = act.activation

            def exps(sl, g):
                u = sl.unit(OFF_ATT)
                if not u:
                    return
                wait(act, "tready", at(NSTEP, u, g + 1))
                wait(act, "pv", at(GROUPS, u, g // 2 - 1))
                src, dst = psT[g % 2][:, 0:SW], pr[:, g % 4, :]
                if u.layer == 0:
                    src = psT[g % 2][:, :].rearrange("p (b n) -> p b n", b=2)[:, :, 0:HPS * BAND]
                    dst = dst.rearrange("p (b n) -> p b n", b=2)
                actv(dst, src, ACT.Exp).then_inc(S["exp"], 1)

            def oev(sl, gg):
                u = sl.unit(OFF_OUT if gg == 3 else OFF_ATT)
                if not u:
                    return
                wait(act, "pv", at(GROUPS, u, gg + 1))
                wait(act, "ott", at(2, u, gg // 2 - 1))
                actv(oT[:, gg, :], psO[:, 0:SEQ], ACT.Copy).then_inc(S["oev"], 1)

            def xtev(sl):
                u = sl.unit(OFF_PROJ)
                if not u:
                    return
                wait(act, "xt", at(1, u, 1))
                wait(act, "v", at(1, u, -1))
                if u.layer == 1:
                    actv(xT[:, u.b % 2, :], psM[:, 0:SEQ], ACT.Identity, bias=cols[:, LN1B:LN1B + 1],
                         scale=cols[:, LN1W:LN1W + 1]).then_inc(S["xtev"], 1)
                else:
                    actv(xT[:, u.b % 2, :], psM[:, 0:SEQ], ACT.Copy).then_inc(S["xtev"], 1)

            def qkev(sl):
                u = sl.unit(OFF_PROJ, (0, 2))
                if not u:
                    return
                wait(act, "qk", at(1, u, 1))
                wait(act, "lo", at(1, u, 0))
                if u.layer == 0:
                    wait(act, "sp", at(1, u, 0))
                bq, bk = (BQ0, BK0) if u.layer == 0 else (BQ2S, BK2)
                actv(qkf[:, 0, :], psM[:, 0:SEQ], ACT.Identity, bias=cols[:, bq:bq + 1],
                     scale=1.0 if u.layer == 0 else float(D) ** -0.5).then_inc(S["qkev"], 1)
                actv(qkf[:, 1, :], psM[:, SEQ:2 * SEQ], ACT.Identity, bias=cols[:, bk:bk + 1],
                     scale=1.0).then_inc(S["qkev"], 1)

            def part(sl, n):
                u = sl.unit(OFF_PROJ)
                if not u:
                    return
                if n == 0:
                    if u.layer == 1:
                        wait(act, "ropeadd", at(1, u, 1, NSEQ))
                    else:
                        wait(act, "qkev", at(2, u, 2))
                    moved(act, "rep", u, 1, n=NREP)
                else:
                    wait(act, "resid", at(1, u, 1))
                actv(parts[:, n], qkf[:, :, :], ACT.Copy).then_inc(S[("hi", "mid")[n]], 1)

            def mtev(sl):
                u = sl.unit(OFF_MAX)
                if not u:
                    return
                wait(act, "mt", at(1, u, 1))
                moved(act, "mrow", u, 1)
                actv(mT[:, :], psM[:, :].bitcast(bf16)[0:PARTS * H, 0:SEQ], ACT.Copy).then_inc(S["mtev"], 1)

            def epads(sl):
                u = sl.unit(OFF_MAX, (0,))
                if not u:
                    return
                wait(act, "earg", at(1, u, 1))
                wait(act, "pnum", at(2, u, 2 - 2 * NBUF))
                actv(epad[:, u.b, :, :], earg[:, u.b % 2, :, :], ACT.Exp).then_inc(S["epad"], 1)

            def obev(sl):
                u = sl.unit(OFF_OUT)
                if not u:
                    return
                wait(act, "ob", at(1, u, 1))
                wait(act, "op", at(1, u, 0))
                actv(onT[:, :], psO[:, 0:SEQ], ACT.Copy).then_inc(S["obev"], 1)

            def hTev(sl):
                u = sl.unit(OFF_ROUTE, (1, 2))
                if not u:
                    return
                wait(act, "hT", at(1, u, 1, NSEQ))
                wait(act, "lg", at(1, u, 0, NSEQ))
                actv(hT[:, :], psM[:, 0:SEQ], ACT.Copy).then_inc(S["hTev"], 1)

            def step(sl):
                xtev(sl)
                exps(sl, 0)
                oev(sl, 3)
                exps(sl, 1)
                epads(sl)
                exps(sl, 2)
                oev(sl, 0)
                qkev(sl)
                exps(sl, 3)
                exps(sl, 4)
                oev(sl, 1)
                mtev(sl)
                exps(sl, 5)
                part(sl, 0)
                obev(sl)
                exps(sl, 6)
                oev(sl, 2)
                hTev(sl)
                exps(sl, 7)
                part(sl, 1)

            def mix(i):
                ntl, F = ((NTILE0, F0), (NTILE1, F1))[i]
                m = {k: v[i] for k, v in M.items()}

                def tile(j, it):
                    jx = j + 2 * it
                    act.wait_ge(m["ht"], jx + 1)
                    if j >= 2:
                        act.wait_ge(m["up"], jx - 1)
                    actv(xfT[:, j % 2, :], psM[:, 0:P], ACT.Copy).then_inc(m["htev"], 1)

                def nonlin(j, it):
                    jx = j + 2 * it
                    if i == 0:
                        act.wait_ge(m["up"], jx + 1)
                        if j >= 2:
                            act.wait_ge(m["act"], jx - 1)
                        actv(gate[:, j % 2, 0:F], psT[j % 2][:, 0:F], ACT.Silu).then_inc(m["actg"], 1)
                    else:
                        act.wait_ge(m["actg"], jx + 1)
                        if j >= 2:
                            act.wait_ge(m["at"], jx - 1)
                        actv(mixact[:, j % 2, 0:F], gate[:, j % 2, 0:F], ACT.Gelu).then_inc(m["act"], 1)

                def result(j, it):
                    jx = j + 2 * it
                    if i == 0:
                        act.wait_ge(m["prod"], jx + 1)
                        if j >= 2:
                            act.wait_ge(MD["store"][i][j % 2], 16 * (j // 2 + it))
                        actv(yt[:, j % 2, :], psO[:, 0:C], ACT.Copy).then_inc(m["yev"], 1)

                def three(j, it):
                    jx = j + 2 * it
                    if j + 1 < ntl:
                        tile(j + 1, it)
                    nonlin(j, it)
                    result(j - 1, it)

                act.wait_ge(m["xres"], 16)
                tile(0, 0)
                tile(1, 0)
                nonlin(0, 0)
                three(1, 0)
                with act.Fori(0, (ntl - 4) // 2) as it:
                    for j in range(2):
                        three(2 + j, it)
                three(ntl - 2, 0)
                three(ntl - 1, 0)
                result(ntl - 1, 0)

            act.wait_ge(S["const"], NCONST)
            act.wait_ge(S["setup"], 3)
            slots(act, step, 0, 2 * NSEQ)
            mix(0)
            slots(act, step, 2 * NSEQ, 3 * NSEQ)
            mix(1)

        @block.vector
        def _(dve):
            tt, ts = dve.tensor_tensor, dve.tensor_scalar

            def reduce(sl, g):
                u = sl.unit(OFF_SCORE)
                if not u:
                    return
                wait(dve, "sready", at(NSTEP, u, g + 1))
                if g == 0:
                    wait(dve, "nmax", at(2, u, -2))
                if u.layer == 0:
                    src = psS[:, :].rearrange("p (b n) -> p b n", b=2)[:, :, 0:HPS * BAND].rearrange(
                        "p b (h n) -> p b h n", h=HPS)
                    n = 4
                else:
                    src = psS[:, 0:SW].rearrange("p (b n) -> p b n", n=P)
                    n = 6
                dve.tensor_reduce(nred[:, u.b % 2, g, 0:n], src, op=ALU.max, axis=AX.X,
                                  negate=True).then_inc(S["red"], 1)

            def nmaxs(sl):
                u = sl.unit(OFF_MAX)
                if not u:
                    return
                b = u.b % 2
                wait(dve, "red", at(NSTEP, u, NSTEP))
                wait(dve, "mres", at(1, u, -1))
                r = nred[:, b, :, :]
                o = nmax[:, b, :, :].rearrange("p q (s h) -> p q s h", h=HPS)
                if u.layer == 0:
                    wait(dve, "spev", at(1, u, 1))
                    sp4 = spad[:, u.b, :, :].rearrange("p q (s h) -> p q s h", h=HPS)
                    for q in range(TPS):
                        tt(o[:, q, :, :], r[:, :, HPS * q:HPS * q + HPS], sp4[:, q, :, :], ALU.min).then_inc(S["nmax"], 1)
                    wait(dve, "nmax", at(2, u, 2))
                    wait(dve, "epad", at(1, u, -1))
                    tt(earg[:, b, :, :], nmax[:, b, :, :], spad[:, u.b, :, :], ALU.subtract).then_inc(S["earg"], 1)
                else:
                    r2 = r[:, :, 0:4].rearrange("p s (h k) -> p s h k", k=2)
                    tt(o[:, 1, :, :], r2[:, :, :, 0], r2[:, :, :, 1], ALU.min).then_inc(S["nmax"], 1)
                    dve.tensor_copy(o[:, 0, :, :], r[:, :, 4:6]).then_inc(S["nmax"], 1)

            def stats(x, st, s1):
                for i in range(TPS):
                    dve.bn_stats(st[:, i, :], x[:, i, :]).then_inc(S[s1], 1)

            def aggr(st, m, s2):
                for i in range(TPS):
                    dve.bn_aggr(m[:, i, :], st[:, i, :]).then_inc(S[s2], 1)

            def normal(o, x, m, r, done):
                for i in range(TPS):
                    ts(o[:, i, :], x[:, i, :], m[:, i, 0:1], r[:, i, 0:1], ALU.subtract, ALU.mult).then_inc(S[done], 1)

            def ln_stats(sl):
                u = sl.unit(OFF_LOAD)
                if not u:
                    return
                moved(dve, "xin", u)
                stats(xin[:, u.b], stat[:, u.b], "stats")

            def aggregate(sl, g, off, layers, name, st, m, first):
                u = sl.unit(off, layers)
                if u:
                    wait(dve, name, at(2, u, 2, first))
                reduce(sl, g)
                if u:
                    b = u.b if st is not stat3 else u.b % 2
                    aggr(st[:, b], m[:, b], "mvs" + name[5:])

            def ln_apply(sl):
                u = sl.unit(OFF_LOAD)
                if not u:
                    return
                wait(dve, "rstds", at(1, u, 1))
                wait(dve, "mvs", at(2, u, 2))
                if u.layer != 1:
                    wait(dve, "xt", at(1, u, 1 - NBUF))
                elif u.rep >= NSEQ + NBUF:
                    moved(dve, "ystore", u, 2, NSEQ)
                else:
                    wait(dve, "xt", at(1, u, 1 - NBUF))
                normal(xn[:, u.b], xin[:, u.b], mv[:, u.b], rstd[:, u.b], "lnout")
                if u.layer == 1:
                    wait(dve, "lnout", at(2, u, 2))
                    stats(xn[:, u.b], stat2[:, u.b], "stats2")

            def ln_again(sl):
                u = sl.unit(OFF_LOAD, (1,))
                if not u:
                    return
                wait(dve, "rstds2", at(1, u, 1, NSEQ))
                wait(dve, "mvs2", at(2, u, 2, NSEQ))
                wait(dve, "xt", at(1, u, -1))
                normal(xn2[:, u.b % 2], xn[:, u.b], mv2[:, u.b], rstd2[:, u.b], "lnout2")

            def ln3_stats(sl):
                u = sl.unit(OFF_ROUTE, (1, 2))
                if not u:
                    return
                b = u.b % 2
                wait(dve, "zout", at(1, u, 1))
                stats(zb[:, b], stat3[:, b], "stats3")

            def ln3_apply(sl):
                u = sl.unit(OFF_ROUTE, (1, 2))
                if not u:
                    return
                b = u.b % 2
                wait(dve, "rstds3", at(1, u, 1, NSEQ))
                wait(dve, "mvs3", at(2, u, 2, NSEQ))
                moved(dve, "hstore", u, 2, NSEQ)
                wait(dve, "hT", at(1, u, -1, NSEQ))
                if u.layer == 1:
                    normal(hn[:, b], zb[:, b], mv3[:, b], rstd3[:, b], "hout")
                else:
                    for i in range(TPS):
                        x = ts(hn[:, b, i, :], zb[:, b, i, :], mv3[:, b, i, 0:1], rstd3[:, b, i, 0:1],
                               ALU.subtract, ALU.mult)
                    x.then_inc(S["hfin"], 1)

            def rope_cos(sl):
                u = sl.unit(OFF_PROJ, (1,))
                if not u:
                    return
                wait(dve, "qk", at(1, u, 1))
                wait(dve, "lo", at(1, u, 0))
                tt(qkf[:, :, :], psM[:, :].rearrange("p (a t) -> p a t", a=2),
                   cf[:, CF["cosq"][0]:CF["cosk"][1]].rearrange("p (a t) -> p a t", a=2), ALU.mult).then_inc(S["qkev"], 2)

            def rope_sin(sl):
                u = sl.unit(OFF_PROJ, (1,))
                if not u:
                    return
                wait(dve, "rot", at(1, u, 1, NSEQ))
                wait(dve, "ropeadd", at(1, u, 0, NSEQ))
                tt(qks[:, :, :], psM[:, :].rearrange("p (a t) -> p a t", a=2),
                   cf[:, CF["sinq"][0]:CF["sink"][1]].rearrange("p (a t) -> p a t", a=2),
                   ALU.mult).then_inc(S["rotev"], 1)

            def sp_ev(sl):
                u = sl.unit(OFF_PROJ, (0,))
                if not u:
                    return
                wait(dve, "sp", at(1, u, 1))
                tt(spad[:, u.b, :, :], psM[:, 0:TPS * H].rearrange("p (q h) -> p q h", q=TPS),
                   Fc("padfar").unsqueeze(2).to_broadcast([P, TPS, H]), ALU.add).then_inc(S["spev"], 1)

            def v_ev(sl):
                u = sl.unit(OFF_SPREAD)
                if not u:
                    return
                wait(dve, "v", at(1, u, 1))
                wait(dve, "pv", at(GROUPS, u, GROUPS - GROUPS * NBUF))
                src = psM[:, 0:TPS * C].rearrange("p (a h d) -> p a h d", a=TPS, h=H)
                dst = vv[:, u.b, :, :, 0:D]
                if u.layer == 1:
                    dve.tensor_copy(dst, src).then_inc(S["vev"], 1)
                else:
                    bias = rows[:, BV0 if u.layer == 0 else BV2, :].rearrange("p (h d) -> p h d", h=H)
                    tt(dst, src, bias.unsqueeze(1).to_broadcast([P, TPS, H, D]), ALU.add).then_inc(S["vev"], 1)

            def norm(sl, x):
                u = sl.unit(OFF_OUT)
                if not u:
                    return
                b = u.b % 2
                wait(dve, "ott", at(2, u, x + 1))
                o = psO[:, :].rearrange("p (q h d) -> p q h d", q=TPS, h=8)
                num, dn_, r = o[:, :, :, 0:D], o[:, :, :, D], rden[:, b, :, :, :].rearrange("p q a b -> p q (a b)")
                if u.layer == 0:
                    wait(dve, "epad64", at(1, u, 1))
                    e = epad[:, u.b, :, 8 * x:8 * x + 8]
                    wait(dve, "norm", at(2, u, x))
                    dd = den[:, b, :, :, :].rearrange("p q a b -> p q (a b)")
                    tt(dd, dn_, e, ALU.add).then_inc(S["den"], 1)
                    for q in range(TPS):
                        y = tt(pnum[:, q, :, :], num[:, q, :, :], e[:, q, :].unsqueeze(2).to_broadcast([P, 8, D]),
                               ALU.subtract)
                    y.then_inc(S["pnum"], 1)
                    wait(dve, "den", at(2, u, x + 1))
                    dn_, num = dd, pnum[:, :, :, :]
                dve.reciprocal(r, dn_).then_inc(S["rden"], 1)
                wait(dve, "rden", at(2, u, x + 1))
                if u.layer == 0:
                    wait(dve, "pnum", at(2, u, x + 1))
                if x == 0:
                    wait(dve, "ob", at(1, u, -1))
                tt(on[:, b, :, 8 * x:8 * x + 8, :], num, r.unsqueeze(3).to_broadcast([P, TPS, 8, D]),
                   ALU.mult).then_inc(S["norm"], 1)

            def residual(sl):
                u = sl.unit(OFF_OUT)
                if not u:
                    return
                b = u.b % 2
                wait(dve, "op", at(1, u, 1))
                if u.layer == 1:
                    moved(dve, "yresdma", u, 0, NSEQ)
                    r = yres
                else:
                    wait(dve, "rbias", (u.n - (0 if u.layer == 0 else NSEQ)) + 1)
                    r = xres
                moved(dve, "xstore", u, 2)
                if u.layer >= 1 and u.rep >= NSEQ + 2:
                    wait(dve, "hfin", at(1, u, -1, NSEQ))
                tt(zb[:, b, :, :], psO[:, 0:TPS * C].rearrange("p (q c) -> p q c", q=TPS), r[:, b, :, :],
                   ALU.add).then_inc(S["zout"], 1)

            def lg_ev(sl):
                u = sl.unit(OFF_LOGIT, (1, 2))
                if not u:
                    return
                E = (E0, E1)[u.layer - 1]
                wait(dve, "lg", at(1, u, 1, NSEQ))
                dst = lg[u.layer - 1][:, bass.ds(u.s * TPS, TPS), :]
                src = psM[:, 0:TPS * E].rearrange("p (t e) -> p t e", e=E)
                if u.layer == 1:
                    dve.tensor_copy(dst, src).then_inc(S["lgev"], 1)
                else:
                    tt(dst, src, br[:, :].unsqueeze(1).to_broadcast([P, TPS, E]), ALU.add).then_inc(S["lgev"], 1)

            def step(sl):
                nmaxs(sl)
                reduce(sl, 0)
                ln3_stats(sl)
                v_ev(sl)
                aggregate(sl, 1, OFF_ROUTE, (1, 2), "stats3", stat3, mv3, NSEQ)
                ln_stats(sl)
                norm(sl, 0)
                lg_ev(sl)
                aggregate(sl, 2, OFF_LOAD, (0, 1, 2), "stats", stat, mv, 0)
                rope_cos(sl)
                reduce(sl, 3)
                ln3_apply(sl)
                sp_ev(sl)
                norm(sl, 1)
                rope_sin(sl)
                reduce(sl, 4)
                ln_apply(sl)
                aggregate(sl, 5, OFF_LOAD, (1,), "stats2", stat2, mv2, NSEQ)
                reduce(sl, 6)
                ln_again(sl)
                reduce(sl, 7)
                residual(sl)

            def mix(i):
                ntl, E, F = ((NTILE0, E0, F0), (NTILE1, E1, F1))[i]
                m = {k: v[i] for k, v in M.items()}
                made = [0]

                def link(ins):
                    made[0] += 1
                    ins.then_inc(m["dve"], 1)
                    dve.wait_ge(m["dve"], made[0])

                dve.wait_ge(S["lgev"], NSEQ * (i + 1))
                L = lg[i][:, :, :]
                eid = Fc("eid")[:, 0:E].unsqueeze(1).to_broadcast([P, NT, E])
                link(dve.tensor_reduce(top[:, :], L, op=ALU.max, axis=AX.X))
                link(tt(eq[:, :, 0:E], L, top[:, :].unsqueeze(2).to_broadcast([P, NT, E]), ALU.is_equal))
                link(tt(eqi[:, :, 0:E], eq[:, :, 0:E], eid, ALU.mult))
                link(dve.tensor_reduce(pick[:, :], eqi[:, :, 0:E], op=ALU.min, axis=AX.X))
                link(tt(oh[:, :, 0:E], eid, pick[:, :].unsqueeze(2).to_broadcast([P, NT, E]), ALU.is_equal))
                with nc.allow_low_precision(reason="counts to 32 are exact in bfloat16"):
                    link(dve.tensor_reduce(cnt[:, 0:E], oh[:, :, 0:E].rearrange("p t e -> p e t"),
                                           op=ALU.add, axis=AX.X))
                dve.wait_ge(m["rank"], 1)
                link(ts(padi[:, 0:E], psT[1][:, 0:E], float(P - 1), None, ALU.add))
                link(ts(padi2[:, 0:E], padi[:, 0:E], 7, 7, ALU.logical_shift_right, ALU.logical_shift_left))
                link(dve.tensor_copy(padf[:, 0:E], padi2[:, 0:E]))
                link(dve.memset(base[:, 0:1], 0.0))
                for e in range(E):
                    link(tt(base[:, e + 1:e + 2], base[:, e:e + 1], padf[:, e:e + 1], ALU.add))
                link(tt(rk[:, :, 0:E], psT[0][:, 0:NT * E].rearrange("p (t e) -> p t e", e=E),
                        base[:, 0:E].unsqueeze(1).to_broadcast([P, NT, E]), ALU.add))
                link(tt(rk2[:, :, 0:E], rk[:, :, 0:E], oh[:, :, 0:E], ALU.mult))
                link(dve.tensor_reduce(destf[:, :], rk2[:, :, 0:E], op=ALU.add, axis=AX.X))
                dve.tensor_copy(dest[i][:, :], destf[:, :]).then_inc(m["dest"], 1)
                link(tt(ge[:, 0:ntl, 0:E - 1], cf[0:1, CF["start"][0]:CF["start"][0] + ntl].unsqueeze(2).to_broadcast(
                    [1, ntl, E - 1]), base[0:1, 1:E].unsqueeze(1).to_broadcast([1, ntl, E - 1]), ALU.is_ge))
                link(dve.tensor_reduce(tef[:, 0:ntl], ge[:, 0:ntl, 0:E - 1], op=ALU.add, axis=AX.X))
                dve.tensor_copy(tei[i][:, :], tef[:, 0:ntl]).then_inc(m["te"], 1)
                if i == 1:
                    dve.wait_ge(m["te"], 1)
                    dve.wait_ge(m["bias"], 32)

                def hidden(j, it):
                    jx = j + 2 * it
                    if i == 0:
                        dve.wait_ge(m["actg"], jx + 1)
                        if j >= 2:
                            dve.wait_ge(m["at"], jx - 1)
                        tt(mixact[:, j % 2, 0:F], gate[:, j % 2, 0:F], psT[j % 2][:, 512:512 + F],
                           ALU.mult).then_inc(m["act"], 1)
                    else:
                        e = dve.value_load(tei[i][0:1, bass.ds(jx, 1)], min_val=0, max_val=E - 1)
                        dve.wait_ge(m["up"], jx + 1)
                        if j >= 2:
                            dve.wait_ge(m["act"], jx - 1)
                        tt(gate[:, j % 2, 0:F], psT[j % 2][:, 0:F], b1r[:, bass.ds(e * F, F)],
                           ALU.add).then_inc(m["actg"], 1)

                def turned(j, it):
                    jx = j + 2 * it
                    dve.wait_ge(m["at"], jx + 1)
                    if j >= 2:
                        dve.wait_ge(m["prod"], jx - 1)
                    dve.tensor_copy(actT[:, j % 2, 0:F], psS[:, 512 * (j % 2):512 * (j % 2) + F]).then_inc(m["atev"], 1)

                def result(j, it):
                    jx = j + 2 * it
                    if i == 1:
                        e = dve.value_load(tei[i][0:1, bass.ds(jx, 1)], min_val=0, max_val=E - 1)
                        dve.wait_ge(m["prod"], jx + 1)
                        if j >= 2:
                            dve.wait_ge(MD["store"][i][j % 2], 16 * (j // 2 + it))
                        tt(yt[:, j % 2, :], psO[:, 0:C], b2r[:, bass.ds(e * C, C)], ALU.add).then_inc(m["yev"], 1)

                def three(j, it):
                    jx = j + 2 * it
                    turned(j - 1, it)
                    hidden(j, it)
                    result(j - 1, it)

                dve.wait_ge(m["xres"], 16)
                hidden(0, 0)
                three(1, 0)
                with dve.Fori(0, (ntl - 4) // 2) as it:
                    for j in range(2):
                        three(2 + j, it)
                three(ntl - 2, 0)
                three(ntl - 1, 0)
                turned(ntl - 1, 0)
                result(ntl - 1, 0)
                for q in range(NT // 4):
                    dve.wait_ge(MD["fin"][i][q], 64)
                    tt(xg[:, 4 * q:4 * q + 4, :], xg[:, 4 * q:4 * q + 4, :], h2[:, 4 * q:4 * q + 4, :],
                       ALU.add).then_inc(m["add"], 1)

            dve.memset(vv[:, :, :, :, :], 0.0).then_inc(S["setup"], 1)
            dve.wait_ge(S["setup"], 1)
            dve.memset(vv[:, :, :, :, D:D + 1], 1.0).then_inc(S["setup"], 1)
            dve.wait_ge(S["const"], NCONST)
            ts(cols[:, BQ2S:BQ2S + 1], cols[:, BQ2:BQ2 + 1], float(D) ** -0.5, None, ALU.mult).then_inc(S["setup"], 1)
            dve.wait_ge(S["setup"], 3)
            slots(dve, step, 0, 2 * NSEQ)
            mix(0)
            made = [0]

            def link(ins):
                made[0] += 1
                ins.then_inc(S["pos"], 1)
                dve.wait_ge(S["pos"], made[0])

            dve.wait_ge(S["wload"], NLATE)
            dve.wait_ge(S["pv"], 2 * NSEQ * GROUPS)
            link(dve.tensor_reduce(posc[:, 0, :], posr[:, :, :], op=ALU.add, axis=AX.X))
            for a in range(PARTS):
                link(dve.tensor_copy(poscp[:, a, :], posc[:, a, :]))
                if a + 1 < PARTS:
                    link(tt(posc[:, a + 1, :], posc[:, a, :], poscp[:, a, :], ALU.subtract))
            dve.tensor_copy(poscb, poscp[:, :, :].unsqueeze(3).to_broadcast([1, PARTS, 8, SEQ])).then_inc(S["posb"], 1)
            dve.wait_ge(S["posb"], 1)
            slots(dve, step, 2 * NSEQ, 3 * NSEQ)
            mix(1)

        @block.gpsimd
        def _(pool):
            tt, ts, cp = pool.tensor_tensor, pool.tensor_scalar, pool.tensor_copy

            def rstds(u, first, m, v, r, need, mid, done, per):
                wait(pool, need, at(2, u, 2, first))
                tt(v[:, :, 1:2], m[:, :, 1:2], eps[:, :].unsqueeze(2), ALU.add).then_inc(S[mid], 1)
                wait(pool, mid, at(1, u, 1, first))
                tt(r[:, :, 0:1], v[:, :, 1:2], half[:, :].unsqueeze(2), ALU.pow).then_inc(S[done], 1)

            def xz(sl):
                u = sl.unit(OFF_ROUTE, (1,))
                if not u:
                    return
                wait(pool, "zout", at(1, u, 1))
                moved(pool, "resdma", u)
                moved(pool, "xstore", u, 2)
                tt(xzb[:, u.b % 2], zb[:, u.b % 2], xres[:, u.b % 2], ALU.add).then_inc(S["xz"], 1)

            def split_max(sl):
                u = sl.unit(OFF_MAX)
                if not u:
                    return
                b = u.b % 2
                zero_m = nil[:, :].unsqueeze(2).to_broadcast([P, TPS, H])
                wait(pool, "nmax", at(2, u, 2))
                wait(pool, "mt", at(1, u, 0))
                tt(mparts[:, :, 0, :], nmax[:, b], zero_m, ALU.add).then_inc(S["mhi"], 1)
                wait(pool, "mhi", at(1, u, 1))
                tt(mres[:, b], nmax[:, b], mparts[:, :, 0, :], ALU.subtract).then_inc(S["mres"], 1)
                wait(pool, "mres", at(1, u, 1))
                tt(mparts[:, :, 1, :], mres[:, b], zero_m, ALU.add).then_inc(S["mmid"], 1)
                wait(pool, "mmid", at(1, u, 1))
                tt(mparts[:, :, 2, :], mres[:, b], mparts[:, :, 1, :], ALU.subtract).then_inc(S["mlo"], 1)

            def rope_add(sl):
                u = sl.unit(OFF_PROJ, (1,))
                if not u:
                    return
                wait(pool, "rotev", at(1, u, 1, NSEQ))
                wait(pool, "qkev", at(2, u, 2))
                tt(qkf[:, :, :], qkf[:, :, :], qks[:, :, :], ALU.add).then_inc(S["ropeadd"], 1)

            def split(sl):
                u = sl.unit(OFF_PROJ)
                if not u:
                    return
                if u.layer == 1:
                    wait(pool, "ropeadd", at(1, u, 1, NSEQ))
                else:
                    wait(pool, "qkev", at(2, u, 2))
                if u.layer == 0:
                    wait(pool, "sp", at(1, u, 1))
                wait(pool, "hi", at(1, u, 1))
                tt(qkf[:, :, :], qkf[:, :, :], parts[:, 0], ALU.subtract).then_inc(S["resid"], 1)

            def split_rest(sl):
                u = sl.unit(OFF_SPREAD)
                if not u:
                    return
                wait(pool, "mid", at(1, u, 1))
                tt(parts[:, 2], qkf[:, :, :], parts[:, 1], ALU.subtract).then_inc(S["lo"], 1)

            def conv(sl):
                u = sl.unit(OFF_PROJ, (1,))
                if not u:
                    return
                b = u.b % 2
                x, o = xT[:, b, :], cT[:, b, :]
                wait(pool, "xtev", at(1, u, 1))
                wait(pool, "v", at(1, u, -1))
                tt(o, x, convw[:, 2:3].to_broadcast([P, SEQ]), ALU.mult).then_inc(S["tap0"], 1)
                tt(tap[:, 0, :], x, convw[:, 1:2].to_broadcast([P, SEQ]), ALU.mult).then_inc(S["tap1"], 1)
                tt(tap[:, 1, :], x, convw[:, 0:1].to_broadcast([P, SEQ]), ALU.mult).then_inc(S["tap2"], 1)
                wait(pool, "tap0", at(1, u, 1, NSEQ))
                wait(pool, "tap1", at(1, u, 1, NSEQ))
                tt(o[:, 1:SEQ], o[:, 1:SEQ], tap[:, 0, 0:SEQ - 1], ALU.add).then_inc(S["tap3"], 1)
                wait(pool, "tap2", at(1, u, 1, NSEQ))
                wait(pool, "tap3", at(1, u, 1, NSEQ))
                tt(o[:, 2:SEQ], o[:, 2:SEQ], tap[:, 1, 0:SEQ - 2], ALU.add).then_inc(S["conv"], 1)

            def res_bias(sl):
                u = sl.unit(OFF_OUT, (0, 2))
                if not u:
                    return
                moved(pool, "resdma", u)
                x, b = xres[:, u.b % 2], rows[:, BO0 if u.layer == 0 else BO2, :]
                tt(x, x, b.unsqueeze(1).to_broadcast([P, TPS, C]), ALU.add).then_inc(S["rbias"], 1)

            def affine(sl):
                u = sl.unit(OFF_ROUTE, (1,))
                if not u:
                    return
                x = hn[:, u.b % 2]
                wait(pool, "hout", at(2, u, 2, NSEQ))
                for name, r, s_ in (("hw", LN2W, ALU.mult), ("hfin", LN2B, ALU.add)):
                    tt(x, x, rows[:, r, :].unsqueeze(1).to_broadcast([P, TPS, C]), s_).then_inc(S[name], 1)
                    if name == "hw":
                        wait(pool, "hw", at(1, u, 1, NSEQ))

            def pads(sl):
                u = sl.unit(OFF_MAX, (0,))
                if not u:
                    return
                wait(pool, "epad", at(1, u, 1))
                e = epad[:, u.b]
                tt(e, e, Fc("pad64").unsqueeze(2).to_broadcast([P, TPS, H]), ALU.mult).then_inc(S["epad64"], 1)

            def step(sl):
                ur, ul = sl.unit(OFF_ROUTE, (1, 2)), sl.unit(OFF_LOAD)
                split_rest(sl)
                conv(sl)
                if ur:
                    b = ur.b % 2
                    rstds(ur, NSEQ, mv3[:, b], rstd3v[:, b], rstd3[:, b], "mvs3", "veps3", "rstds3", 1)
                split_max(sl)
                if ul:
                    rstds(ul, 0, mv[:, ul.b], rstdv[:, ul.b], rstd[:, ul.b], "mvs", "veps", "rstds", 1)
                xz(sl)
                pads(sl)
                res_bias(sl)
                affine(sl)
                rope_add(sl)
                if ul and ul.layer == 1:
                    rstds(ul, NSEQ, mv2[:, ul.b], rstd2v[:, ul.b], rstd2[:, ul.b], "mvs2", "veps2", "rstds2", 1)
                split(sl)

            def mix(i):
                m = {k: v[i] for k, v in M.items()}
                ntl = (NTILE0, NTILE1)[i]
                pool.wait_ge(S["hs0"], 64)
                for q in range(2):
                    pool.wait_ge(D_["hstore"][q], 8 * NSEQ * (i + 1))
                pool.wait_ge(m["dest"], 1)
                for tt_ in range(NT):
                    pool.indirect_dma_start(hs_d[i][:, :], bass.IndirectOffsetOnAxis(ap=dest[i][:, tt_:tt_ + 1], axis=0),
                                            h2[:, tt_, :], None).then_inc(m["scat"], 16)
                for q in range(2):
                    pool.wait_ge(MD["store"][i][q], 16 * ntl // 2)
                for tt_ in range(NT):
                    pool.indirect_dma_start(h2[:, tt_, :], None, ys_d[i][:, :],
                                            bass.IndirectOffsetOnAxis(ap=dest[i][:, tt_:tt_ + 1], axis=0)).then_inc(
                                                MD["fin"][i][tt_ // 4], 16)

            pool.memset(h2[:, :, :], 0.0).then_inc(S["zero"], 1)
            pool.memset(half[:, :], -0.5).then_inc(S["half"], 1)
            pool.memset(mparts[:, :, :, :], 0.0).then_inc(S["half"], 1)
            pool.memset(nil[:, :], 0.0).then_inc(S["half"], 1)
            pool.memset(eps[:, :], EPS).then_inc(S["half"], 1)
            pool.wait_ge(S["half"], 4)
            pool.wait_ge(S["const"], NCONST)
            slots(pool, step, 0, 2 * NSEQ)
            mix(0)
            slots(pool, step, 2 * NSEQ, 3 * NSEQ)
            mix(1)




def _constants():
    import numpy as np
    bf = mybir.dt.np(mybir.dt.bfloat16)
    far = -1e30
    i, j = np.arange(P)[:, None], np.arange(P)[None, :]
    cf = np.zeros((P, CF["all"]), np.float32)

    def put(dst, where, name, a):
        dst[:, where[name][0]:where[name][1]] = a

    inv = (np.float32(1.0) / np.float32(10000.0) ** (np.arange(0, D, 2, dtype=np.float32) / np.float32(D))).astype(np.float32)
    freqs = (np.arange(SEQ, dtype=np.float32)[:, None] * inv[None, :]).astype(np.float32)
    emb = np.concatenate([freqs, freqs], axis=-1).T
    cos, sin = np.cos(emb), np.sin(emb) * np.where(np.arange(D) < D // 2, -1, 1)[:, None]
    cos, sin = np.repeat(cos, H, axis=0), np.repeat(sin, H, axis=0)
    scale = float(D) ** -0.5
    put(cf, CF, "ident", np.eye(P))
    put(cf, CF, "cosq", cos * scale)
    put(cf, CF, "cosk", cos)
    put(cf, CF, "sinq", sin * scale)
    put(cf, CF, "sink", sin)
    put(cf, CF, "heads", np.arange(P)[:, None] % H == np.arange(H)[None, :])
    tok = np.arange(SEQ).reshape(TPS, P).T
    put(cf, CF, "padfar", np.where((tok < WS) | (tok >= SEQ - WS), 0.0, 1e30))
    put(cf, CF, "pad64", float(WS))
    put(cf, CF, "ones", 1.0)
    put(cf, CF, "eid", np.arange(8)[None, :] - 64.0)
    put(cf, CF, "start", P * np.arange(64)[None, :])
    cb = np.zeros((P, CB["all"]), bf)
    jb = np.arange(BAND)[None, :]
    band = np.concatenate([np.where(np.abs(jb - i) <= WS, 0, far), np.where((jb >= i) & (jb <= i + 2 * WS), 0, far)], 1)
    put(cb, CB, "ident", np.eye(P))
    put(cb, CB, "band", band)
    put(cb, CB, "causal_q", np.where(j > i, far, 0))
    put(cb, CB, "causal_k", np.where(j < i, far, 0))
    put(cb, CB, "before", i < j)
    put(cb, CB, "ones", 1.0)
    f = (1.0 / 1250.0 ** (np.arange(C // 2, dtype=np.float64) / (C // 2)))[:C // 4].astype(np.float32).astype(np.float64)
    th = np.arange(SEQ)[None, :] * f[:, None]
    ti, tj = np.empty((8, D, SEQ)), np.empty((8, D, SEQ))
    for h in range(8):
        for a in range(4):
            x = th[4 * h + a]
            ti[h, 2 * a], ti[h, 2 * a + 1] = np.cos(x), np.sin(x)
            tj[h, 2 * a], tj[h, 2 * a + 1] = np.cos(x) - np.sin(x), np.cos(x) + np.sin(x)

    def split(a):
        out, r = [], a.astype(np.float32)
        for _ in range(PARTS):
            out.append(r.astype(bf))
            r = r - out[-1].astype(np.float32)
        return out
    pi, pj = split(ti), split(tj)
    trig = np.zeros((2, ROWS, H, SEQ), bf)
    for n, (a, b) in enumerate(PAIRS):
        trig[0, D * n:D * n + D, 0:8] = pi[a].transpose(1, 0, 2)
        trig[1, D * n:D * n + D, 0:8] = pj[b].transpose(1, 0, 2)
    trig[0, 0:PARTS, 8:H] = 1.0
    return cf, cb, trig, np.ones((PARTS, H, SEQ), bf)


def kernel(**inputs):
    import numpy as np
    import concourse.bacc as bacc
    from concourse.bass_utils import run_bass_kernel_spmd

    g = {k: np.asarray(v) for k, v in inputs.items()}
    hd = np.arange(P).reshape(H, D).T.reshape(P)
    rot = hd.reshape(D, H)[(np.arange(D) + D // 2) % D].reshape(P)
    wqkv, aw = g["L1_attn_w_qkv"], g["L0_ffn_attn_w"]
    bqkv = g["L1_attn_b_qkv"]
    cf, cb, trig, ones = _constants()
    A, F_ = "L0_attn_", "L0_ffn_"
    ws = [g[A + "wq"].T[:, hd], g[A + "wk"].T[:, hd], g[A + "wv"].T, g[A + "wo"].T,
          aw[:, 0:C][:, hd], aw[:, C:2 * C][:, hd], aw[:, 2 * C:], g[F_ + "proj_w"],
          aw[:, 0:C][:, rot], aw[:, C:2 * C][:, rot],
          wqkv[0:C].T[:, hd], wqkv[C:2 * C].T[:, hd], wqkv[2 * C:].T, g["L1_attn_w_proj"].T]
    arrays = {
        "x": g["L0_attn_x"].reshape(NSEQ * SEQ, C), "cf": cf, "cb": cb, "trig": trig, "onesb": ones,
        "wt": np.stack(ws, axis=1),
        "cols": np.stack([g[A + "bq"][hd], g[A + "bk"][hd], g[F_ + "ln1_w"], g[F_ + "ln1_b"],
                          bqkv[0:C][hd], bqkv[C:2 * C][hd]], axis=1),
        "convw": g[F_ + "conv_w"].reshape(C, 3),
        "rows": np.stack([g[A + "bv"], g[A + "bo"], g[F_ + "ln2_w"], g[F_ + "ln2_b"], bqkv[2 * C:],
                          g["L1_attn_b_proj"]]),
        "wr": np.concatenate([g[F_ + "router_w"], g["L1_ffn_Wr"]], axis=1), "br": g["L1_ffn_br"],
        "up0": g[F_ + "expert_wv"], "dn0": g[F_ + "expert_proj"],
        "up1": g["L1_ffn_W1"], "dn1": g["L1_ffn_W2"], "b1": g["L1_ffn_b1"].reshape(E1 * F1),
        "b2": g["L1_ffn_b2"].reshape(E1 * C), "pos": g["L1_attn_pos_independent"].reshape(1, 8, 8),
    }
    nc = bacc.Bacc("TRN2", target_bir_lowering=False, num_devices=1)
    arrays = {f"in_{k}": np.ascontiguousarray(v) for k, v in arrays.items()}
    t = {k[3:]: nc.dram_tensor(k, v.shape, mybir.dt.from_np(v.dtype), kind="ExternalInput").ap() for k, v in arrays.items()}
    out = nc.dram_tensor("out", (NSEQ * SEQ, C), mybir.dt.float32, kind="ExternalOutput").ap()
    build(nc, t, out)
    r = run_bass_kernel_spmd(nc, [arrays], core_ids=[0])
    return r.results[0]["out"].reshape(NSEQ, SEQ, C)
```

```python
import concourse.bass as bass
from concourse import mybir
from contextlib import ExitStack

NSEQ, SEQ, C, P = 16, 256, 128, 128
H, D = 16, 8
NT = NSEQ * SEQ // P
TPS = SEQ // P
WS = 64
BAND = 3 * WS
PARTS = 3
PAIRS = [(0, 0), (0, 1), (0, 2), (1, 0), (1, 1), (2, 0)]
ROWS = len(PAIRS) * D
ROW_BIAS = ROWS
ROW_MAX = (ROWS, ROWS, 2 * ROWS)
HPS = 2
NSTEP = H // HPS
GROUPS = H // 4
PACK = 2
HALF = 32 // PACK
SW = 2 * SEQ + 2 * P
NBUF = 4
E0, F0 = 4, 512
E1, F1 = 8, 384
NTILE0 = NT + E0
NTILE1 = NT + E1
ROW = 2 * C + 1
OUTSIDE = 2 * NSEQ * SEQ
EPS = 1e-5
OFF_LOAD, OFF_PROJ, OFF_SPREAD, OFF_SCORE, OFF_MAX, OFF_ATT, OFF_OUT, OFF_ROUTE, OFF_LOGIT = 5, 4, 3, 2, 1, 0, -1, -2, -3
ATTN0, ATTN1, ATTN2 = range(3)

CF = {}
CB = {}


def _columns():
    at = 0
    for name, n in (("ident", P), ("cosq", SEQ), ("cosk", SEQ), ("sinq", SEQ), ("sink", SEQ), ("heads", H),
                    ("padfar", TPS), ("pad64", TPS), ("ones", P), ("eid", 8), ("start", 64), ("tokid", NT), ("row", 1)):
        CF[name] = (at, at + n)
        at += n
    CF["all"] = at
    at = 0
    for name, n in (("ident", P), ("band", 2 * BAND), ("causal_q", P), ("causal_k", P), ("before", P), ("ones", P)):
        CB[name] = (at, at + n)
        at += n
    CB["all"] = at


_columns()


class Unit:

    def __init__(self, rep, it):
        self.layer, self.rep, self.n = rep // NSEQ, rep, rep + NBUF * it
        self.s = self.n - NSEQ * self.layer
        self.b, self.it = rep % NBUF, it


class Slot:

    def __init__(self, rep, it, first, last):
        self.rep, self.it, self.first, self.last = rep, it, first, last

    def unit(self, off, layers=(0, 1, 2)):
        r = self.rep + off
        if not self.first <= r < self.last or r // NSEQ not in layers:
            return None
        return Unit(r, self.it)

    def before(self):
        return Slot(self.rep - 1, self.it, self.first, self.last)


def build(nc, t, out):
    f32, bf16, i32, u32 = mybir.dt.float32, mybir.dt.bfloat16, mybir.dt.int32, mybir.dt.uint32
    ALU, ACT, AX = mybir.AluOpType, mybir.ActivationFunctionType, mybir.AxisListType
    ctx = ExitStack()
    with ctx:
        def sb(name, shape, dt=f32):
            return ctx.enter_context(nc.sbuf_tensor(name, shape, dt))

        def pb(name, shape):
            return ctx.enter_context(nc.psum_tensor(name, shape, f32))

        def sem(name):
            return ctx.enter_context(nc.semaphore(name))

        def dram(name, shape):
            return nc.dram_tensor(name, shape, f32, kind="Internal").ap()

        x1_d = dram("x1_d", (NSEQ * SEQ, C))
        y_d = dram("y_d", (NSEQ * SEQ, C))
        xz_d = dram("xz_d", (NSEQ * SEQ, C))
        x2_d = dram("x2_d", (NSEQ * SEQ, C))
        x3_d = dram("x3_d", (NSEQ * SEQ, C))
        hs_d = [dram("hs0_d", (NTILE0 * P, ROW)), dram("hs1_d", (NTILE1 * P, ROW))]

        cf = sb("cf", [P, CF["all"]])
        cb = sb("cb", [P, CB["all"]], bf16)
        Fc = lambda name: cf[:, CF[name][0]:CF[name][1]]
        Bc = lambda name: cb[:, CB[name][0]:CB[name][1]]
        wt = sb("wt", [P, 12, C])
        WQ, WK, WV, WO = range(4)
        W = lambda layer, which: wt[:, 4 * layer + which, :]
        cols = sb("cols", [P, 9])
        BQ0, BK0, LN1W, LN1B, BQ2, BK2, BQ2S = range(7)
        convw = sb("convw", [P, 3])
        rows = sb("rows", [P, 6, C])
        BV0, BO0, LN2W, LN2B, BV2, BO2 = range(6)
        wr = sb("wr", [P, E0 + E1])
        br = sb("br", [P, E1])
        wm = sb("wm", [P, 2 * E1 * F1])
        up = [wm[:, 0:E0 * 2 * F0], wm[:, 0:E1 * F1]]
        dn = [wm[:, E0 * 2 * F0:E0 * 3 * F0], wm[:, E1 * F1:2 * E1 * F1]]
        posr = sb("posr", [1, 8, 8])
        posc = sb("posc", [1, 3, 8])
        poscp = sb("poscp", [1, PARTS, 8], bf16)

        xin = sb("xin", [P, NBUF, TPS, C])
        stat = sb("stat", [P, NBUF, TPS, 6])
        mv = sb("mv", [P, NBUF, TPS, 2])
        rstd = sb("rstd", [P, NBUF, TPS, 2])
        xn = sb("xn", [P, NBUF, TPS, C])
        stat2 = sb("stat2", [P, NBUF, TPS, 6])
        mv2 = sb("mv2", [P, NBUF, TPS, 2])
        rstd2 = sb("rstd2", [P, NBUF, TPS, 2])
        xn2 = sb("xn2", [P, 2, TPS, C])
        xT = sb("xT", [P, 2, SEQ])
        cT = sb("cT", [P, 2, SEQ])
        tap = sb("tap", [P, 2, SEQ])
        qkf = sb("qkf", [P, 2, SEQ])
        qks = sb("qks", [P, 2, SEQ])
        parts = sb("parts", [P, PARTS, 2, SEQ], bf16)
        arena = sb("arena", [P, 2 * NBUF * H * SEQ // 2])
        QK = [arena[:, i * H * SEQ // 2:(i + 1) * H * SEQ // 2].bitcast(bf16).rearrange("p (h t) -> p h t", h=H)
              for i in range(2 * NBUF)]
        QA, KA = QK[0:NBUF], QK[NBUF:]
        vv = sb("vv", [P, NBUF, TPS * H * 32 + HALF])
        nred = sb("nred", [P, 2, NSTEP, 6])
        nmax = sb("nmax", [P, 2, TPS, H])
        mres = sb("mres", [P, 2, TPS, H])
        mparts = sb("mparts", [P, TPS, P // H, H], bf16)
        mT = sb("mT", [PARTS * H, SEQ], bf16)
        spad = sb("spad", [P, NBUF, TPS, H])
        epad = sb("epad", [P, NBUF, TPS, H])
        earg = sb("earg", [P, 2, TPS, H])
        pr = sb("pr", [P, 4, SW])
        poscb = pr[0:1, :, :].rearrange("o a b -> o (a b)").bitcast(bf16).rearrange(
            "o (a h t) -> o a h t", a=PARTS, h=8)
        oT = sb("oT", [P, GROUPS // PACK, SEQ])
        rden = sb("rden", [P, 2, TPS * H])
        den = sb("den", [P, 2, TPS * H])
        on = sb("on", [P, 2, TPS * H, D])
        onT = sb("onT", [P, SEQ])
        xres = sb("xres", [P, 2, TPS, C])
        yres = sb("yres", [P, 2, TPS, C])
        zb = sb("zb", [P, 2, TPS, C])
        xzb = sb("xzb", [P, 2, TPS, C])
        stat3 = sb("stat3", [P, 2, TPS, 6])
        mv3 = sb("mv3", [P, 2, TPS, 2])
        rstd3 = sb("rstd3", [P, 2, TPS, 2])
        hn = sb("hn", [P, 2, TPS, C])
        pnum = sb("pnum", [P, TPS * H, D])
        hT = sb("hT", [P, SEQ])
        half = sb("half", [P, TPS])
        nil = sb("nil", [P, TPS])
        eps = sb("eps", [P, TPS])
        rstdv = sb("rstdv", [P, NBUF, TPS, 2])
        rstd2v = sb("rstd2v", [P, NBUF, TPS, 2])
        rstd3v = sb("rstd3v", [P, 2, TPS, 2])
        lg = [sb("lg0", [P, NT, E0]), sb("lg1", [P, NT, E1])]
        h2 = sb("h2", [P, NT, C])
        zrow = sb("zrow", [P, ROW])

        def piece(n):
            a = piece.at
            piece.at += n
            return arena[:, a:a + n]
        piece.at = 0
        hx = piece(NTILE1 * ROW).rearrange("p (t c) -> p t c", c=ROW)
        b1r, b2r = piece(E1 * F1), piece(E1 * C)
        spare = h2[:, :, :].rearrange("p t c -> p (t c)")
        def small(b, n):
            a = small.at
            small.at += b * n
            return spare[:, a:a + b * n].rearrange("p (b c) -> p b c", b=b)
        small.at = 0
        xf, xfT, yt = small(2, C), small(2, C), small(4, C)
        gate, mixact, actT = small(2, F0), small(2, F0), small(2, F0)
        top = sb("top", [P, NT])
        eq = sb("eq", [P, NT, E1])
        eqi = sb("eqi", [P, NT, E1])
        pick = sb("pick", [P, NT])
        oh = sb("oh", [P, NT, E1], bf16)
        cnt = sb("cnt", [P, E1], bf16)
        padi = sb("padi", [P, E1], i32)
        padi2 = sb("padi2", [P, E1], i32)
        padf = sb("padf", [P, E1])
        base = sb("base", [P, E1 + 1])
        rk = sb("rk", [P, NT, E1])
        rk2 = sb("rk2", [P, NT, E1])
        destf = sb("destf", [P, NT])
        dest = [sb("dest0", [P, NT], u32), sb("dest1", [P, NT], u32)]
        ge = sb("ge", [1, NTILE1, E1])
        tef = sb("tef", [1, NTILE1])
        idf = sb("idf", [P, NTILE1])
        ids = [sb("ids0", [P, NTILE0], u32), sb("ids1", [P, NTILE1], u32)]
        tei = [sb("te0", [1, NTILE0], i32), sb("te1", [1, NTILE1], i32)]

        psS = pb("psS", [P, 1024])
        psT = [pb("psT0", [P, 1024]), pb("psT1", [P, 1024])]
        psO = pb("psO", [P, 512])
        psM = pb("psM", [P, 512])

        S = {n: sem("s_" + n) for n in (
            "const half pos wload dn1load zero setup posb posd trig krow "
            "stats mvs veps rstds shifts lnout lnout2 stats2 mvs2 veps2 rstds2 shifts2 "
            "xt xtev tap0 tap1 tap2 tap3 conv qk qkev rotev ropeadd sp spev "
            "hi resid mid lo v vev sready red nmax mhi mres mmid mlo mt mtev "
            "tready exp earg epad epad64 pv oev ott den rden norm pnum ob obev op rbias zout "
            "xz stats3 mvs3 veps3 rstds3 hout hw hfin hT hTev lg lgev ").split()}
        M = {n: [sem(f"m{i}_{n}") for i in range(2)] for n in (
            "dve rank dest scat ht htev up act prod at atev yev "
            "xres hcopy ids idf te bias actg ready xf".split())}
        MD = {n: [[sem(f"m{i}{j}_{n}") for j in range(k)] for i in range(2)] for n, k in
              (("load", 2), ("store", 4))}

        def at(per, u, c, first=0):
            return per * (u.n - first) + c

        def wait(eng, name, value):
            if isinstance(value, int) and value <= 0:
                return
            eng.wait_ge(S[name], value)

        D_ = {n: [sem(f"d{i}_{n}") for i in range(2)] for n in
              "xin resdma yresdma xstore hstore ystore rep mrow".split()}
        NREP = 2 * len(PAIRS)

        def moved(eng, name, u, back=0, first=0, n=1):
            r = u.rep - back
            if r >= first:
                eng.wait_ge(D_[name][r % 2], 16 * n * ((r - first) // 2 + 1 + NBUF // 2 * u.it))

        TEN_M = [("v", OFF_SPREAD, (0, 1, 2), "vev", 1, 0), ("lg", OFF_LOGIT, (1, 2), "lgev", 1, NSEQ),
                 ("qk", OFF_PROJ, (0, 1, 2), "qkev", 2, 0), ("sp", OFF_PROJ, (0,), "spev", 1, 0),
                 ("rot", OFF_PROJ, (1,), "rotev", 1, NSEQ), ("mt", OFF_MAX, (0, 1, 2), "mtev", 1, 0),
                 ("hT", OFF_ROUTE, (1, 2), "hTev", 1, NSEQ), ("xt", OFF_LOAD, (0, 1, 2), "xtev", 1, 0)]
        TEN_O = [("pvB", OFF_OUT, (0, 1, 2), "oev", 2, 2), ("ott", OFF_OUT, (0, 1, 2), "norm", 1, 1),
                 ("pvA", OFF_ATT, (0, 1, 2), "oev", 2, 1), ("ob", OFF_OUT, (0, 1, 2), "obev", 1, 1),
                 ("op", OFF_OUT, (0, 1, 2), "zout", 1, 1), ("pvB0", OFF_ATT, (0, 1, 2), "oev", 2, 2)]

        def wait_bank(eng, table, slot, name):
            i = [x[0] for x in table].index(name)
            sl = slot
            for _ in range(3 * len(table)):
                i -= 1
                if i < 0:
                    i, sl = len(table) - 1, sl.before()
                _, off, layers, done, per, c = table[i]
                u = sl.unit(off, layers)
                if u:
                    if table is TEN_M:
                        wait(eng, done, at(per, u, per, c))
                    else:
                        wait(eng, done, at(per, u, c))
                    return

        def slots(eng, step, first, last):
            k = first - OFF_LOAD
            while k < last - OFF_LOGIT:
                inner = k % NSEQ
                if k >= first and inner == 3:
                    with eng.Fori(0, (NSEQ - 4 - 4) // NBUF) as i:
                        for j in range(NBUF):
                            step(Slot(k + j, i, first, last))
                    k += NSEQ - 4 - 4
                else:
                    step(Slot(k, 0, first, last))
                    k += 1

        def tok(d, s, n=TPS):
            return d.rearrange("(s t p) c -> s p t c", t=TPS, p=P)[bass.ds(s, 1), :, :, :].rearrange(
                "s p t c -> p (s t) c")

        wm_parts = [
            (cf[:, :], t["cf"]), (cb[:, :], t["cb"]),
            (wt[:, :, :], t["wt"]), (cols[:, 0:6], t["cols"]), (convw[:, :], t["convw"]),
            (rows[:, :, :], t["rows"].partition_broadcast(P)),
            (wr[:, :], t["wr"]), (br[:, :], t["br"].partition_broadcast(P)),
        ]
        late_parts = [
            (up[0].rearrange("p (e n) -> p e n", e=E0), t["up0"].rearrange("e p n -> p e n")),
            (dn[0].rearrange("p (e k n) -> p e k n", e=E0, n=C), t["dn0"].rearrange("e (k p) n -> p e k n", p=P)),
            (posr[:, :, :], t["pos"]),
        ]
        for n, d in zip((NTILE0, NTILE1), hs_d):
            z = d.rearrange("(t p) c -> p t c", p=P)
            for a in range(0, n, n // 4):
                late_parts.append((z[:, a:a + n // 4, :], zrow[:, :].unsqueeze(1).to_broadcast([P, n // 4, ROW])))
        LATER = dict(zip((0, 1, 2, *range(NSEQ - 5, NSEQ + 3)), late_parts))
        NCONST, NLATE = 16 * len(wm_parts), 16 * len(late_parts)
        mix1_parts = [
            (up[1].rearrange("p (e n) -> p e n", e=E1), t["up1"].rearrange("e p n -> p e n")),
            (dn[1].rearrange("p (e k n) -> p e k n", e=E1, n=C), t["dn1"].rearrange("e (k p) n -> p e k n", p=P)),
        ]
        bias_parts = [(b1r, t["b1"].partition_broadcast(P)), (b2r, t["b2"].partition_broadcast(P))]

        block = ctx.enter_context(nc.Block())

        @block.sync
        def _(sp):
            for dst, src in wm_parts:
                sp.dma_start(dst, src).then_inc(S["const"], 16)

            def step(sl):
                ul, up, um = sl.unit(OFF_LOAD), sl.unit(OFF_SPREAD), sl.unit(OFF_MAX)
                uo, ur = sl.unit(OFF_OUT), sl.unit(OFF_ROUTE)
                if ul:
                    wait(sp, "lnout", at(2, ul, -2))
                    if ul.layer == 1:
                        moved(sp, "xstore", ul, NSEQ)
                    src = (t["x"], x1_d, x2_d)[ul.layer]
                    sp.dma_start(xin[:, ul.b, :, :], tok(src, ul.s)).then_inc(D_["xin"][ul.b % 2], 16)
                if up:
                    wait(sp, "hi", at(1, up, 1))
                    wait(sp, "tready", at(NSTEP, up, NSTEP - NSTEP * NBUF))
                    for n, made in enumerate((None, "mid", "lo")):
                        if made:
                            wait(sp, made, at(1, up, 1))
                        for w, buf in enumerate((QA, KA)):
                            for j, pair in enumerate(PAIRS):
                                if pair[w] == n:
                                    sp.dma_start(buf[up.b][D * j:D * j + D, :, :],
                                                 parts[:, n, w, :]).then_inc(D_["rep"][up.b % 2], 16)
                if uo:
                    if uo.rep >= NSEQ + 2 and uo.layer == 1:
                        wait(sp, "xz", at(1, uo, -1, NSEQ))
                    else:
                        wait(sp, "zout", at(1, uo, -1))
                    src = (t["x"], x1_d, x2_d)[uo.layer]
                    sp.dma_start(xres[:, uo.b % 2, :, :], tok(src, uo.s)).then_inc(D_["resdma"][uo.b % 2], 16)
                    if uo.layer == 1:
                        moved(sp, "ystore", uo, 0, NSEQ)
                        sp.dma_start(yres[:, uo.b % 2, :, :], tok(y_d, uo.s)).then_inc(D_["yresdma"][uo.b % 2], 16)
                if ur:
                    if ur.layer == 1:
                        wait(sp, "xz", at(1, ur, 1, NSEQ))
                        sp.dma_start(tok(xz_d, ur.s), xzb[:, ur.b % 2, :, :]).then_inc(D_["xstore"][ur.b % 2], 16)
                    else:
                        wait(sp, "zout", at(1, ur, 1))
                        sp.dma_start(tok((x1_d, None, x3_d)[ur.layer], ur.s),
                                     zb[:, ur.b % 2, :, :]).then_inc(D_["xstore"][ur.b % 2], 16)
                if ur and ur.layer >= 1:
                    wait(sp, "hfin", at(1, ur, 1, NSEQ))
                    sp.dma_start(h2[:, bass.ds(ur.s * TPS, TPS), :], hn[:, ur.b % 2, :, :]).then_inc(D_["hstore"][ur.b % 2], 16)
                if um:
                    wait(sp, "mtev", at(1, um, 1))
                    sp.dma_start(QA[um.b][ROW_MAX[um.layer]:ROW_MAX[um.layer] + PARTS, :, :], mT[:, :]).then_inc(D_["mrow"][um.b % 2], 16)
                if ul and ul.layer == 1:
                    wait(sp, "lnout", at(2, ul, 2))
                    sp.dma_start(tok(y_d, ul.s), xn[:, ul.b, :, :]).then_inc(D_["ystore"][ul.b % 2], 16)

            def mix(i):
                ntl = (NTILE0, NTILE1)[i]
                sp.wait_ge(S["tready"], NSTEP * NSEQ * (2, 3)[i])
                if i == 1:
                    for dst, src in bias_parts:
                        sp.dma_start(dst, src).then_inc(M["bias"][i], 16)
                for q in range(2):
                    sp.wait_ge(D_["xstore"][q], 8 * NSEQ * (2, 3)[i])
                sp.dma_start(hx[:, 0:NT, C:2 * C], (xz_d, x3_d)[i].rearrange("(t p) c -> p t c", p=P)).then_inc(
                    M["xres"][i], 16)
                sp.wait_ge(M["scat"][i], 16 * NT)
                rows_of = hs_d[i].rearrange("(t p) c -> p t c", p=P)
                for q, (a, b) in enumerate(((0, 4), (4, ntl))):
                    sp.dma_start(hx[:, a:b, :], rows_of[:, a:b, :]).then_inc(MD["load"][i][q], 16)
                for q in range(4):
                    sp.wait_ge(MD["store"][i][q], 16 * (ntl // 4))

            for i in range(NBUF):
                sp.dma_start(KA[i][ROW_MAX[0]:ROW_MAX[0] + PARTS, :, :], t["onesb"]).then_inc(S["krow"], 16)
            slots(sp, step, 0, 2 * NSEQ)
            mix(0)
            for i in range(NBUF):
                sp.dma_start(QA[i][ROW_BIAS:ROW_MAX[2], :, :], t["trig"][0]).then_inc(S["trig"], 16)
                sp.dma_start(KA[i][ROW_BIAS:ROW_MAX[2], :, :], t["trig"][1]).then_inc(S["trig"], 16)
                sp.dma_start(KA[i][ROW_MAX[2]:ROW_MAX[2] + PARTS, :, :], t["onesb"]).then_inc(S["krow"], 16)
            sp.wait_ge(S["trig"], 16 * 2 * NBUF)
            sp.wait_ge(S["posb"], 1)
            for i in range(NBUF):
                sp.dma_start(KA[i][ROW_BIAS:ROW_BIAS + PARTS, 8:H, :], poscb).then_inc(S["posd"], 16)
            sp.wait_ge(S["posd"], 16 * NBUF)
            for dst, src in mix1_parts:
                sp.dma_start(dst, src).then_inc(S["dn1load"], 16)
            slots(sp, step, 2 * NSEQ, 3 * NSEQ)
            mix(1)
            for name, n in (("xstore", 3), ("hstore", 2), ("ystore", 1)):
                for q in range(2):
                    sp.wait_ge(D_[name][q], 8 * n * NSEQ)

        @block.tensor
        def _(pe):
            mm = pe.matmul

            def score(sl, g):
                u = sl.unit(OFF_SCORE)
                if not u:
                    return
                if g == 0:
                    if u.layer == 2:
                        pe.wait_ge(S["posd"], 16 * NBUF)
                    moved(pe, "rep", u, n=NREP)
                q, k = QA[u.b], KA[u.b]
                n = ROW_MAX[u.layer]
                for qt in (1, 0):
                    wait(pe, "red", at(2 * NSTEP, u, 2 * g - qt))
                    o = psS[:, 512 * (1 - qt):512 * (2 - qt)]
                    keys = (64 * qt, BAND) if u.layer == 0 else (0, P * (qt + 1))
                    for hh in range(HPS):
                        h = HPS * g + hh
                        mm(o[:, hh * keys[1]:(hh + 1) * keys[1]], q[0:n, h, P * qt:P * qt + P],
                           k[0:n, h, keys[0]:keys[0] + keys[1]], start=(hh == 0), stop=False, skip_group_check=True)
                    o2 = o[:, 0:HPS * keys[1]].rearrange("p (h k) -> p h k", h=HPS)
                    if u.layer == 0:
                        mask = Bc("band")[:, BAND * qt:BAND * qt + BAND]
                    else:
                        mask = Bc("causal_q")
                        o2 = o2[:, :, P * qt:P * qt + P]
                    w = mask.shape[-1]
                    mm(o2, Bc("ident"), mask.unsqueeze(1).to_broadcast([P, HPS, w]), start=False, stop=True,
                       skip_group_check=True).then_inc(S["sready"], 1)

            def scoreT(sl, g):
                u = sl.unit(OFF_ATT)
                if not u:
                    return
                if g == 0:
                    pe.wait_ge(S["krow"], 16 * NBUF * (1 + (u.layer == 2)))
                    moved(pe, "mrow", u)
                wait(pe, "exp", at(NSTEP, u, g - 1))
                n = ROW_MAX[u.layer] + PARTS
                q, k = QA[u.b][0:n], KA[u.b][0:n]
                for kt in range(2):
                    o = psT[g % 2][:, 512 * kt:512 * kt + 512]
                    q0, qn = (64 * kt, BAND) if u.layer == 0 else (P * kt, SEQ - P * kt)
                    for hh in range(HPS):
                        h = HPS * g + hh
                        mm(o[:, hh * qn:hh * qn + qn], k[:, h, P * kt:P * kt + P], q[:, h, q0:q0 + qn],
                           start=(hh == 0), stop=False, skip_group_check=True)
                    o2 = o[:, 0:HPS * qn].rearrange("p (h k) -> p h k", h=HPS)
                    if u.layer == 0:
                        mask = Bc("band")[:, BAND * kt:BAND * kt + BAND]
                    else:
                        mask = Bc("causal_k")
                        o2 = o2[:, :, 0:P]
                    w = mask.shape[-1]
                    last = mm(o2, Bc("ident"), mask.unsqueeze(1).to_broadcast([P, HPS, w]), start=False, stop=True,
                              skip_group_check=True)
                last.then_inc(S["tready"], 1)

            def pv(sl, gg):
                u = sl.unit(OFF_OUT if gg == 3 else OFF_ATT)
                if not u:
                    return
                if gg % 2 == 0:
                    wait_bank(pe, TEN_O, sl, "pvB0" if gg else "pvA")
                wait(pe, "exp", at(NSTEP, u, 2 * gg + 2))
                if gg == 0:
                    wait(pe, "vev", at(1, u, 1))
                for kt in range(2):
                    q0, qn = (64 * kt, BAND) if u.layer == 0 else (P * kt, SEQ - P * kt)
                    off = 0 if kt == 0 else HPS * (BAND if u.layer == 0 else SEQ)
                    for j in range(4):
                        h = 4 * gg + j
                        a = off + (h % 2) * qn
                        v = 32 * (kt * H + h) + HALF * (1 - gg % PACK)
                        last = mm(psO[32 * j:32 * j + 32, q0:q0 + qn], vv[:, u.b, v:v + 32],
                                  pr[:, (h // 2) % 4, a:a + qn], start=(kt == 0 and gg % PACK == 0),
                                  stop=(kt == 1 and gg % PACK == 1), skip_group_check=True)
                last.then_inc(S["pv"], 1)

            def ott(sl):
                u = sl.unit(OFF_OUT)
                if not u:
                    return
                wait_bank(pe, TEN_O, sl, "ott")
                wait(pe, "oev", at(2, u, 2))
                for qt in range(TPS):
                    for y in range(2):
                        a = (2 * qt + y) * P
                        last = pe.transpose(psO[:, a:a + P], oT[:, y, P * qt:P * qt + P], Fc("ident"))
                last.then_inc(S["ott"], 1)

            def ob(sl):
                u = sl.unit(OFF_OUT)
                if not u:
                    return
                wait_bank(pe, TEN_O, sl, "ob")
                wait(pe, "norm", at(1, u, 1))
                for qt in range(TPS):
                    last = pe.transpose(psO[:, P * qt:P * qt + P],
                                        on[:, u.b % 2, H * qt:H * qt + H, :].rearrange("p h d -> p (h d)"), Fc("ident"))
                last.then_inc(S["ob"], 1)

            def outproj(sl):
                u = sl.unit(OFF_OUT)
                if not u:
                    return
                wait(pe, "obev", at(1, u, 1))
                wait_bank(pe, TEN_O, sl, "op")
                for qt in range(TPS):
                    last = mm(psO[:, P * qt:P * qt + P], onT[:, P * qt:P * qt + P], W(u.layer, WO),
                              start=True, stop=True)
                last.then_inc(S["op"], 1)

            def xt(sl):
                u = sl.unit(OFF_LOAD)
                if not u:
                    return
                wait_bank(pe, TEN_M, sl, "xt")
                if u.layer == 1:
                    wait(pe, "lnout2", at(2, u, 2, NSEQ))
                else:
                    wait(pe, "lnout", at(2, u, 2))
                for i in range(TPS):
                    src = xn2[:, u.b % 2, i, :] if u.layer == 1 else xn[:, u.b, i, :]
                    last = pe.transpose(psM[:, P * i:P * i + P], src, Fc("ident"))
                last.then_inc(S["xt"], 1)

            def x_of(u):
                return cT[:, u.b % 2, :] if u.layer == 1 else xT[:, u.b % 2, :]

            def project(sl, name):
                u = sl.unit(OFF_SPREAD if name == "v" else OFF_PROJ)
                if not u:
                    return
                if name == "qk":
                    if u.layer == 1:
                        wait(pe, "conv", at(1, u, 1, NSEQ))
                    else:
                        wait(pe, "xtev", at(1, u, 1))
                wait_bank(pe, TEN_M, sl, name)
                x = x_of(u)
                if name == "v":
                    for i in range(TPS):
                        last = mm(psM[:, P * i:P * i + P], x[:, P * i:P * i + P], W(u.layer, WV), start=True, stop=True)
                else:
                    for i, w in enumerate((WQ, WK)):
                        last = mm(psM[:, SEQ * i:SEQ * i + SEQ], W(u.layer, w), x, start=True, stop=True)
                last.then_inc(S[name], 1)

            def sumq(sl):
                u = sl.unit(OFF_PROJ, (0,))
                if not u:
                    return
                wait_bank(pe, TEN_M, sl, "sp")
                wait(pe, "qkev", at(2, u, 2))
                for i in range(TPS):
                    last = mm(psM[:, H * i:H * i + H], qkf[:, 0, P * i:P * i + P], Fc("heads"), start=True, stop=True)
                last.then_inc(S["sp"], 1)

            def mt(sl):
                u = sl.unit(OFF_MAX)
                if not u:
                    return
                wait_bank(pe, TEN_M, sl, "mt")
                wait(pe, "mlo", at(1, u, 1))
                for i in range(TPS):
                    last = pe.transpose(psM[:, :].bitcast(bf16)[:, P * i:P * i + P],
                                        mparts[:, i, :, :].rearrange("p a h -> p (a h)"), Bc("ident"))
                last.then_inc(S["mt"], 1)

            def route(sl, name):
                u = sl.unit(OFF_ROUTE if name == "hT" else OFF_LOGIT, (1, 2))
                if not u:
                    return
                wait_bank(pe, TEN_M, sl, name)
                if name == "hT":
                    wait(pe, "hfin", at(1, u, 1, NSEQ))
                    for i in range(TPS):
                        last = pe.transpose(psM[:, P * i:P * i + P], hn[:, u.b % 2, i, :], Fc("ident"))
                    last.then_inc(S["hT"], 1)
                else:
                    wait(pe, "hTev", at(1, u, 1, NSEQ))
                    w = wr[:, 0:E0] if u.layer == 1 else wr[:, E0:E0 + E1]
                    n = w.shape[-1]
                    for i in range(TPS):
                        last = mm(psM[:, n * i:n * i + n], hT[:, P * i:P * i + P], w, start=True, stop=True)
                    last.then_inc(S["lg"], 1)

            def step(sl):
                score(sl, 0)
                scoreT(sl, 0)
                pv(sl, 3)
                project(sl, "v")
                score(sl, 1)
                scoreT(sl, 1)
                ott(sl)
                route(sl, "lg")
                score(sl, 2)
                scoreT(sl, 2)
                pv(sl, 0)
                project(sl, "qk")
                score(sl, 3)
                scoreT(sl, 3)
                sumq(sl)
                score(sl, 4)
                scoreT(sl, 4)
                pv(sl, 1)
                score(sl, 5)
                scoreT(sl, 5)
                ob(sl)
                mt(sl)
                score(sl, 6)
                scoreT(sl, 6)
                outproj(sl)
                route(sl, "hT")
                score(sl, 7)
                scoreT(sl, 7)
                pv(sl, 2)
                xt(sl)

            def mix(i):
                ntl, E, F = ((NTILE0, E0, F0), (NTILE1, E1, F1))[i]
                m = {k: v[i] for k, v in M.items()}
                pe.wait_ge(m["dve"], 6)
                mm(psT[1][:, 0:E], Bc("ones"), cnt[:, 0:E], start=True, stop=True)
                rank = psT[0][:, 0:NT * E].rearrange("p (t e) -> p t e", e=E)
                mm(rank, Bc("before"), oh[:, :, 0:E], start=True, stop=False, skip_group_check=True)
                for tt in range(NT - 1):
                    last = mm(rank[:, tt + 1:NT, :], Bc("ones"),
                              oh[:, tt:tt + 1, 0:E].to_broadcast([P, NT - 1 - tt, E]),
                              start=False, stop=(tt == NT - 2), skip_group_check=True)
                last.then_inc(m["rank"], 1)
                pe.wait_ge(m["te"], 1)
                if i == 0:
                    pe.wait_ge(S["wload"], NLATE)
                else:
                    pe.wait_ge(S["dn1load"], 32)
                nk = F // P

                def turn(j, it):
                    jx = j + 4 * it
                    if j >= 1:
                        pe.wait_ge(m["htev"], jx)
                    pe.wait_ge(m["xf"], jx + 1)
                    pe.transpose(psM[:, 0:P], xf[:, j % 2, :], Fc("ident")).then_inc(m["ht"], 1)

                def upward(j, it):
                    jx = j + 4 * it
                    e = pe.value_load(tei[i][0:1, bass.ds(jx, 1)], min_val=0, max_val=E - 1)
                    pe.wait_ge(m["htev"], jx + 1)
                    if j >= 2:
                        pe.wait_ge(m["act"], jx - 1)
                    for n in range(2 if i == 0 else 1):
                        w = F0 if i == 0 else F1
                        last = mm(psT[j % 2][:, 512 * n:512 * n + w], xfT[:, j % 2, :],
                                  up[i][:, bass.ds(e * (2 * F0 if i == 0 else F1) + n * F0, w)], start=True, stop=True)
                    last.then_inc(m["up"], 1)

                def turn_act(j, it):
                    jx = j + 4 * it
                    pe.wait_ge(m["act"], jx + 1)
                    if j >= 2:
                        pe.wait_ge(m["atev"], jx - 1)
                    for n in range(nk):
                        last = pe.transpose(psS[:, 512 * (j % 2) + P * n:512 * (j % 2) + P * n + P],
                                            mixact[:, j % 2, P * n:P * n + P], Fc("ident"))
                    last.then_inc(m["at"], 1)

                def downward(j, it):
                    jx = j + 4 * it
                    e = pe.value_load(tei[i][0:1, bass.ds(jx, 1)], min_val=0, max_val=E - 1)
                    pe.wait_ge(m["atev"], jx + 1)
                    if j >= 1:
                        pe.wait_ge(m["yev"], jx)
                    for n in range(nk):
                        last = mm(psO[:, 0:C], actT[:, j % 2, P * n:P * n + P],
                                  dn[i][:, bass.ds(e * F + n * C, C)], start=(n == 0), stop=(n == nk - 1))
                    last.then_inc(m["prod"], 1)

                def tile(j, it):
                    if j + 1 < ntl:
                        turn(j + 1, it)
                    if j < ntl:
                        upward(j, it)
                    if 1 <= j <= ntl:
                        turn_act(j - 1, it)
                    if j >= 2:
                        downward(j - 2, it)

                turn(0, 0)
                for j in range(4):
                    tile(j, 0)
                with pe.Fori(0, (ntl - 8) // 4) as it:
                    for j in range(4):
                        tile(4 + j, it)
                for j in range(ntl - 4, ntl + 2):
                    tile(j, 0)

            pe.wait_ge(S["const"], NCONST)
            slots(pe, step, 0, 2 * NSEQ)
            mix(0)
            slots(pe, step, 2 * NSEQ, 3 * NSEQ)
            mix(1)

        @block.scalar
        def _(act_e):
            act = act_e
            actv = act.activation

            def exps(sl, g):
                u = sl.unit(OFF_ATT)
                if not u:
                    return
                wait(act, "tready", at(NSTEP, u, g + 1))
                wait(act, "pv", at(GROUPS, u, g // 2 - 1))
                src, dst = psT[g % 2][:, 0:SW], pr[:, g % 4, :]
                if u.layer == 0:
                    src = psT[g % 2][:, :].rearrange("p (b n) -> p b n", b=2)[:, :, 0:HPS * BAND]
                    dst = dst.rearrange("p (b n) -> p b n", b=2)
                actv(dst, src, ACT.Exp).then_inc(S["exp"], 1)

            def oev(sl, y):
                u = sl.unit((OFF_ATT, OFF_OUT)[y])
                if not u:
                    return
                wait(act, "pv", at(GROUPS, u, 2 * y + 2))
                wait(act, "ott", at(1, u, 0))
                actv(oT[:, y, :], psO[:, 0:SEQ], ACT.Copy).then_inc(S["oev"], 1)

            def xtev(sl):
                u = sl.unit(OFF_PROJ)
                if not u:
                    return
                wait(act, "xt", at(1, u, 1))
                wait(act, "v", at(1, u, -1))
                if u.layer == 1:
                    actv(xT[:, u.b % 2, :], psM[:, 0:SEQ], ACT.Identity, bias=cols[:, LN1B:LN1B + 1],
                         scale=cols[:, LN1W:LN1W + 1]).then_inc(S["xtev"], 1)
                else:
                    actv(xT[:, u.b % 2, :], psM[:, 0:SEQ], ACT.Copy).then_inc(S["xtev"], 1)

            def qkev(sl):
                u = sl.unit(OFF_PROJ, (0, 2))
                if not u:
                    return
                wait(act, "qk", at(1, u, 1))
                wait(act, "lo", at(1, u, 0))
                if u.layer == 0:
                    wait(act, "sp", at(1, u, 0))
                bq, bk = (BQ0, BK0) if u.layer == 0 else (BQ2S, BK2)
                actv(qkf[:, 0, :], psM[:, 0:SEQ], ACT.Identity, bias=cols[:, bq:bq + 1],
                     scale=1.0 if u.layer == 0 else float(D) ** -0.5).then_inc(S["qkev"], 1)
                actv(qkf[:, 1, :], psM[:, SEQ:2 * SEQ], ACT.Identity, bias=cols[:, bk:bk + 1],
                     scale=1.0).then_inc(S["qkev"], 1)

            def part(sl, n):
                u = sl.unit(OFF_PROJ)
                if not u:
                    return
                if n == 0:
                    if u.layer == 1:
                        wait(act, "ropeadd", at(1, u, 1, NSEQ))
                    else:
                        wait(act, "qkev", at(2, u, 2))
                    moved(act, "rep", u, 1, n=NREP)
                else:
                    wait(act, "resid", at(1, u, 1))
                actv(parts[:, n], qkf[:, :, :], ACT.Copy).then_inc(S[("hi", "mid")[n]], 1)

            def mtev(sl):
                u = sl.unit(OFF_MAX)
                if not u:
                    return
                wait(act, "mt", at(1, u, 1))
                moved(act, "mrow", u, 1)
                actv(mT[:, :], psM[:, :].bitcast(bf16)[0:PARTS * H, 0:SEQ], ACT.Copy).then_inc(S["mtev"], 1)

            def normal(o, x, m, r, done):
                for i in range(TPS):
                    actv(o[:, i, :], x[:, i, :], ACT.Identity, bias=m[:, i, 1:2], scale=r[:, i, 0:1]).then_inc(S[done], 1)

            def ln_apply(sl):
                u = sl.unit(OFF_LOAD)
                if not u:
                    return
                wait(act, "shifts", at(1, u, 1))
                if u.layer == 1 and u.rep >= NSEQ + NBUF:
                    moved(act, "ystore", u, 2, NSEQ)
                else:
                    wait(act, "xt", at(1, u, 1 - NBUF))
                normal(xn[:, u.b], xin[:, u.b], rstd[:, u.b], rstd[:, u.b], "lnout")

            def ln_again(sl):
                u = sl.unit(OFF_LOAD, (1,))
                if not u:
                    return
                wait(act, "shifts2", at(1, u, 1, NSEQ))
                wait(act, "xt", at(1, u, -1))
                normal(xn2[:, u.b % 2], xn[:, u.b], rstd2[:, u.b], rstd2[:, u.b], "lnout2")

            def epads(sl):
                u = sl.unit(OFF_MAX, (0,))
                if not u:
                    return
                wait(act, "earg", at(1, u, 1))
                wait(act, "pnum", at(1, u, 1 - NBUF))
                actv(epad[:, u.b, :, :].rearrange("p q (g j s) -> p (q g) s j", s=PACK, j=4),
                     earg[:, u.b % 2, :, :].rearrange("p q (g s j) -> p (q g) s j", s=PACK, j=4), ACT.Exp).then_inc(S["epad"], 1)

            def obev(sl):
                u = sl.unit(OFF_OUT)
                if not u:
                    return
                wait(act, "ob", at(1, u, 1))
                wait(act, "op", at(1, u, 0))
                actv(onT[:, :], psO[:, 0:SEQ], ACT.Copy).then_inc(S["obev"], 1)

            def hTev(sl):
                u = sl.unit(OFF_ROUTE, (1, 2))
                if not u:
                    return
                wait(act, "hT", at(1, u, 1, NSEQ))
                wait(act, "lg", at(1, u, 0, NSEQ))
                actv(hT[:, :], psM[:, 0:SEQ], ACT.Copy).then_inc(S["hTev"], 1)

            def step(sl):
                if sl.rep in LATER:
                    act.wait_ge(S["zero"], 1)
                    act.dma_start(*LATER[sl.rep]).then_inc(S["wload"], 16)
                xtev(sl)
                exps(sl, 0)
                oev(sl, 1)
                exps(sl, 1)
                epads(sl)
                exps(sl, 2)
                qkev(sl)
                exps(sl, 3)
                ln_apply(sl)
                exps(sl, 4)
                oev(sl, 0)
                exps(sl, 5)
                obev(sl)
                mtev(sl)
                part(sl, 0)
                exps(sl, 6)
                ln_again(sl)
                hTev(sl)
                exps(sl, 7)
                part(sl, 1)

            def mix(i):
                ntl, F = ((NTILE0, F0), (NTILE1, F1))[i]
                m = {k: v[i] for k, v in M.items()}

                def rows_turned(j, it):
                    jx = j + 4 * it
                    act.wait_ge(m["ht"], jx + 1)
                    if j >= 2:
                        act.wait_ge(m["up"], jx - 1)
                    actv(xfT[:, j % 2, :], psM[:, 0:P], ACT.Copy).then_inc(m["htev"], 1)

                def nonlin(j, it):
                    jx = j + 4 * it
                    if i == 0:
                        act.wait_ge(m["up"], jx + 1)
                        if j >= 2:
                            act.wait_ge(m["act"], jx - 1)
                        actv(gate[:, j % 2, 0:F], psT[j % 2][:, 0:F], ACT.Silu).then_inc(m["actg"], 1)
                    else:
                        act.wait_ge(m["actg"], jx + 1)
                        if j >= 2:
                            act.wait_ge(m["at"], jx - 1)
                        actv(mixact[:, j % 2, 0:F], gate[:, j % 2, 0:F], ACT.Gelu).then_inc(m["act"], 1)

                def fetch(j, it):
                    jx = j + 4 * it
                    if j >= 2:
                        act.wait_ge(m["ht"], jx - 1)
                    actv(xf[:, j % 2, :], hx[:, bass.ds(jx, 1), 0:C].rearrange("p t c -> p (t c)"),
                         ACT.Copy).then_inc(m["xf"], 1)

                def tile(j, it):
                    if j + 2 < ntl:
                        fetch(j + 2, it)
                    if j + 1 < ntl:
                        rows_turned(j + 1, it)
                    nonlin(j, it)

                act.wait_ge(S["tready"], NSTEP * NSEQ * (2, 3)[i])
                for q in range(2):
                    act.wait_ge(D_["hstore"][q], 8 * NSEQ * (i + 1))
                for q in range(4):
                    t8 = slice(NT // 4 * q, NT // 4 * (q + 1))
                    actv(hx[:, t8, 0:C], h2[:, t8, :], ACT.Copy).then_inc(m["hcopy"], 1)
                act.wait_ge(m["hcopy"], 5)
                act.wait_ge(MD["load"][i][0], 16)
                fetch(0, 0)
                fetch(1, 0)
                rows_turned(0, 0)
                tile(0, 0)
                tile(1, 0)
                act.wait_ge(MD["load"][i][1], 16)
                tile(2, 0)
                tile(3, 0)
                with act.Fori(0, (ntl - 8) // 4) as it:
                    for j in range(4):
                        tile(4 + j, it)
                for j in range(ntl - 4, ntl):
                    tile(j, 0)

            act.wait_ge(S["const"], NCONST)
            act.wait_ge(S["setup"], 3)
            slots(act, step, 0, 2 * NSEQ)
            mix(0)
            slots(act, step, 2 * NSEQ, 3 * NSEQ)
            mix(1)

        @block.vector
        def _(dve):
            tt, ts = dve.tensor_tensor, dve.tensor_scalar

            def reduce(sl, g):
                u = sl.unit(OFF_SCORE)
                if not u:
                    return
                if g == 0:
                    wait(dve, "nmax", at(2, u, -2))
                for qt in (1, 0):
                    wait(dve, "sready", at(2 * NSTEP, u, 2 * g + 2 - qt))
                    if u.layer == 0:
                        src, a, n = psS[:, 512 * (1 - qt):512 * (1 - qt) + HPS * BAND].rearrange(
                            "p (h n) -> p h n", h=HPS), HPS * qt, HPS
                    elif qt == 1:
                        src, a, n = psS[:, 0:512].rearrange("p (b n) -> p b n", n=P), 0, 2 * HPS
                    else:
                        src, a, n = psS[:, 512:512 + HPS * P].rearrange("p (b n) -> p b n", n=P), 2 * HPS, HPS
                    dve.tensor_reduce(nred[:, u.b % 2, g, a:a + n], src, op=ALU.max, axis=AX.X,
                                      negate=True).then_inc(S["red"], 1)

            def nmaxs(sl):
                u = sl.unit(OFF_MAX)
                if not u:
                    return
                b = u.b % 2
                wait(dve, "red", at(2 * NSTEP, u, 2 * NSTEP))
                wait(dve, "mres", at(1, u, -1))
                r = nred[:, b, :, :]
                o = nmax[:, b, :, :].rearrange("p q (s h) -> p q s h", h=HPS)
                if u.layer == 0:
                    wait(dve, "spev", at(1, u, 1))
                    sp4 = spad[:, u.b, :, :].rearrange("p q (s h) -> p q s h", h=HPS)
                    for q in range(TPS):
                        tt(o[:, q, :, :], r[:, :, HPS * q:HPS * q + HPS], sp4[:, q, :, :], ALU.min).then_inc(S["nmax"], 1)
                    wait(dve, "nmax", at(2, u, 2))
                    wait(dve, "epad", at(1, u, -1))
                    tt(earg[:, b, :, :], nmax[:, b, :, :], spad[:, u.b, :, :], ALU.subtract).then_inc(S["earg"], 1)
                else:
                    r2 = r[:, :, 0:4].rearrange("p s (h k) -> p s h k", k=2)
                    tt(o[:, 1, :, :], r2[:, :, :, 0], r2[:, :, :, 1], ALU.min).then_inc(S["nmax"], 1)
                    dve.tensor_copy(o[:, 0, :, :], r[:, :, 4:6]).then_inc(S["nmax"], 1)

            def stats(x, st, s1):
                for i in range(TPS):
                    dve.bn_stats(st[:, i, :], x[:, i, :]).then_inc(S[s1], 1)

            def aggr(st, m, s2):
                for i in range(TPS):
                    dve.bn_aggr(m[:, i, :], st[:, i, :]).then_inc(S[s2], 1)

            def normal(o, x, m, r, done):
                for i in range(TPS):
                    ts(o[:, i, :], x[:, i, :], m[:, i, 0:1], r[:, i, 0:1], ALU.subtract, ALU.mult).then_inc(S[done], 1)

            def ln_stats(sl):
                u = sl.unit(OFF_LOAD)
                if not u:
                    return
                moved(dve, "xin", u)
                stats(xin[:, u.b], stat[:, u.b], "stats")

            def aggregate(sl, g, off, layers, name, st, m, first):
                u = sl.unit(off, layers)
                if u:
                    wait(dve, name, at(2, u, 2, first))
                reduce(sl, g)
                if u:
                    b = u.b if st is not stat3 else u.b % 2
                    aggr(st[:, b], m[:, b], "mvs" + name[5:])

            def ln_stats2(sl):
                u = sl.unit(OFF_LOAD, (1,))
                if not u:
                    return
                wait(dve, "lnout", at(2, u, 2))
                stats(xn[:, u.b], stat2[:, u.b], "stats2")

            def ln3_stats(sl):
                u = sl.unit(OFF_ROUTE, (1, 2))
                if not u:
                    return
                b = u.b % 2
                wait(dve, "zout", at(1, u, 1))
                stats(zb[:, b], stat3[:, b], "stats3")

            def ln3_apply(sl):
                u = sl.unit(OFF_ROUTE, (1, 2))
                if not u:
                    return
                b = u.b % 2
                wait(dve, "rstds3", at(1, u, 1, NSEQ))
                wait(dve, "mvs3", at(2, u, 2, NSEQ))
                moved(dve, "hstore", u, 2, NSEQ)
                wait(dve, "hT", at(1, u, -1, NSEQ))
                if u.layer == 1:
                    normal(hn[:, b], zb[:, b], mv3[:, b], rstd3[:, b], "hout")
                else:
                    for i in range(TPS):
                        x = ts(hn[:, b, i, :], zb[:, b, i, :], mv3[:, b, i, 0:1], rstd3[:, b, i, 0:1],
                               ALU.subtract, ALU.mult)
                    x.then_inc(S["hfin"], 1)

            def rope_cos(sl):
                u = sl.unit(OFF_PROJ, (1,))
                if not u:
                    return
                wait(dve, "qk", at(1, u, 1))
                wait(dve, "lo", at(1, u, 0))
                tt(qkf[:, :, :], psM[:, :].rearrange("p (a t) -> p a t", a=2),
                   cf[:, CF["cosq"][0]:CF["cosk"][1]].rearrange("p (a t) -> p a t", a=2), ALU.mult).then_inc(S["qkev"], 2)

            def rope_sin(sl, half):
                u = sl.unit(OFF_PROJ, (1,))
                if not u:
                    return
                if half == 0:
                    wait(dve, "qk", at(1, u, 1))
                    wait(dve, "ropeadd", at(1, u, 0, NSEQ))
                a, b = (0, P // 2) if half == 0 else (P // 2, 0)
                x = tt(qks[a:a + P // 2, :, :], psM[b:b + P // 2, :].rearrange("p (a t) -> p a t", a=2),
                       cf[b:b + P // 2, CF["sinq"][0]:CF["sink"][1]].rearrange("p (a t) -> p a t", a=2), ALU.mult)
                if half == 1:
                    x.then_inc(S["rotev"], 1)

            def sp_ev(sl):
                u = sl.unit(OFF_PROJ, (0,))
                if not u:
                    return
                wait(dve, "sp", at(1, u, 1))
                tt(spad[:, u.b, :, :], psM[:, 0:TPS * H].rearrange("p (q h) -> p q h", q=TPS),
                   Fc("padfar").unsqueeze(2).to_broadcast([P, TPS, H]), ALU.add).then_inc(S["spev"], 1)

            def v_ev(sl):
                u = sl.unit(OFF_SPREAD)
                if not u:
                    return
                wait(dve, "v", at(1, u, 1))
                wait(dve, "pv", at(GROUPS, u, GROUPS - GROUPS * NBUF))
                src = psM[:, 0:TPS * C].rearrange("p (a h d) -> p a h d", a=TPS, h=H)
                dst = vv[:, u.b, 0:TPS * H * 32].rearrange("p (a h c) -> p a h c", a=TPS, h=H)[:, :, :, HALF:HALF + D]
                if u.layer == 1:
                    dve.tensor_copy(dst, src).then_inc(S["vev"], 1)
                else:
                    bias = rows[:, BV0 if u.layer == 0 else BV2, :].rearrange("p (h d) -> p h d", h=H)
                    tt(dst, src, bias.unsqueeze(1).to_broadcast([P, TPS, H, D]), ALU.add).then_inc(S["vev"], 1)

            def norm(sl):
                u = sl.unit(OFF_OUT)
                if not u:
                    return
                b = u.b % 2
                wait(dve, "ott", at(1, u, 1))
                o = psO[:, :].rearrange("p (n c) -> p n c", c=HALF)
                num, dn_, r = o[:, :, 0:D], o[:, :, D], rden[:, b, :]
                if u.layer == 0:
                    wait(dve, "epad64", at(1, u, 1))
                    e = epad[:, u.b, :, :].rearrange("p q h -> p (q h)")
                    wait(dve, "norm", at(1, u, 0))
                    tt(den[:, b, :], dn_, e, ALU.add).then_inc(S["den"], 1)
                    tt(pnum[:, :, :], num, e.unsqueeze(2).to_broadcast([P, TPS * H, D]), ALU.subtract).then_inc(S["pnum"], 1)
                    wait(dve, "den", at(1, u, 1))
                    dn_, num = den[:, b, :], pnum[:, :, :]
                dve.reciprocal(r, dn_).then_inc(S["rden"], 1)
                wait(dve, "rden", at(1, u, 1))
                if u.layer == 0:
                    wait(dve, "pnum", at(1, u, 1))
                wait(dve, "ob", at(1, u, -1))
                tt(on[:, b, :, :], num, r.unsqueeze(2).to_broadcast([P, TPS * H, D]), ALU.mult).then_inc(S["norm"], 1)

            def residual(sl):
                u = sl.unit(OFF_OUT)
                if not u:
                    return
                b = u.b % 2
                wait(dve, "op", at(1, u, 1))
                if u.layer == 1:
                    moved(dve, "yresdma", u, 0, NSEQ)
                    r = yres
                else:
                    wait(dve, "rbias", (u.n - (0 if u.layer == 0 else NSEQ)) + 1)
                    r = xres
                moved(dve, "xstore", u, 2)
                if u.layer >= 1 and u.rep >= NSEQ + 2:
                    wait(dve, "hfin", at(1, u, -1, NSEQ))
                tt(zb[:, b, :, :], psO[:, 0:TPS * C].rearrange("p (q c) -> p q c", q=TPS), r[:, b, :, :],
                   ALU.add).then_inc(S["zout"], 1)

            def lg_ev(sl):
                u = sl.unit(OFF_LOGIT, (1, 2))
                if not u:
                    return
                E = (E0, E1)[u.layer - 1]
                wait(dve, "lg", at(1, u, 1, NSEQ))
                dst = lg[u.layer - 1][:, bass.ds(u.s * TPS, TPS), :]
                src = psM[:, 0:TPS * E].rearrange("p (t e) -> p t e", e=E)
                if u.layer == 1:
                    dve.tensor_copy(dst, src).then_inc(S["lgev"], 1)
                else:
                    tt(dst, src, br[:, :].unsqueeze(1).to_broadcast([P, TPS, E]), ALU.add).then_inc(S["lgev"], 1)

            def step(sl):
                nmaxs(sl)
                reduce(sl, 0)
                ln3_stats(sl)
                ln_stats(sl)
                v_ev(sl)
                aggregate(sl, 1, OFF_ROUTE, (1, 2), "stats3", stat3, mv3, NSEQ)
                norm(sl)
                lg_ev(sl)
                aggregate(sl, 2, OFF_LOAD, (0, 1, 2), "stats", stat, mv, 0)
                rope_cos(sl)
                reduce(sl, 3)
                ln3_apply(sl)
                sp_ev(sl)
                rope_sin(sl, 0)
                reduce(sl, 4)
                rope_sin(sl, 1)
                ln_stats2(sl)
                aggregate(sl, 5, OFF_LOAD, (1,), "stats2", stat2, mv2, NSEQ)
                reduce(sl, 6)
                residual(sl)
                reduce(sl, 7)

            def mix(i):
                ntl, E, F = ((NTILE0, E0, F0), (NTILE1, E1, F1))[i]
                m = {k: v[i] for k, v in M.items()}
                made = [0]

                def link(ins):
                    made[0] += 1
                    ins.then_inc(m["dve"], 1)
                    dve.wait_ge(m["dve"], made[0])

                dve.wait_ge(S["tready"], NSTEP * NSEQ * (2, 3)[i])
                dve.tensor_copy(hx[:, 0:NT, 2 * C], Fc("tokid")).then_inc(m["hcopy"], 1)
                dve.wait_ge(S["lgev"], NSEQ * (i + 1))
                L = lg[i][:, :, :]
                eid = Fc("eid")[:, 0:E].unsqueeze(1).to_broadcast([P, NT, E])
                link(dve.tensor_reduce(top[:, :], L, op=ALU.max, axis=AX.X))
                link(tt(eq[:, :, 0:E], L, top[:, :].unsqueeze(2).to_broadcast([P, NT, E]), ALU.is_equal))
                link(tt(eqi[:, :, 0:E], eq[:, :, 0:E], eid, ALU.mult))
                link(dve.tensor_reduce(pick[:, :], eqi[:, :, 0:E], op=ALU.min, axis=AX.X))
                link(tt(oh[:, :, 0:E], eid, pick[:, :].unsqueeze(2).to_broadcast([P, NT, E]), ALU.is_equal))
                with nc.allow_low_precision(reason="counts to 32 are exact in bfloat16"):
                    link(dve.tensor_reduce(cnt[:, 0:E], oh[:, :, 0:E].rearrange("p t e -> p e t"),
                                           op=ALU.add, axis=AX.X))
                dve.wait_ge(m["rank"], 1)
                link(ts(padi[:, 0:E], psT[1][:, 0:E], float(P - 1), None, ALU.add))
                link(ts(padi2[:, 0:E], padi[:, 0:E], 7, 7, ALU.logical_shift_right, ALU.logical_shift_left))
                link(dve.tensor_copy(padf[:, 0:E], padi2[:, 0:E]))
                link(dve.memset(base[:, 0:1], 0.0))
                for e in range(E):
                    link(tt(base[:, e + 1:e + 2], base[:, e:e + 1], padf[:, e:e + 1], ALU.add))
                link(tt(rk[:, :, 0:E], psT[0][:, 0:NT * E].rearrange("p (t e) -> p t e", e=E),
                        base[:, 0:E].unsqueeze(1).to_broadcast([P, NT, E]), ALU.add))
                link(tt(rk2[:, :, 0:E], rk[:, :, 0:E], oh[:, :, 0:E], ALU.mult))
                link(dve.tensor_reduce(destf[:, :], rk2[:, :, 0:E], op=ALU.add, axis=AX.X))
                dve.tensor_copy(dest[i][:, :], destf[:, :]).then_inc(m["dest"], 1)
                link(tt(ge[:, 0:ntl, 0:E - 1], cf[0:1, CF["start"][0]:CF["start"][0] + ntl].unsqueeze(2).to_broadcast(
                    [1, ntl, E - 1]), base[0:1, 1:E].unsqueeze(1).to_broadcast([1, ntl, E - 1]), ALU.is_ge))
                link(dve.tensor_reduce(tef[:, 0:ntl], ge[:, 0:ntl, 0:E - 1], op=ALU.add, axis=AX.X))
                dve.tensor_copy(tei[i][:, :], tef[:, 0:ntl]).then_inc(m["te"], 1)
                if i == 1:
                    dve.wait_ge(m["te"], 1)
                    dve.wait_ge(m["bias"], 32)
                def hidden(j, it):
                    jx = j + 4 * it
                    if i == 0:
                        dve.wait_ge(m["actg"], jx + 1)
                        if j >= 2:
                            dve.wait_ge(m["at"], jx - 1)
                        tt(mixact[:, j % 2, 0:F], gate[:, j % 2, 0:F], psT[j % 2][:, 512:512 + F],
                           ALU.mult).then_inc(m["act"], 1)
                    else:
                        e = dve.value_load(tei[i][0:1, bass.ds(jx, 1)], min_val=0, max_val=E - 1)
                        dve.wait_ge(m["up"], jx + 1)
                        if j >= 2:
                            dve.wait_ge(m["act"], jx - 1)
                        tt(gate[:, j % 2, 0:F], psT[j % 2][:, 0:F], b1r[:, bass.ds(e * F, F)],
                           ALU.add).then_inc(m["actg"], 1)
                    if j >= 4:
                        dve.wait_ge(MD["store"][i][j % 4], 16 * (j // 4 + it))
                    if i == 1:
                        tt(yt[:, j % 4, :], hx[:, bass.ds(jx, 1), C:2 * C].rearrange("p t c -> p (t c)"),
                           b2r[:, bass.ds(e * C, C)], ALU.add).then_inc(m["ready"], 1)

                def turned(j, it):
                    jx = j + 4 * it
                    dve.wait_ge(m["at"], jx + 1)
                    if j >= 2:
                        dve.wait_ge(m["prod"], jx - 1)
                    dve.tensor_copy(actT[:, j % 2, 0:F], psS[:, 512 * (j % 2):512 * (j % 2) + F]).then_inc(m["atev"], 1)

                def result(j, it):
                    jx = j + 4 * it
                    if i == 0:
                        r = hx[:, bass.ds(jx, 1), C:2 * C].rearrange("p t c -> p (t c)")
                    else:
                        r = yt[:, j % 4, :]
                        dve.wait_ge(m["ready"], jx + 1)
                    dve.wait_ge(m["prod"], jx + 1)
                    tt(yt[:, j % 4, :], psO[:, 0:C], r, ALU.add).then_inc(m["yev"], 1)

                def tile(j, it):
                    if j < ntl:
                        hidden(j, it)
                    if 1 <= j <= ntl:
                        turned(j - 1, it)
                    if j >= 2:
                        result(j - 2, it)

                tile(0, 0)
                tile(1, 0)
                for q in range(2):
                    dve.wait_ge(MD["load"][i][q], 16)
                where = hx[:, 0:ntl, 2 * C]
                ts(idf[:, 0:ntl], where, 0.0, Fc("row"), ALU.is_equal, ALU.mult).then_inc(m["idf"], 1)
                dve.wait_ge(m["idf"], 1)
                tt(idf[:, 0:ntl], idf[:, 0:ntl], where, ALU.add).then_inc(m["idf"], 1)
                dve.wait_ge(m["idf"], 2)
                ts(ids[i][:, :], idf[:, 0:ntl], float(OUTSIDE), None, ALU.add).then_inc(m["ids"], 1)
                tile(2, 0)
                tile(3, 0)
                with dve.Fori(0, (ntl - 8) // 4) as it:
                    for j in range(4):
                        tile(4 + j, it)
                for j in range(ntl - 4, ntl + 2):
                    tile(j, 0)

            dve.memset(vv[:, :, :], 0.0).then_inc(S["setup"], 1)
            dve.wait_ge(S["setup"], 1)
            dve.memset(vv[:, :, 0:TPS * H * 32].rearrange("p b (h c) -> p b h c", c=32)[:, :, :, HALF + D:HALF + D + 1], 1.0).then_inc(S["setup"], 1)
            dve.wait_ge(S["const"], NCONST)
            ts(cols[:, BQ2S:BQ2S + 1], cols[:, BQ2:BQ2 + 1], float(D) ** -0.5, None, ALU.mult).then_inc(S["setup"], 1)
            dve.wait_ge(S["setup"], 3)
            slots(dve, step, 0, 2 * NSEQ)
            mix(0)
            made = [0]

            def link(ins):
                made[0] += 1
                ins.then_inc(S["pos"], 1)
                dve.wait_ge(S["pos"], made[0])

            dve.wait_ge(S["wload"], NLATE)
            dve.wait_ge(S["pv"], 2 * NSEQ * GROUPS)
            link(dve.tensor_reduce(posc[:, 0, :], posr[:, :, :], op=ALU.add, axis=AX.X))
            for a in range(PARTS):
                link(dve.tensor_copy(poscp[:, a, :], posc[:, a, :]))
                if a + 1 < PARTS:
                    link(tt(posc[:, a + 1, :], posc[:, a, :], poscp[:, a, :], ALU.subtract))
            dve.tensor_copy(poscb, poscp[:, :, :].unsqueeze(3).to_broadcast([1, PARTS, 8, SEQ])).then_inc(S["posb"], 1)
            dve.wait_ge(S["posb"], 1)
            slots(dve, step, 2 * NSEQ, 3 * NSEQ)
            mix(1)

        @block.gpsimd
        def _(pool):
            tt, ts, cp = pool.tensor_tensor, pool.tensor_scalar, pool.tensor_copy

            def rstds(u, first, m, v, r, need, mid, done, shift):
                wait(pool, need, at(2, u, 2, first))
                tt(v[:, :, 1:2], m[:, :, 1:2], eps[:, :].unsqueeze(2), ALU.add).then_inc(S[mid], 1)
                wait(pool, mid, at(1, u, 1, first))
                if shift:
                    tt(v[:, :, 0:1], nil[:, :].unsqueeze(2), m[:, :, 0:1], ALU.subtract)
                tt(r[:, :, 0:1], v[:, :, 1:2], half[:, :].unsqueeze(2), ALU.pow).then_inc(S[done], 1)
                if shift:
                    wait(pool, done, at(1, u, 1, first))
                    tt(r[:, :, 1:2], v[:, :, 0:1], r[:, :, 0:1], ALU.mult).then_inc(S[shift], 1)

            def xz(sl):
                u = sl.unit(OFF_ROUTE, (1,))
                if not u:
                    return
                wait(pool, "zout", at(1, u, 1))
                moved(pool, "resdma", u)
                moved(pool, "xstore", u, 2)
                tt(xzb[:, u.b % 2], zb[:, u.b % 2], xres[:, u.b % 2], ALU.add).then_inc(S["xz"], 1)

            def split_max(sl):
                u = sl.unit(OFF_MAX)
                if not u:
                    return
                b = u.b % 2
                zero_m = nil[:, :].unsqueeze(2).to_broadcast([P, TPS, H])
                wait(pool, "nmax", at(2, u, 2))
                wait(pool, "mt", at(1, u, 0))
                tt(mparts[:, :, 0, :], nmax[:, b], zero_m, ALU.add).then_inc(S["mhi"], 1)
                wait(pool, "mhi", at(1, u, 1))
                tt(mres[:, b], nmax[:, b], mparts[:, :, 0, :], ALU.subtract).then_inc(S["mres"], 1)
                wait(pool, "mres", at(1, u, 1))
                tt(mparts[:, :, 1, :], mres[:, b], zero_m, ALU.add).then_inc(S["mmid"], 1)
                wait(pool, "mmid", at(1, u, 1))
                tt(mparts[:, :, 2, :], mres[:, b], mparts[:, :, 1, :], ALU.subtract).then_inc(S["mlo"], 1)

            def rope_add(sl):
                u = sl.unit(OFF_PROJ, (1,))
                if not u:
                    return
                wait(pool, "rotev", at(1, u, 1, NSEQ))
                wait(pool, "qkev", at(2, u, 2))
                tt(qkf[:, :, :], qkf[:, :, :], qks[:, :, :], ALU.add).then_inc(S["ropeadd"], 1)

            def split(sl):
                u = sl.unit(OFF_PROJ)
                if not u:
                    return
                if u.layer == 1:
                    wait(pool, "ropeadd", at(1, u, 1, NSEQ))
                else:
                    wait(pool, "qkev", at(2, u, 2))
                if u.layer == 0:
                    wait(pool, "sp", at(1, u, 1))
                wait(pool, "hi", at(1, u, 1))
                tt(qkf[:, :, :], qkf[:, :, :], parts[:, 0], ALU.subtract).then_inc(S["resid"], 1)

            def split_rest(sl):
                u = sl.unit(OFF_SPREAD)
                if not u:
                    return
                wait(pool, "mid", at(1, u, 1))
                tt(parts[:, 2], qkf[:, :, :], parts[:, 1], ALU.subtract).then_inc(S["lo"], 1)

            def conv(sl):
                u = sl.unit(OFF_PROJ, (1,))
                if not u:
                    return
                b = u.b % 2
                x, o = xT[:, b, :], cT[:, b, :]
                wait(pool, "xtev", at(1, u, 1))
                wait(pool, "v", at(1, u, -1))
                tt(o, x, convw[:, 2:3].to_broadcast([P, SEQ]), ALU.mult).then_inc(S["tap0"], 1)
                tt(tap[:, 0, :], x, convw[:, 1:2].to_broadcast([P, SEQ]), ALU.mult).then_inc(S["tap1"], 1)
                tt(tap[:, 1, :], x, convw[:, 0:1].to_broadcast([P, SEQ]), ALU.mult).then_inc(S["tap2"], 1)
                wait(pool, "tap0", at(1, u, 1, NSEQ))
                wait(pool, "tap1", at(1, u, 1, NSEQ))
                tt(o[:, 1:SEQ], o[:, 1:SEQ], tap[:, 0, 0:SEQ - 1], ALU.add).then_inc(S["tap3"], 1)
                wait(pool, "tap2", at(1, u, 1, NSEQ))
                wait(pool, "tap3", at(1, u, 1, NSEQ))
                tt(o[:, 2:SEQ], o[:, 2:SEQ], tap[:, 1, 0:SEQ - 2], ALU.add).then_inc(S["conv"], 1)

            def res_bias(sl):
                u = sl.unit(OFF_OUT, (0, 2))
                if not u:
                    return
                moved(pool, "resdma", u)
                x, b = xres[:, u.b % 2], rows[:, BO0 if u.layer == 0 else BO2, :]
                tt(x, x, b.unsqueeze(1).to_broadcast([P, TPS, C]), ALU.add).then_inc(S["rbias"], 1)

            def affine(sl):
                u = sl.unit(OFF_ROUTE, (1,))
                if not u:
                    return
                x = hn[:, u.b % 2]
                wait(pool, "hout", at(2, u, 2, NSEQ))
                for name, r, s_ in (("hw", LN2W, ALU.mult), ("hfin", LN2B, ALU.add)):
                    tt(x, x, rows[:, r, :].unsqueeze(1).to_broadcast([P, TPS, C]), s_).then_inc(S[name], 1)
                    if name == "hw":
                        wait(pool, "hw", at(1, u, 1, NSEQ))

            def pads(sl):
                u = sl.unit(OFF_MAX, (0,))
                if not u:
                    return
                wait(pool, "epad", at(1, u, 1))
                e = epad[:, u.b]
                tt(e, e, Fc("pad64").unsqueeze(2).to_broadcast([P, TPS, H]), ALU.mult).then_inc(S["epad64"], 1)

            def step(sl):
                ur, ul = sl.unit(OFF_ROUTE, (1, 2)), sl.unit(OFF_LOAD)
                split_rest(sl)
                conv(sl)
                if ur:
                    b = ur.b % 2
                    rstds(ur, NSEQ, mv3[:, b], rstd3v[:, b], rstd3[:, b], "mvs3", "veps3", "rstds3", None)
                split_max(sl)
                if ul:
                    rstds(ul, 0, mv[:, ul.b], rstdv[:, ul.b], rstd[:, ul.b], "mvs", "veps", "rstds", "shifts")
                xz(sl)
                pads(sl)
                res_bias(sl)
                affine(sl)
                rope_add(sl)
                if ul and ul.layer == 1:
                    rstds(ul, NSEQ, mv2[:, ul.b], rstd2v[:, ul.b], rstd2[:, ul.b], "mvs2", "veps2", "rstds2", "shifts2")
                split(sl)

            def mix(i):
                m = {k: v[i] for k, v in M.items()}
                ntl = (NTILE0, NTILE1)[i]
                pool.wait_ge(S["wload"], NLATE)
                pool.wait_ge(m["hcopy"], 5)
                pool.wait_ge(m["xres"], 16)
                pool.wait_ge(m["dest"], 1)
                for tt_ in range(NT):
                    pool.indirect_dma_start(hs_d[i][:, :], bass.IndirectOffsetOnAxis(ap=dest[i][:, tt_:tt_ + 1], axis=0),
                                            hx[:, tt_, :], None).then_inc(m["scat"], 16)
                pool.wait_ge(m["ids"], 1)
                for j in range(ntl):
                    pool.wait_ge(m["yev"], j + 1)
                    pool.indirect_dma_start((x2_d, out)[i][:, :], bass.IndirectOffsetOnAxis(ap=ids[i][:, j:j + 1], axis=0),
                                            yt[:, j % 4, :], None, bounds_check=NSEQ * SEQ - 1,
                                            oob_is_err=False).then_inc(MD["store"][i][j % 4], 16)

            pool.memset(zrow[:, :], 0.0).then_inc(S["zero"], 1)
            pool.memset(half[:, :], -0.5).then_inc(S["half"], 1)
            pool.memset(mparts[:, :, :, :], 0.0).then_inc(S["half"], 1)
            pool.memset(nil[:, :], 0.0).then_inc(S["half"], 1)
            pool.memset(eps[:, :], EPS).then_inc(S["half"], 1)
            pool.wait_ge(S["half"], 4)
            pool.wait_ge(S["const"], NCONST)
            slots(pool, step, 0, 2 * NSEQ)
            mix(0)
            slots(pool, step, 2 * NSEQ, 3 * NSEQ)
            mix(1)




def _constants():
    import numpy as np
    bf = mybir.dt.np(mybir.dt.bfloat16)
    far = -1e30
    i, j = np.arange(P)[:, None], np.arange(P)[None, :]
    cf = np.zeros((P, CF["all"]), np.float32)

    def put(dst, where, name, a):
        dst[:, where[name][0]:where[name][1]] = a

    inv = (np.float32(1.0) / np.float32(10000.0) ** (np.arange(0, D, 2, dtype=np.float32) / np.float32(D))).astype(np.float32)
    freqs = (np.arange(SEQ, dtype=np.float32)[:, None] * inv[None, :]).astype(np.float32)
    emb = np.concatenate([freqs, freqs], axis=-1).T
    cos, sin = np.cos(emb), np.sin(emb) * np.where(np.arange(D) < D // 2, 1, -1)[:, None]
    cos, sin = np.repeat(cos, H, axis=0), np.repeat(sin, H, axis=0)
    scale = float(D) ** -0.5
    put(cf, CF, "ident", np.eye(P))
    put(cf, CF, "cosq", cos * scale)
    put(cf, CF, "cosk", cos)
    put(cf, CF, "sinq", sin * scale)
    put(cf, CF, "sink", sin)
    put(cf, CF, "heads", np.arange(P)[:, None] % H == np.arange(H)[None, :])
    tok = np.arange(SEQ).reshape(TPS, P).T
    put(cf, CF, "padfar", np.where((tok < WS) | (tok >= SEQ - WS), 0.0, 1e30))
    put(cf, CF, "pad64", float(WS))
    put(cf, CF, "ones", 1.0)
    put(cf, CF, "eid", np.arange(8)[None, :] - 64.0)
    put(cf, CF, "start", P * np.arange(64)[None, :])
    put(cf, CF, "tokid", P * j[:, 0:NT] + i - OUTSIDE)
    put(cf, CF, "row", i)
    cb = np.zeros((P, CB["all"]), bf)
    jb = np.arange(BAND)[None, :]
    band = np.concatenate([np.where(np.abs(jb - i) <= WS, 0, far), np.where((jb >= i) & (jb <= i + 2 * WS), 0, far)], 1)
    put(cb, CB, "ident", np.eye(P))
    put(cb, CB, "band", band)
    put(cb, CB, "causal_q", np.where(j > i, far, 0))
    put(cb, CB, "causal_k", np.where(j < i, far, 0))
    put(cb, CB, "before", i < j)
    put(cb, CB, "ones", 1.0)
    f = (1.0 / 1250.0 ** (np.arange(C // 2, dtype=np.float64) / (C // 2)))[:C // 4].astype(np.float32).astype(np.float64)
    th = np.arange(SEQ)[None, :] * f[:, None]
    ti, tj = np.empty((8, D, SEQ)), np.empty((8, D, SEQ))
    for h in range(8):
        for a in range(4):
            x = th[4 * h + a]
            ti[h, 2 * a], ti[h, 2 * a + 1] = np.cos(x), np.sin(x)
            tj[h, 2 * a], tj[h, 2 * a + 1] = np.cos(x) - np.sin(x), np.cos(x) + np.sin(x)

    def split(a):
        out, r = [], a.astype(np.float32)
        for _ in range(PARTS):
            out.append(r.astype(bf))
            r = r - out[-1].astype(np.float32)
        return out
    pi, pj = split(ti), split(tj)
    trig = np.zeros((2, ROWS, H, SEQ), bf)
    for n, (a, b) in enumerate(PAIRS):
        trig[0, D * n:D * n + D, 0:8] = pi[a].transpose(1, 0, 2)
        trig[1, D * n:D * n + D, 0:8] = pj[b].transpose(1, 0, 2)
    trig[0, 0:PARTS, 8:H] = 1.0
    return cf, cb, trig, np.ones((PARTS, H, SEQ), bf)


def kernel(**inputs):
    import numpy as np
    import concourse.bacc as bacc
    from concourse.bass_utils import run_bass_kernel_spmd

    g = {k: np.asarray(v) for k, v in inputs.items()}
    hd = np.arange(P).reshape(H, D).T.reshape(P)
    oh = np.arange(P).reshape(2, PACK, 4, D).transpose(0, 2, 1, 3).reshape(P)
    wqkv, aw = g["L1_attn_w_qkv"], g["L0_ffn_attn_w"]
    bqkv = g["L1_attn_b_qkv"]
    cf, cb, trig, ones = _constants()
    A, F_ = "L0_attn_", "L0_ffn_"
    ws = [g[A + "wq"].T[:, hd], g[A + "wk"].T[:, hd], g[A + "wv"].T, g[A + "wo"].T[oh],
          aw[:, 0:C][:, hd], aw[:, C:2 * C][:, hd], aw[:, 2 * C:], g[F_ + "proj_w"][oh],
          wqkv[0:C].T[:, hd], wqkv[C:2 * C].T[:, hd], wqkv[2 * C:].T, g["L1_attn_w_proj"].T[oh]]
    arrays = {
        "x": g["L0_attn_x"].reshape(NSEQ * SEQ, C), "cf": cf, "cb": cb, "trig": trig, "onesb": ones,
        "wt": np.stack(ws, axis=1),
        "cols": np.stack([g[A + "bq"][hd], g[A + "bk"][hd], g[F_ + "ln1_w"], g[F_ + "ln1_b"],
                          bqkv[0:C][hd], bqkv[C:2 * C][hd]], axis=1),
        "convw": g[F_ + "conv_w"].reshape(C, 3),
        "rows": np.stack([g[A + "bv"], g[A + "bo"], g[F_ + "ln2_w"], g[F_ + "ln2_b"], bqkv[2 * C:],
                          g["L1_attn_b_proj"]]),
        "wr": np.concatenate([g[F_ + "router_w"], g["L1_ffn_Wr"]], axis=1), "br": g["L1_ffn_br"],
        "up0": g[F_ + "expert_wv"], "dn0": g[F_ + "expert_proj"],
        "up1": g["L1_ffn_W1"], "dn1": g["L1_ffn_W2"], "b1": g["L1_ffn_b1"].reshape(E1 * F1),
        "b2": g["L1_ffn_b2"].reshape(E1 * C), "pos": g["L1_attn_pos_independent"].reshape(1, 8, 8),
    }
    nc = bacc.Bacc("TRN2", target_bir_lowering=False, num_devices=1)
    arrays = {f"in_{k}": np.ascontiguousarray(v) for k, v in arrays.items()}
    t = {k[3:]: nc.dram_tensor(k, v.shape, mybir.dt.from_np(v.dtype), kind="ExternalInput").ap() for k, v in arrays.items()}
    out = nc.dram_tensor("out", (NSEQ * SEQ, C), mybir.dt.float32, kind="ExternalOutput").ap()
    build(nc, t, out)
    r = run_bass_kernel_spmd(nc, [arrays], core_ids=[0])
    return r.results[0]["out"].reshape(NSEQ, SEQ, C)
```

```python
import concourse.bass as bass
from concourse import mybir
from contextlib import ExitStack

NSEQ, SEQ, C, P = 16, 256, 128, 128
H, D = 16, 8
NT = NSEQ * SEQ // P
TPS = SEQ // P
WS = 64
BAND = 3 * WS
PARTS = 3
PAIRS = [(0, 0), (0, 1), (0, 2), (1, 0), (1, 1), (2, 0)]
ROWS = len(PAIRS) * D
ROW_BIAS = ROWS
ROW_MAX = (ROWS, ROWS, 2 * ROWS)
HPS = 2
NSTEP = H // HPS
GROUPS = H // 4
PACK = 2
HALF = 32 // PACK
SW = 2 * SEQ + 2 * P
NBUF = 4
E0, F0 = 4, 512
E1, F1 = 8, 384
NTILE0 = NT + E0
NTILE1 = NT + E1
ROW = 2 * C + 1
OUTSIDE = 2 * NSEQ * SEQ
REGION = NSEQ * SEQ
NOWHERE = 1 << 20
NROUTE = 10
EPS = 1e-5
OFF_LOAD, OFF_PROJ, OFF_SPREAD, OFF_SCORE, OFF_MAX, OFF_ATT, OFF_OUT, OFF_ROUTE, OFF_LOGIT = 5, 4, 3, 2, 1, 0, -1, -2, -3
ATTN0, ATTN1, ATTN2 = range(3)

CF = {}
CB = {}


def _columns():
    at = 0
    for name, n in (("ident", P), ("cosq", SEQ), ("cosk", SEQ), ("sinq", SEQ), ("sink", SEQ), ("heads", H),
                    ("padfar", TPS), ("pad64", TPS), ("ones", P), ("eid", 8), ("start", 64), ("tokid", NT), ("row", 1), ("region", 8)):
        CF[name] = (at, at + n)
        at += n
    CF["all"] = at
    at = 0
    for name, n in (("ident", P), ("band", 2 * BAND), ("causal_q", P), ("causal_k", P), ("before", P), ("ones", P)):
        CB[name] = (at, at + n)
        at += n
    CB["all"] = at


_columns()


class Unit:

    def __init__(self, rep, it):
        self.layer, self.rep, self.n = rep // NSEQ, rep, rep + NBUF * it
        self.s = self.n - NSEQ * self.layer
        self.b, self.it = rep % NBUF, it


class Slot:

    def __init__(self, rep, it, first, last):
        self.rep, self.it, self.first, self.last = rep, it, first, last

    def unit(self, off, layers=(0, 1, 2)):
        r = self.rep + off
        if not self.first <= r < self.last or r // NSEQ not in layers:
            return None
        return Unit(r, self.it)

    def before(self):
        return Slot(self.rep - 1, self.it, self.first, self.last)


def build(nc, t, out):
    f32, bf16, i32, u32 = mybir.dt.float32, mybir.dt.bfloat16, mybir.dt.int32, mybir.dt.uint32
    ALU, ACT, AX = mybir.AluOpType, mybir.ActivationFunctionType, mybir.AxisListType
    ctx = ExitStack()
    with ctx:
        def sb(name, shape, dt=f32):
            return ctx.enter_context(nc.sbuf_tensor(name, shape, dt))

        def pb(name, shape):
            return ctx.enter_context(nc.psum_tensor(name, shape, f32))

        def sem(name):
            return ctx.enter_context(nc.semaphore(name))

        def dram(name, shape):
            return nc.dram_tensor(name, shape, f32, kind="Internal").ap()

        x1_d = dram("x1_d", (NSEQ * SEQ, C))
        y_d = dram("y_d", (NSEQ * SEQ, C))
        x2_d = dram("x2_d", (NSEQ * SEQ, C))
        hs_d = [dram("hs0_d", (E0 * REGION + P, ROW)), dram("hs1_d", (E1 * REGION + P, ROW))]

        cf = sb("cf", [P, CF["all"]])
        cb = sb("cb", [P, CB["all"]], bf16)
        Fc = lambda name: cf[:, CF[name][0]:CF[name][1]]
        Bc = lambda name: cb[:, CB[name][0]:CB[name][1]]
        wt = sb("wt", [P, 12, C])
        WQ, WK, WV, WO = range(4)
        W = lambda layer, which: wt[:, 4 * layer + which, :]
        cols = sb("cols", [P, 9])
        BQ0, BK0, LN1W, LN1B, BQ2, BK2, BQ2S = range(7)
        convw = sb("convw", [P, 3])
        rows = sb("rows", [P, 6, C])
        BV0, BO0, LN2W, LN2B, BV2, BO2 = range(6)
        wr = sb("wr", [P, E0 + E1])
        br = sb("br", [P, E1])
        wm = sb("wm", [P, 2 * E1 * F1])
        up = [wm[:, 0:E0 * 2 * F0], wm[:, 0:E1 * F1]]
        dn = [wm[:, E0 * 2 * F0:E0 * 3 * F0], wm[:, E1 * F1:2 * E1 * F1]]
        posr = sb("posr", [1, 8, 8])
        posc = sb("posc", [1, 3, 8])
        poscp = sb("poscp", [1, PARTS, 8], bf16)

        xin = sb("xin", [P, NBUF, TPS, C])
        stat = sb("stat", [P, NBUF, TPS, 6])
        mv = sb("mv", [P, NBUF, TPS, 2])
        rstd = sb("rstd", [P, NBUF, TPS, 2])
        xn = sb("xn", [P, NBUF, TPS, C])
        stat2 = sb("stat2", [P, NBUF, TPS, 6])
        mv2 = sb("mv2", [P, NBUF, TPS, 2])
        rstd2 = sb("rstd2", [P, NBUF, TPS, 2])
        xn2 = sb("xn2", [P, 2, TPS, C])
        xT = sb("xT", [P, 2, SEQ])
        cT = sb("cT", [P, 2, SEQ])
        tap = sb("tap", [P, 2, SEQ])
        qkf = sb("qkf", [P, 2, SEQ])
        qks = sb("qks", [P, 2, SEQ])
        parts = sb("parts", [P, PARTS, 2, SEQ], bf16)
        arena = sb("arena", [P, 2 * NBUF * H * SEQ // 2])
        QK = [arena[:, i * H * SEQ // 2:(i + 1) * H * SEQ // 2].bitcast(bf16).rearrange("p (h t) -> p h t", h=H)
              for i in range(2 * NBUF)]
        QA, KA = QK[0:NBUF], QK[NBUF:]
        QKall = arena[:, :].bitcast(bf16).rearrange("p (b h t) -> p b h t", h=H, t=SEQ)
        vv = sb("vv", [P, NBUF, TPS * H * 32 + HALF])
        nred = sb("nred", [P, 2, NSTEP, 6])
        nmax = sb("nmax", [P, 2, TPS, H])
        mres = sb("mres", [P, 2, TPS, H])
        mparts = sb("mparts", [P, TPS, P // H, H], bf16)
        mT = sb("mT", [PARTS * H, SEQ], bf16)
        spad = sb("spad", [P, NBUF, TPS, H])
        epad = sb("epad", [P, NBUF, TPS, H])
        earg = sb("earg", [P, 2, TPS, H])
        pr = sb("pr", [P, 4, SW])
        poscb = pr[0:1, :, :].rearrange("o a b -> o (a b)").bitcast(bf16).rearrange(
            "o (a n) -> o a n", a=PARTS)
        oT = sb("oT", [P, GROUPS // PACK, SEQ])
        rden = sb("rden", [P, 2, TPS * H])
        den = sb("den", [P, 2, TPS * H])
        on = sb("on", [P, 2, TPS * H, D])
        onT = sb("onT", [P, SEQ])
        xres = sb("xres", [P, 2, TPS, C])
        yres = sb("yres", [P, 2, TPS, C])
        zb = sb("zb", [P, 2, TPS, C])
        stat3 = sb("stat3", [P, 2, TPS, 6])
        mv3 = sb("mv3", [P, 2, TPS, 2])
        rstd3 = sb("rstd3", [P, 2, TPS, 2])
        hrow = sb("hrow", [P, 2, TPS, ROW])
        pnum = sb("pnum", [P, TPS * H, D])
        hT = sb("hT", [P, SEQ])
        half = sb("half", [P, TPS])
        tick = sb("tick", [P, 1])
        nil = sb("nil", [P, TPS])
        eps = sb("eps", [P, TPS])
        rstdv = sb("rstdv", [P, NBUF, TPS, 2])
        rstd2v = sb("rstd2v", [P, NBUF, TPS, 2])
        rstd3v = sb("rstd3v", [P, 2, TPS, 2])
        lg = sb("lg", [P, TPS, E1])
        spare = sb("spare", [P, NT * C])
        zrow = sb("zrow", [P, ROW])

        def piece(n):
            a = piece.at
            piece.at += n
            return arena[:, a:a + n]
        piece.at = 0
        hx = piece(NTILE1 * ROW).rearrange("p (t c) -> p t c", c=ROW)
        b1r, b2r = piece(E1 * F1), piece(E1 * C)
        def small(b, n):
            a = small.at
            small.at += b * n
            return spare[:, a:a + b * n].rearrange("p (b c) -> p b c", b=b)
        small.at = 0
        xf, xfT, yt = small(2, C), small(2, C), small(4, C)
        gate, mixact, actT = small(2, F0), small(2, F0), small(2, F0)
        top = sb("top", [P, TPS])
        eq = sb("eq", [P, TPS, E1])
        eqi = sb("eqi", [P, TPS, E1])
        pick = sb("pick", [P, TPS])
        oh = sb("oh", [P, TPS, E1], bf16)
        acc = sb("acc", [P, E1], bf16)
        rk = sb("rk", [P, TPS, E1])
        rk2 = sb("rk2", [P, TPS, E1])
        destf = sb("destf", [P, TPS])
        dest = sb("dest", [P, 2, TPS], u32)
        cntf = sb("cntf", [P, E1])
        padi = sb("padi", [P, E1], i32)
        padi2 = sb("padi2", [P, E1], i32)
        padf = sb("padf", [P, E1])
        base = sb("base", [P, E1 + 1])
        fill = sb("fill", [P, 4, E1])
        filld = [sb("filld0", [P, E0], u32), sb("filld1", [P, E1], u32)]
        short = sb("short", [1, E1])
        rowf = sb("rowf", [1, 4, NTILE1])
        rowi = [sb("row0", [1, NTILE0], i32), sb("row1", [1, NTILE1], i32)]
        idt = sb("idt", [P, 2, NTILE1])
        ge = sb("ge", [1, NTILE1, E1])
        tef = sb("tef", [1, NTILE1])
        ids = [sb("ids0", [P, NTILE0], u32), sb("ids1", [P, NTILE1], u32)]
        tei = [sb("te0", [1, NTILE0], i32), sb("te1", [1, NTILE1], i32)]

        psS = pb("psS", [P, 1024])
        psT = [pb("psT0", [P, 1024]), pb("psT1", [P, 1024])]
        psO = pb("psO", [P, 512])
        psM = pb("psM", [P, 512])

        S = {n: sem("s_" + n) for n in (
            "const half pos wload dn1load zero setup posb posd krow "
            "stats mvs veps rstds shifts lnout lnout2 stats2 mvs2 veps2 rstds2 shifts2 "
            "xt xtev tap0 tap1 tap2 tap3 conv qk qkev rotev ropeadd sp spev "
            "hi resid mid lo v vev sready red nmax mhi mres mmid mlo mt mtev "
            "tready exp earg epad epad64 pv oev ott den rden norm pnum ob obev op rbias zout "
            "xz stats3 mvs3 veps3 rstds3 shifts3 hout hw hfin hT hTev lg lgev routing rank rankev tick ").split()}
        M = {n: [sem(f"m{i}_{n}") for i in range(2)] for n in (
            "dve count fill filled rows ht htev up act prod at atev yev "
            "ids idt te bias actg ready xf".split())}
        MD = {n: [[sem(f"m{i}{j}_{n}") for j in range(k)] for i in range(2)] for n, k in
              (("load", 4), ("store", 4))}

        def at(per, u, c, first=0):
            return per * (u.n - first) + c

        def wait(eng, name, value):
            if isinstance(value, int) and value <= 0:
                return
            eng.wait_ge(S[name], value)

        D_ = {n: [sem(f"d{i}_{n}") for i in range(2)] for n in
              "xin resdma yresdma xstore ystore rep mrow scat".split()}
        NREP = 2 * len(PAIRS)

        def moved(eng, name, u, back=0, first=0, n=1):
            r = u.rep - back
            ahead = 1 if name == "scat" else 0
            if r >= first - 2 * ahead:
                eng.wait_ge(D_[name][r % 2], 16 * n * ((r - first) // 2 + 1 + ahead + NBUF // 2 * u.it))

        TEN_M = [("v", OFF_SPREAD, (0, 1, 2), "vev", 1, 0), ("lg", OFF_LOGIT, (1, 2), "lgev", 1, NSEQ),
                 ("qk", OFF_PROJ, (0, 1, 2), "qkev", 2, 0), ("sp", OFF_PROJ, (0,), "spev", 1, 0),
                 ("rot", OFF_PROJ, (1,), "rotev", 1, NSEQ), ("rank", OFF_LOGIT, (1, 2), "rankev", 1, NSEQ),
                 ("mt", OFF_MAX, (0, 1, 2), "mtev", 1, 0),
                 ("hT", OFF_ROUTE, (1, 2), "hTev", 1, NSEQ), ("xt", OFF_LOAD, (0, 1, 2), "xtev", 1, 0)]
        TEN_O = [("pvB", OFF_OUT, (0, 1, 2), "oev", 2, 2), ("ott", OFF_OUT, (0, 1, 2), "norm", 1, 1),
                 ("pvA", OFF_ATT, (0, 1, 2), "oev", 2, 1), ("ob", OFF_OUT, (0, 1, 2), "obev", 1, 1),
                 ("op", OFF_OUT, (0, 1, 2), "zout", 1, 1), ("pvB0", OFF_ATT, (0, 1, 2), "oev", 2, 2)]

        def wait_bank(eng, table, slot, name):
            i = [x[0] for x in table].index(name)
            sl = slot
            for _ in range(3 * len(table)):
                i -= 1
                if i < 0:
                    i, sl = len(table) - 1, sl.before()
                _, off, layers, done, per, c = table[i]
                u = sl.unit(off, layers)
                if u:
                    if table is TEN_M:
                        wait(eng, done, at(per, u, per, c))
                    else:
                        wait(eng, done, at(per, u, c))
                    return

        def slots(eng, step, first, last):
            k = first - OFF_LOAD
            while k < last - OFF_LOGIT:
                inner = k % NSEQ
                if k >= first and inner == 3:
                    with eng.Fori(0, (NSEQ - 4 - 4) // NBUF) as i:
                        for j in range(NBUF):
                            step(Slot(k + j, i, first, last))
                    k += NSEQ - 4 - 4
                else:
                    step(Slot(k, 0, first, last))
                    k += 1

        def tok(d, s, n=TPS):
            return d.rearrange("(s t p) c -> s p t c", t=TPS, p=P)[bass.ds(s, 1), :, :, :].rearrange(
                "s p t c -> p (s t) c")

        wm_parts = [
            (cf[:, :], t["cf"]), (cb[:, :], t["cb"]),
            (wt[:, :, :], t["wt"]), (cols[:, 0:6], t["cols"]), (convw[:, :], t["convw"]),
            (rows[:, :, :], t["rows"].partition_broadcast(P)),
            (wr[:, :], t["wr"]), (br[:, :], t["br"].partition_broadcast(P)),
            (posr[:, :, :], t["pos"]),
        ]
        late_parts = [
            (up[0].rearrange("p (e n) -> p e n", e=E0), t["up0"].rearrange("e p n -> p e n")),
            (dn[0].rearrange("p (e k n) -> p e k n", e=E0, n=C), t["dn0"].rearrange("e (k p) n -> p e k n", p=P)),
        ]
        LATER = dict(zip(range(NSEQ - 5, NSEQ), late_parts))
        NCONST, NLATE = 16 * len(wm_parts), 16 * len(late_parts)
        mix1_parts = [
            (up[1].rearrange("p (e n) -> p e n", e=E1), t["up1"].rearrange("e p n -> p e n")),
            (dn[1].rearrange("p (e k n) -> p e k n", e=E1, n=C), t["dn1"].rearrange("e (k p) n -> p e k n", p=P)),
        ]
        bias_parts = [(b1r, t["b1"].partition_broadcast(P)), (b2r, t["b2"].partition_broadcast(P))]

        def v_of(u):
            return vv[:, u.b, 0:TPS * H * 32].rearrange("p (a h c) -> p a h c", a=TPS, h=H)[:, :, :, HALF:HALF + D]

        def ones_rows(eng, layer):
            r = ROW_MAX[layer]
            eng.dma_start(QKall[r:r + PARTS, NBUF:, :, :], t["onesb"].unsqueeze(1).to_broadcast(
                [PARTS, NBUF, H, SEQ])).then_inc(S["krow"], 16)

        block = ctx.enter_context(nc.Block())

        @block.sync
        def _(sp):
            for dst, src in wm_parts:
                sp.dma_start(dst, src).then_inc(S["const"], 16)

            def step(sl):
                ul, up, um = sl.unit(OFF_LOAD), sl.unit(OFF_SPREAD), sl.unit(OFF_MAX)
                uo, ur = sl.unit(OFF_OUT), sl.unit(OFF_ROUTE)
                if ul:
                    wait(sp, "lnout", at(2, ul, -2))
                    if ul.layer == 1:
                        moved(sp, "xstore", ul, NSEQ)
                    src = (t["x"], x1_d, x2_d)[ul.layer]
                    sp.dma_start(xin[:, ul.b, :, :], tok(src, ul.s)).then_inc(D_["xin"][ul.b % 2], 16)
                if up:
                    wait(sp, "hi", at(1, up, 1))
                    wait(sp, "tready", at(NSTEP, up, NSTEP - NSTEP * NBUF))
                    for n, made in enumerate((None, "mid", "lo")):
                        if made:
                            wait(sp, made, at(1, up, 1))
                        for w, buf in enumerate((QA, KA)):
                            for j, pair in enumerate(PAIRS):
                                if pair[w] == n:
                                    sp.dma_start(buf[up.b][D * j:D * j + D, :, :],
                                                 parts[:, n, w, :]).then_inc(D_["rep"][up.b % 2], 16)
                if uo:
                    if uo.rep >= NSEQ + 2 and uo.layer == 1:
                        wait(sp, "xz", at(1, uo, -1, NSEQ))
                    else:
                        wait(sp, "zout", at(1, uo, -1))
                    src = (t["x"], x1_d, x2_d)[uo.layer]
                    sp.dma_start(xres[:, uo.b % 2, :, :], tok(src, uo.s)).then_inc(D_["resdma"][uo.b % 2], 16)
                    if uo.layer == 1:
                        moved(sp, "ystore", uo, 0, NSEQ)
                        sp.dma_start(yres[:, uo.b % 2, :, :], tok(y_d, uo.s)).then_inc(D_["yresdma"][uo.b % 2], 16)
                if ur and ur.layer == 0:
                    wait(sp, "zout", at(1, ur, 1))
                    sp.dma_start(tok(x1_d, ur.s), zb[:, ur.b % 2, :, :]).then_inc(D_["xstore"][ur.b % 2], 16)
                if um:
                    wait(sp, "mtev", at(1, um, 1))
                    sp.dma_start(QA[um.b][ROW_MAX[um.layer]:ROW_MAX[um.layer] + PARTS, :, :], mT[:, :]).then_inc(D_["mrow"][um.b % 2], 16)
                if ul and ul.layer == 1:
                    wait(sp, "lnout", at(2, ul, 2))
                    sp.dma_start(tok(y_d, ul.s), xn[:, ul.b, :, :]).then_inc(D_["ystore"][ul.b % 2], 16)

            def mix(i):
                ntl = (NTILE0, NTILE1)[i]
                sp.wait_ge(S["tready"], NSTEP * NSEQ * (2, 3)[i])
                if i == 1:
                    for dst, src in bias_parts:
                        sp.dma_start(dst, src).then_inc(M["bias"][i], 16)
                sp.wait_ge(M["rows"][i], 1)
                sp.wait_ge(M["filled"][i], 16 * (E0, E1)[i])
                for q in range(2):
                    sp.wait_ge(D_["scat"][q], 32 * (1 + NSEQ // 2 * (i + 1)))

                def load(j, it):
                    if j >= 4:
                        sp.wait_ge(MD["load"][i][j % 4], 16 * (j // 4 + it))
                    r = sp.value_load(rowi[i][0:1, bass.ds(j + 4 * it, 1)], min_val=0, max_val=(E0, E1)[i] * REGION)
                    sp.dma_start(hx[:, bass.ds(j + 4 * it, 1), :].rearrange("p t c -> p (t c)"),
                                 hs_d[i][bass.ds(r, P), :]).then_inc(MD["load"][i][j % 4], 16)

                for j in range(4):
                    load(j, 0)
                with sp.Fori(0, (ntl - 4) // 4) as it:
                    for j in range(4):
                        load(4 + j, it)
                for q in range(4):
                    sp.wait_ge(MD["store"][i][q], 16 * (ntl // 4))

            ones_rows(sp, 0)
            slots(sp, step, 0, 2 * NSEQ)
            mix(0)
            slots(sp, step, 2 * NSEQ, 3 * NSEQ)
            mix(1)
            for name in ("xstore", "ystore"):
                for q in range(2):
                    sp.wait_ge(D_[name][q], 8 * NSEQ)

        @block.tensor
        def _(pe):
            mm = pe.matmul

            def score(sl, g):
                u = sl.unit(OFF_SCORE)
                if not u:
                    return
                if g == 0:
                    if u.layer == 2:
                        pe.wait_ge(S["posd"], 16 * (3 + NBUF))
                    moved(pe, "rep", u, n=NREP)
                q, k = QA[u.b], KA[u.b]
                n = ROW_MAX[u.layer]
                for qt in (1, 0):
                    wait(pe, "red", at(2 * NSTEP, u, 2 * g - qt))
                    o = psS[:, 512 * (1 - qt):512 * (2 - qt)]
                    keys = (64 * qt, BAND) if u.layer == 0 else (0, P * (qt + 1))
                    for hh in range(HPS):
                        h = HPS * g + hh
                        mm(o[:, hh * keys[1]:(hh + 1) * keys[1]], q[0:n, h, P * qt:P * qt + P],
                           k[0:n, h, keys[0]:keys[0] + keys[1]], start=(hh == 0), stop=False, skip_group_check=True)
                    o2 = o[:, 0:HPS * keys[1]].rearrange("p (h k) -> p h k", h=HPS)
                    if u.layer == 0:
                        mask = Bc("band")[:, BAND * qt:BAND * qt + BAND]
                    else:
                        mask = Bc("causal_q")
                        o2 = o2[:, :, P * qt:P * qt + P]
                    w = mask.shape[-1]
                    mm(o2, Bc("ident"), mask.unsqueeze(1).to_broadcast([P, HPS, w]), start=False, stop=True,
                       skip_group_check=True).then_inc(S["sready"], 1)

            def scoreT(sl, g):
                u = sl.unit(OFF_ATT)
                if not u:
                    return
                if g == 0:
                    pe.wait_ge(S["krow"], 16 * (1 + (u.layer == 2)))
                    moved(pe, "mrow", u)
                wait(pe, "exp", at(NSTEP, u, g - 1))
                n = ROW_MAX[u.layer] + PARTS
                q, k = QA[u.b][0:n], KA[u.b][0:n]
                for kt in range(2):
                    o = psT[g % 2][:, 512 * kt:512 * kt + 512]
                    q0, qn = (64 * kt, BAND) if u.layer == 0 else (P * kt, SEQ - P * kt)
                    for hh in range(HPS):
                        h = HPS * g + hh
                        mm(o[:, hh * qn:hh * qn + qn], k[:, h, P * kt:P * kt + P], q[:, h, q0:q0 + qn],
                           start=(hh == 0), stop=False, skip_group_check=True)
                    o2 = o[:, 0:HPS * qn].rearrange("p (h k) -> p h k", h=HPS)
                    if u.layer == 0:
                        mask = Bc("band")[:, BAND * kt:BAND * kt + BAND]
                    else:
                        mask = Bc("causal_k")
                        o2 = o2[:, :, 0:P]
                    w = mask.shape[-1]
                    last = mm(o2, Bc("ident"), mask.unsqueeze(1).to_broadcast([P, HPS, w]), start=False, stop=True,
                              skip_group_check=True)
                last.then_inc(S["tready"], 1)

            def pv(sl, gg):
                u = sl.unit(OFF_OUT if gg == 3 else OFF_ATT)
                if not u:
                    return
                if gg % 2 == 0:
                    wait_bank(pe, TEN_O, sl, "pvB0" if gg else "pvA")
                wait(pe, "exp", at(NSTEP, u, 2 * gg + 2))
                if gg == 0:
                    wait(pe, "vev", at(1, u, 1))
                for kt in range(2):
                    q0, qn = (64 * kt, BAND) if u.layer == 0 else (P * kt, SEQ - P * kt)
                    off = 0 if kt == 0 else HPS * (BAND if u.layer == 0 else SEQ)
                    for j in range(4):
                        h = 4 * gg + j
                        a = off + (h % 2) * qn
                        v = 32 * (kt * H + h) + HALF * (1 - gg % PACK)
                        last = mm(psO[32 * j:32 * j + 32, q0:q0 + qn], vv[:, u.b, v:v + 32],
                                  pr[:, (h // 2) % 4, a:a + qn], start=(kt == 0 and gg % PACK == 0),
                                  stop=(kt == 1 and gg % PACK == 1), skip_group_check=True)
                last.then_inc(S["pv"], 1)

            def ott(sl):
                u = sl.unit(OFF_OUT)
                if not u:
                    return
                wait_bank(pe, TEN_O, sl, "ott")
                wait(pe, "oev", at(2, u, 2))
                for qt in range(TPS):
                    for y in range(2):
                        a = (2 * qt + y) * P
                        last = pe.transpose(psO[:, a:a + P], oT[:, y, P * qt:P * qt + P], Fc("ident"))
                last.then_inc(S["ott"], 1)

            def ob(sl):
                u = sl.unit(OFF_OUT)
                if not u:
                    return
                wait_bank(pe, TEN_O, sl, "ob")
                wait(pe, "norm", at(1, u, 1))
                for qt in range(TPS):
                    last = pe.transpose(psO[:, P * qt:P * qt + P],
                                        on[:, u.b % 2, H * qt:H * qt + H, :].rearrange("p h d -> p (h d)"), Fc("ident"))
                last.then_inc(S["ob"], 1)

            def outproj(sl):
                u = sl.unit(OFF_OUT)
                if not u:
                    return
                wait(pe, "obev", at(1, u, 1))
                wait_bank(pe, TEN_O, sl, "op")
                for qt in range(TPS):
                    last = mm(psO[:, P * qt:P * qt + P], onT[:, P * qt:P * qt + P], W(u.layer, WO),
                              start=True, stop=True)
                last.then_inc(S["op"], 1)

            def xt(sl):
                u = sl.unit(OFF_LOAD)
                if not u:
                    return
                wait_bank(pe, TEN_M, sl, "xt")
                if u.layer == 1:
                    wait(pe, "lnout2", at(2, u, 2, NSEQ))
                else:
                    wait(pe, "lnout", at(2, u, 2))
                for i in range(TPS):
                    src = xn2[:, u.b % 2, i, :] if u.layer == 1 else xn[:, u.b, i, :]
                    last = pe.transpose(psM[:, P * i:P * i + P], src, Fc("ident"))
                last.then_inc(S["xt"], 1)

            def x_of(u):
                return cT[:, u.b % 2, :] if u.layer == 1 else xT[:, u.b % 2, :]

            def project(sl, name):
                u = sl.unit(OFF_SPREAD if name == "v" else OFF_PROJ)
                if not u:
                    return
                if name == "qk":
                    if u.layer == 1:
                        wait(pe, "conv", at(1, u, 1, NSEQ))
                    else:
                        wait(pe, "xtev", at(1, u, 1))
                wait_bank(pe, TEN_M, sl, name)
                x = x_of(u)
                if name == "v":
                    for i in range(TPS):
                        last = mm(psM[:, P * i:P * i + P], x[:, P * i:P * i + P], W(u.layer, WV), start=True, stop=True)
                else:
                    for i, w in enumerate((WQ, WK)):
                        last = mm(psM[:, SEQ * i:SEQ * i + SEQ], W(u.layer, w), x, start=True, stop=True)
                last.then_inc(S[name], 1)

            def sumq(sl):
                u = sl.unit(OFF_PROJ, (0,))
                if not u:
                    return
                wait_bank(pe, TEN_M, sl, "sp")
                wait(pe, "qkev", at(2, u, 2))
                for i in range(TPS):
                    last = mm(psM[:, H * i:H * i + H], qkf[:, 0, P * i:P * i + P], Fc("heads"), start=True, stop=True)
                last.then_inc(S["sp"], 1)

            def mt(sl):
                u = sl.unit(OFF_MAX)
                if not u:
                    return
                wait_bank(pe, TEN_M, sl, "mt")
                wait(pe, "mlo", at(1, u, 1))
                for i in range(TPS):
                    last = pe.transpose(psM[:, :].bitcast(bf16)[:, P * i:P * i + P],
                                        mparts[:, i, :, :].rearrange("p a h -> p (a h)"), Bc("ident"))
                last.then_inc(S["mt"], 1)

            def route(sl, name):
                u = sl.unit(OFF_ROUTE if name == "hT" else OFF_LOGIT, (1, 2))
                if not u:
                    return
                wait_bank(pe, TEN_M, sl, name)
                if name == "hT":
                    wait(pe, "hfin", at(1, u, 1, NSEQ))
                    for i in range(TPS):
                        last = pe.transpose(psM[:, P * i:P * i + P], hrow[:, u.b % 2, i, 0:C], Fc("ident"))
                    last.then_inc(S["hT"], 1)
                else:
                    wait(pe, "hTev", at(1, u, 1, NSEQ))
                    w = wr[:, 0:E0] if u.layer == 1 else wr[:, E0:E0 + E1]
                    n = w.shape[-1]
                    for i in range(TPS):
                        last = mm(psM[:, n * i:n * i + n], hT[:, P * i:P * i + P], w, start=True, stop=True)
                    last.then_inc(S["lg"], 1)

            def rank(sl):
                u = sl.unit(OFF_LOGIT, (1, 2))
                if not u:
                    return
                E = (E0, E1)[u.layer - 1]
                wait_bank(pe, TEN_M, sl, "rank")
                wait(pe, "routing", at(NROUTE, u, 5, NSEQ))
                r = psM[:, 0:TPS * E].rearrange("p (t e) -> p t e", e=E)
                mm(r, Bc("before"), oh[:, :, 0:E], start=True, stop=False, skip_group_check=True)
                mm(r, Bc("ones"), acc[:, 0:E].unsqueeze(1).to_broadcast([P, TPS, E]), start=False, stop=False,
                   skip_group_check=True)
                mm(r[:, 1, :], Bc("ones"), oh[:, 0, 0:E], start=False, stop=True,
                   skip_group_check=True).then_inc(S["rank"], 1)

            def step(sl):
                score(sl, 0)
                scoreT(sl, 0)
                pv(sl, 3)
                project(sl, "v")
                score(sl, 1)
                scoreT(sl, 1)
                ott(sl)
                route(sl, "lg")
                score(sl, 2)
                scoreT(sl, 2)
                project(sl, "qk")
                score(sl, 3)
                scoreT(sl, 3)
                pv(sl, 0)
                sumq(sl)
                score(sl, 4)
                scoreT(sl, 4)
                pv(sl, 1)
                rank(sl)
                score(sl, 5)
                scoreT(sl, 5)
                ob(sl)
                mt(sl)
                score(sl, 6)
                scoreT(sl, 6)
                outproj(sl)
                route(sl, "hT")
                score(sl, 7)
                scoreT(sl, 7)
                pv(sl, 2)
                xt(sl)

            def mix(i):
                ntl, E, F = ((NTILE0, E0, F0), (NTILE1, E1, F1))[i]
                m = {k: v[i] for k, v in M.items()}
                pe.wait_ge(S["routing"], NROUTE * NSEQ * (i + 1))
                mm(psT[1][:, 0:E], Bc("ones"), acc[:, 0:E], start=True, stop=True).then_inc(m["count"], 1)
                pe.wait_ge(m["te"], 1)
                if i == 0:
                    pe.wait_ge(S["wload"], NLATE)
                else:
                    pe.wait_ge(S["dn1load"], 32)
                nk = F // P

                def turn(j, it):
                    jx = j + 4 * it
                    if j >= 1:
                        pe.wait_ge(m["htev"], jx)
                    pe.wait_ge(m["xf"], jx + 1)
                    pe.transpose(psM[:, 0:P], xf[:, j % 2, :], Fc("ident")).then_inc(m["ht"], 1)

                def upward(j, it):
                    jx = j + 4 * it
                    e = pe.value_load(tei[i][0:1, bass.ds(jx, 1)], min_val=0, max_val=E - 1)
                    pe.wait_ge(m["htev"], jx + 1)
                    if j >= 2:
                        pe.wait_ge(m["act"], jx - 1)
                    for n in range(2 if i == 0 else 1):
                        w = F0 if i == 0 else F1
                        last = mm(psT[j % 2][:, 512 * n:512 * n + w], xfT[:, j % 2, :],
                                  up[i][:, bass.ds(e * (2 * F0 if i == 0 else F1) + n * F0, w)], start=True, stop=True)
                    last.then_inc(m["up"], 1)

                def turn_act(j, it):
                    jx = j + 4 * it
                    pe.wait_ge(m["act"], jx + 1)
                    if j >= 2:
                        pe.wait_ge(m["atev"], jx - 1)
                    for n in range(nk):
                        last = pe.transpose(psS[:, 512 * (j % 2) + P * n:512 * (j % 2) + P * n + P],
                                            mixact[:, j % 2, P * n:P * n + P], Fc("ident"))
                    last.then_inc(m["at"], 1)

                def downward(j, it):
                    jx = j + 4 * it
                    e = pe.value_load(tei[i][0:1, bass.ds(jx, 1)], min_val=0, max_val=E - 1)
                    pe.wait_ge(m["atev"], jx + 1)
                    if j >= 1:
                        pe.wait_ge(m["yev"], jx)
                    for n in range(nk):
                        last = mm(psO[:, 0:C], actT[:, j % 2, P * n:P * n + P],
                                  dn[i][:, bass.ds(e * F + n * C, C)], start=(n == 0), stop=(n == nk - 1))
                    last.then_inc(m["prod"], 1)

                def tile(j, it):
                    if j + 1 < ntl:
                        turn(j + 1, it)
                    if j < ntl:
                        upward(j, it)
                    if 1 <= j <= ntl:
                        turn_act(j - 1, it)
                    if j >= 2:
                        downward(j - 2, it)

                turn(0, 0)
                for j in range(4):
                    tile(j, 0)
                with pe.Fori(0, (ntl - 8) // 4) as it:
                    for j in range(4):
                        tile(4 + j, it)
                for j in range(ntl - 4, ntl + 2):
                    tile(j, 0)

            pe.wait_ge(S["const"], NCONST)
            slots(pe, step, 0, 2 * NSEQ)
            mix(0)
            slots(pe, step, 2 * NSEQ, 3 * NSEQ)
            mix(1)

        @block.scalar
        def _(act_e):
            act = act_e
            actv = act.activation

            def exps(sl, g):
                u = sl.unit(OFF_ATT)
                if not u:
                    return
                wait(act, "tready", at(NSTEP, u, g + 1))
                wait(act, "pv", at(GROUPS, u, g // 2 - 1))
                src, dst = psT[g % 2][:, 0:SW], pr[:, g % 4, :]
                if u.layer == 0:
                    src = psT[g % 2][:, :].rearrange("p (b n) -> p b n", b=2)[:, :, 0:HPS * BAND]
                    dst = dst.rearrange("p (b n) -> p b n", b=2)
                actv(dst, src, ACT.Exp).then_inc(S["exp"], 1)

            def oev(sl, y):
                u = sl.unit((OFF_ATT, OFF_OUT)[y])
                if not u:
                    return
                wait(act, "pv", at(GROUPS, u, 2 * y + 2))
                wait(act, "ott", at(1, u, 0))
                actv(oT[:, y, :], psO[:, 0:SEQ], ACT.Copy).then_inc(S["oev"], 1)

            def xtev(sl):
                u = sl.unit(OFF_PROJ)
                if not u:
                    return
                wait(act, "xt", at(1, u, 1))
                wait(act, "v", at(1, u, -1))
                if u.layer == 1:
                    actv(xT[:, u.b % 2, :], psM[:, 0:SEQ], ACT.Identity, bias=cols[:, LN1B:LN1B + 1],
                         scale=cols[:, LN1W:LN1W + 1]).then_inc(S["xtev"], 1)
                else:
                    actv(xT[:, u.b % 2, :], psM[:, 0:SEQ], ACT.Copy).then_inc(S["xtev"], 1)

            def qkev(sl):
                u = sl.unit(OFF_PROJ, (0, 2))
                if not u:
                    return
                wait(act, "qk", at(1, u, 1))
                wait(act, "lo", at(1, u, 0))
                if u.layer == 0:
                    wait(act, "sp", at(1, u, 0))
                bq, bk = (BQ0, BK0) if u.layer == 0 else (BQ2S, BK2)
                actv(qkf[:, 0, :], psM[:, 0:SEQ], ACT.Identity, bias=cols[:, bq:bq + 1],
                     scale=1.0 if u.layer == 0 else float(D) ** -0.5).then_inc(S["qkev"], 1)
                actv(qkf[:, 1, :], psM[:, SEQ:2 * SEQ], ACT.Identity, bias=cols[:, bk:bk + 1],
                     scale=1.0).then_inc(S["qkev"], 1)

            def part(sl, n):
                u = sl.unit(OFF_PROJ)
                if not u:
                    return
                if n == 0:
                    if u.layer == 1:
                        wait(act, "ropeadd", at(1, u, 1, NSEQ))
                    else:
                        wait(act, "qkev", at(2, u, 2))
                    moved(act, "rep", u, 1, n=NREP)
                else:
                    wait(act, "resid", at(1, u, 1))
                actv(parts[:, n], qkf[:, :, :], ACT.Copy).then_inc(S[("hi", "mid")[n]], 1)

            def mtev(sl):
                u = sl.unit(OFF_MAX)
                if not u:
                    return
                wait(act, "mt", at(1, u, 1))
                moved(act, "mrow", u, 1)
                actv(mT[:, :], psM[:, :].bitcast(bf16)[0:PARTS * H, 0:SEQ], ACT.Copy).then_inc(S["mtev"], 1)

            def v_ev(sl):
                u = sl.unit(OFF_SPREAD, (1,))
                if not u:
                    return
                wait(act, "v", at(1, u, 1))
                wait(act, "pv", at(GROUPS, u, GROUPS - GROUPS * NBUF))
                actv(v_of(u), psM[:, 0:TPS * C].rearrange("p (a h d) -> p a h d", a=TPS, h=H),
                     ACT.Copy).then_inc(S["vev"], 1)

            def ln3_apply(sl):
                u = sl.unit(OFF_ROUTE, (1, 2))
                if not u:
                    return
                b = u.b % 2
                wait(act, "shifts3", at(1, u, 1, NSEQ))
                moved(act, "scat", u, 2, NSEQ, n=TPS)
                wait(act, "hT", at(1, u, -1, NSEQ))
                if u.layer == 1:
                    normal(hrow[:, b, :, 0:C], zb[:, b], rstd3[:, b], rstd3[:, b], "hout")
                else:
                    for i in range(TPS):
                        x = actv(hrow[:, b, i, 0:C], zb[:, b, i, :], ACT.Identity, bias=rstd3[:, b, i, 1:2],
                                 scale=rstd3[:, b, i, 0:1])
                    x.then_inc(S["hfin"], 1)

            def normal(o, x, m, r, done):
                for i in range(TPS):
                    actv(o[:, i, :], x[:, i, :], ACT.Identity, bias=m[:, i, 1:2], scale=r[:, i, 0:1]).then_inc(S[done], 1)

            def ln_apply(sl):
                u = sl.unit(OFF_LOAD)
                if not u:
                    return
                wait(act, "shifts", at(1, u, 1))
                if u.layer == 1 and u.rep >= NSEQ + NBUF:
                    moved(act, "ystore", u, 2, NSEQ)
                else:
                    wait(act, "xt", at(1, u, 1 - NBUF))
                normal(xn[:, u.b], xin[:, u.b], rstd[:, u.b], rstd[:, u.b], "lnout")

            def ln_again(sl):
                u = sl.unit(OFF_LOAD, (1,))
                if not u:
                    return
                wait(act, "shifts2", at(1, u, 1, NSEQ))
                wait(act, "xt", at(1, u, -1))
                normal(xn2[:, u.b % 2], xn[:, u.b], rstd2[:, u.b], rstd2[:, u.b], "lnout2")

            def epads(sl):
                u = sl.unit(OFF_MAX, (0,))
                if not u:
                    return
                wait(act, "earg", at(1, u, 1))
                wait(act, "pnum", at(1, u, 1 - NBUF))
                actv(epad[:, u.b, :, :].rearrange("p q (g j s) -> p (q g) s j", s=PACK, j=4),
                     earg[:, u.b % 2, :, :].rearrange("p q (g s j) -> p (q g) s j", s=PACK, j=4), ACT.Exp).then_inc(S["epad"], 1)

            def obev(sl):
                u = sl.unit(OFF_OUT)
                if not u:
                    return
                wait(act, "ob", at(1, u, 1))
                wait(act, "op", at(1, u, 0))
                actv(onT[:, :], psO[:, 0:SEQ], ACT.Copy).then_inc(S["obev"], 1)

            def hTev(sl):
                u = sl.unit(OFF_ROUTE, (1, 2))
                if not u:
                    return
                wait(act, "hT", at(1, u, 1, NSEQ))
                wait(act, "lg", at(1, u, 0, NSEQ))
                actv(hT[:, :], psM[:, 0:SEQ], ACT.Copy).then_inc(S["hTev"], 1)

            def bias_rows():
                act.wait_ge(M["yev"][0], NTILE0)
                r, r1 = ROW_BIAS, ROW_BIAS + PARTS
                tq, tk = (t["trig"][w].unsqueeze(1).to_broadcast([ROWS, NBUF, H, SEQ]) for w in range(2))
                for dst, src in ((QKall[r:r + ROWS, 0:NBUF, :, :], tq),
                                 (QKall[r:r + ROWS, NBUF:, 0:8, :], tk[:, :, 0:8, :]),
                                 (QKall[r1:r + ROWS, NBUF:, 8:H, :], tk[PARTS:ROWS, :, 8:H, :])):
                    act.dma_start(dst, src).then_inc(S["posd"], 16)
                ones_rows(act, 2)
                act.wait_ge(S["posb"], 1)
                for b in range(NBUF):
                    act.dma_start(KA[b][r:r1, 8:H, :], poscb).then_inc(S["posd"], 16)

            def step(sl):
                if sl.rep in LATER:
                    act.dma_start(*LATER[sl.rep]).then_inc(S["wload"], 16)
                xtev(sl)
                exps(sl, 0)
                oev(sl, 1)
                v_ev(sl)
                exps(sl, 1)
                epads(sl)
                exps(sl, 2)
                qkev(sl)
                exps(sl, 3)
                ln3_apply(sl)
                ln_apply(sl)
                exps(sl, 4)
                oev(sl, 0)
                exps(sl, 5)
                obev(sl)
                mtev(sl)
                part(sl, 0)
                exps(sl, 6)
                ln_again(sl)
                hTev(sl)
                exps(sl, 7)
                part(sl, 1)
                if sl.first == 2 * NSEQ:
                    if sl.rep == sl.first - OFF_LOAD:
                        bias_rows()
                    if sl.rep == sl.first:
                        for dst, src in mix1_parts:
                            act.dma_start(dst, src).then_inc(S["dn1load"], 16)

            def mix(i):
                ntl, F = ((NTILE0, F0), (NTILE1, F1))[i]
                m = {k: v[i] for k, v in M.items()}

                def rows_turned(j, it):
                    jx = j + 4 * it
                    act.wait_ge(m["ht"], jx + 1)
                    if j >= 2:
                        act.wait_ge(m["up"], jx - 1)
                    actv(xfT[:, j % 2, :], psM[:, 0:P], ACT.Copy).then_inc(m["htev"], 1)

                def nonlin(j, it):
                    jx = j + 4 * it
                    if i == 0:
                        act.wait_ge(m["up"], jx + 1)
                        if j >= 2:
                            act.wait_ge(m["act"], jx - 1)
                        actv(gate[:, j % 2, 0:F], psT[j % 2][:, 0:F], ACT.Silu).then_inc(m["actg"], 1)
                    else:
                        act.wait_ge(m["actg"], jx + 1)
                        if j >= 2:
                            act.wait_ge(m["at"], jx - 1)
                        actv(mixact[:, j % 2, 0:F], gate[:, j % 2, 0:F], ACT.Gelu).then_inc(m["act"], 1)

                def fetch(j, it):
                    jx = j + 4 * it
                    act.wait_ge(MD["load"][i][j % 4], 16 * (j // 4 + 1 + it))
                    if j >= 2:
                        act.wait_ge(m["ht"], jx - 1)
                    actv(xf[:, j % 2, :], hx[:, bass.ds(jx, 1), 0:C].rearrange("p t c -> p (t c)"),
                         ACT.Copy).then_inc(m["xf"], 1)

                def tile(j, it):
                    if j + 2 < ntl:
                        fetch(j + 2, it)
                    if j + 1 < ntl:
                        rows_turned(j + 1, it)
                    nonlin(j, it)

                fetch(0, 0)
                fetch(1, 0)
                rows_turned(0, 0)
                for j in range(4):
                    tile(j, 0)
                with act.Fori(0, (ntl - 8) // 4) as it:
                    for j in range(4):
                        tile(4 + j, it)
                for j in range(ntl - 4, ntl):
                    tile(j, 0)

            act.wait_ge(S["const"], NCONST)
            act.wait_ge(S["setup"], 4)
            slots(act, step, 0, 2 * NSEQ)
            mix(0)
            slots(act, step, 2 * NSEQ, 3 * NSEQ)
            mix(1)

        @block.vector
        def _(dve):
            tt, ts = dve.tensor_tensor, dve.tensor_scalar

            def reduce(sl, g):
                u = sl.unit(OFF_SCORE)
                if not u:
                    return
                if g == 0:
                    wait(dve, "nmax", at(2, u, -2))
                for qt in (1, 0):
                    wait(dve, "sready", at(2 * NSTEP, u, 2 * g + 2 - qt))
                    if u.layer == 0:
                        src, a, n = psS[:, 512 * (1 - qt):512 * (1 - qt) + HPS * BAND].rearrange(
                            "p (h n) -> p h n", h=HPS), HPS * qt, HPS
                    elif qt == 1:
                        src, a, n = psS[:, 0:512].rearrange("p (b n) -> p b n", n=P), 0, 2 * HPS
                    else:
                        src, a, n = psS[:, 512:512 + HPS * P].rearrange("p (b n) -> p b n", n=P), 2 * HPS, HPS
                    dve.tensor_reduce(nred[:, u.b % 2, g, a:a + n], src, op=ALU.max, axis=AX.X,
                                      negate=True).then_inc(S["red"], 1)

            def nmaxs(sl):
                u = sl.unit(OFF_MAX)
                if not u:
                    return
                b = u.b % 2
                wait(dve, "red", at(2 * NSTEP, u, 2 * NSTEP))
                wait(dve, "mres", at(1, u, -1))
                r = nred[:, b, :, :]
                o = nmax[:, b, :, :].rearrange("p q (s h) -> p q s h", h=HPS)
                if u.layer == 0:
                    wait(dve, "spev", at(1, u, 1))
                    sp4 = spad[:, u.b, :, :].rearrange("p q (s h) -> p q s h", h=HPS)
                    for q in range(TPS):
                        tt(o[:, q, :, :], r[:, :, HPS * q:HPS * q + HPS], sp4[:, q, :, :], ALU.min).then_inc(S["nmax"], 1)
                    wait(dve, "nmax", at(2, u, 2))
                    wait(dve, "epad", at(1, u, -1))
                    tt(earg[:, b, :, :], nmax[:, b, :, :], spad[:, u.b, :, :], ALU.subtract).then_inc(S["earg"], 1)
                else:
                    r2 = r[:, :, 0:4].rearrange("p s (h k) -> p s h k", k=2)
                    tt(o[:, 1, :, :], r2[:, :, :, 0], r2[:, :, :, 1], ALU.min).then_inc(S["nmax"], 1)
                    dve.tensor_copy(o[:, 0, :, :], r[:, :, 4:6]).then_inc(S["nmax"], 1)

            def stats(x, st, s1):
                for i in range(TPS):
                    dve.bn_stats(st[:, i, :], x[:, i, :]).then_inc(S[s1], 1)

            def aggr(st, m, s2):
                for i in range(TPS):
                    dve.bn_aggr(m[:, i, :], st[:, i, :]).then_inc(S[s2], 1)

            def normal(o, x, m, r, done):
                for i in range(TPS):
                    ts(o[:, i, :], x[:, i, :], m[:, i, 0:1], r[:, i, 0:1], ALU.subtract, ALU.mult).then_inc(S[done], 1)

            def ln_stats(sl):
                u = sl.unit(OFF_LOAD)
                if not u:
                    return
                moved(dve, "xin", u)
                stats(xin[:, u.b], stat[:, u.b], "stats")

            def aggregate(sl, g, off, layers, name, st, m, first):
                u = sl.unit(off, layers)
                if u:
                    wait(dve, name, at(2, u, 2, first))
                reduce(sl, g)
                if u:
                    b = u.b if st is not stat3 else u.b % 2
                    aggr(st[:, b], m[:, b], "mvs" + name[5:])

            def ln_stats2(sl):
                u = sl.unit(OFF_LOAD, (1,))
                if not u:
                    return
                wait(dve, "lnout", at(2, u, 2))
                stats(xn[:, u.b], stat2[:, u.b], "stats2")

            def ln3_stats(sl):
                u = sl.unit(OFF_ROUTE, (1, 2))
                if not u:
                    return
                b = u.b % 2
                wait(dve, "zout", at(1, u, 1))
                stats(zb[:, b], stat3[:, b], "stats3")

            def rope_cos(sl):
                u = sl.unit(OFF_PROJ, (1,))
                if not u:
                    return
                wait(dve, "qk", at(1, u, 1))
                wait(dve, "lo", at(1, u, 0))
                tt(qkf[:, :, :], psM[:, :].rearrange("p (a t) -> p a t", a=2),
                   cf[:, CF["cosq"][0]:CF["cosk"][1]].rearrange("p (a t) -> p a t", a=2), ALU.mult).then_inc(S["qkev"], 2)

            def rope_sin(sl, half):
                u = sl.unit(OFF_PROJ, (1,))
                if not u:
                    return
                if half == 0:
                    wait(dve, "qk", at(1, u, 1))
                    wait(dve, "ropeadd", at(1, u, 0, NSEQ))
                a, b = (0, P // 2) if half == 0 else (P // 2, 0)
                x = tt(qks[a:a + P // 2, :, :], psM[b:b + P // 2, :].rearrange("p (a t) -> p a t", a=2),
                       cf[b:b + P // 2, CF["sinq"][0]:CF["sink"][1]].rearrange("p (a t) -> p a t", a=2), ALU.mult)
                if half == 1:
                    x.then_inc(S["rotev"], 1)

            def sp_ev(sl):
                u = sl.unit(OFF_PROJ, (0,))
                if not u:
                    return
                wait(dve, "sp", at(1, u, 1))
                tt(spad[:, u.b, :, :], psM[:, 0:TPS * H].rearrange("p (q h) -> p q h", q=TPS),
                   Fc("padfar").unsqueeze(2).to_broadcast([P, TPS, H]), ALU.add).then_inc(S["spev"], 1)

            def v_ev(sl):
                u = sl.unit(OFF_SPREAD, (0, 2))
                if not u:
                    return
                wait(dve, "v", at(1, u, 1))
                wait(dve, "pv", at(GROUPS, u, GROUPS - GROUPS * NBUF))
                bias = rows[:, BV0 if u.layer == 0 else BV2, :].rearrange("p (h d) -> p h d", h=H)
                tt(v_of(u), psM[:, 0:TPS * C].rearrange("p (a h d) -> p a h d", a=TPS, h=H),
                   bias.unsqueeze(1).to_broadcast([P, TPS, H, D]), ALU.add).then_inc(S["vev"], 1)

            def norm(sl):
                u = sl.unit(OFF_OUT)
                if not u:
                    return
                b = u.b % 2
                wait(dve, "ott", at(1, u, 1))
                o = psO[:, :].rearrange("p (n c) -> p n c", c=HALF)
                num, dn_, r = o[:, :, 0:D], o[:, :, D], rden[:, b, :]
                if u.layer == 0:
                    wait(dve, "epad64", at(1, u, 1))
                    e = epad[:, u.b, :, :].rearrange("p q h -> p (q h)")
                    wait(dve, "norm", at(1, u, 0))
                    tt(den[:, b, :], dn_, e, ALU.add).then_inc(S["den"], 1)
                    tt(pnum[:, :, :], num, e.unsqueeze(2).to_broadcast([P, TPS * H, D]), ALU.subtract).then_inc(S["pnum"], 1)
                    wait(dve, "den", at(1, u, 1))
                    dn_, num = den[:, b, :], pnum[:, :, :]
                dve.reciprocal(r, dn_).then_inc(S["rden"], 1)
                wait(dve, "rden", at(1, u, 1))
                if u.layer == 0:
                    wait(dve, "pnum", at(1, u, 1))
                wait(dve, "ob", at(1, u, -1))
                tt(on[:, b, :, :], num, r.unsqueeze(2).to_broadcast([P, TPS * H, D]), ALU.mult).then_inc(S["norm"], 1)

            def residual(sl):
                u = sl.unit(OFF_OUT)
                if not u:
                    return
                b = u.b % 2
                wait(dve, "op", at(1, u, 1))
                if u.layer == 1:
                    moved(dve, "yresdma", u, 0, NSEQ)
                    r = yres
                else:
                    wait(dve, "rbias", (u.n - (0 if u.layer == 0 else NSEQ)) + 1)
                    r = xres
                if u.rep < NSEQ + 2:
                    moved(dve, "xstore", u, 2)
                else:
                    wait(dve, "xz", at(1, u, -1, NSEQ))
                    wait(dve, "hfin", at(1, u, -1, NSEQ))
                tt(zb[:, b, :, :], psO[:, 0:TPS * C].rearrange("p (q c) -> p q c", q=TPS), r[:, b, :, :],
                   ALU.add).then_inc(S["zout"], 1)

            def lg_ev(sl):
                u = sl.unit(OFF_LOGIT, (1, 2))
                if not u:
                    return
                E = (E0, E1)[u.layer - 1]
                wait(dve, "lg", at(1, u, 1, NSEQ))
                dst = lg[:, :, 0:E]
                src = psM[:, 0:TPS * E].rearrange("p (t e) -> p t e", e=E)
                if u.layer == 1:
                    dve.tensor_copy(dst, src).then_inc(S["lgev"], 1)
                else:
                    tt(dst, src, br[:, :].unsqueeze(1).to_broadcast([P, TPS, E]), ALU.add).then_inc(S["lgev"], 1)

            def routing(sl, n):
                u = sl.unit(OFF_LOGIT, (1, 2))
                if not u:
                    return
                E, b = (E0, E1)[u.layer - 1], u.b % 2
                wide = [P, TPS, E]
                eid = Fc("eid")[:, 0:E].unsqueeze(1).to_broadcast(wide)
                L, o = lg[:, :, 0:E], oh[:, :, 0:E]
                if n == 1:
                    wait(dve, "lgev", at(1, u, 1, NSEQ))
                elif n == 6:
                    wait(dve, "rank", at(1, u, 1, NSEQ))
                elif n == 8:
                    wait(dve, "rankev", at(1, u, 1, NSEQ))
                if n > 1:
                    wait(dve, "routing", at(NROUTE, u, n - 1, NSEQ))
                if n == 1:
                    x = dve.tensor_reduce(top[:, :], L, op=ALU.max, axis=AX.X)
                elif n == 2:
                    x = tt(eq[:, :, 0:E], L, top[:, :].unsqueeze(2).to_broadcast(wide), ALU.is_equal)
                elif n == 3:
                    x = tt(eqi[:, :, 0:E], eq[:, :, 0:E], eid, ALU.mult)
                elif n == 4:
                    x = dve.tensor_reduce(pick[:, :], eqi[:, :, 0:E], op=ALU.min, axis=AX.X)
                elif n == 5:
                    x = tt(o, eid, pick[:, :].unsqueeze(2).to_broadcast(wide), ALU.is_equal)
                elif n in (6, 7):
                    x = tt(acc[:, 0:E], acc[:, 0:E], oh[:, n - 6, 0:E], ALU.add)
                elif n == 8:
                    x = tt(rk2[:, :, 0:E], rk[:, :, 0:E], o, ALU.mult)
                elif n == 9:
                    x = dve.tensor_reduce(destf[:, :], rk2[:, :, 0:E], op=ALU.add, axis=AX.X)
                else:
                    x = dve.tensor_copy(dest[:, b, :], destf[:, :])
                x.then_inc(S["routing"], 1)

            def rank_ev(sl):
                u = sl.unit(OFF_LOGIT, (1, 2))
                if not u:
                    return
                E = (E0, E1)[u.layer - 1]
                wait(dve, "rank", at(1, u, 1, NSEQ))
                tt(rk[:, :, 0:E], psM[:, 0:TPS * E].rearrange("p (t e) -> p t e", e=E),
                   Fc("region")[:, 0:E].unsqueeze(1).to_broadcast([P, TPS, E]), ALU.add).then_inc(S["rankev"], 1)

            def step(sl):
                nmaxs(sl)
                reduce(sl, 0)
                ln3_stats(sl)
                ln_stats(sl)
                v_ev(sl)
                aggregate(sl, 1, OFF_ROUTE, (1, 2), "stats3", stat3, mv3, NSEQ)
                norm(sl)
                lg_ev(sl)
                aggregate(sl, 2, OFF_LOAD, (0, 1, 2), "stats", stat, mv, 0)
                routing(sl, 1)
                rope_cos(sl)
                routing(sl, 2)
                reduce(sl, 3)
                routing(sl, 3)
                rope_sin(sl, 0)
                routing(sl, 4)
                rope_sin(sl, 1)
                sp_ev(sl)
                routing(sl, 5)
                reduce(sl, 4)
                ln_stats2(sl)
                rank_ev(sl)
                aggregate(sl, 5, OFF_LOAD, (1,), "stats2", stat2, mv2, NSEQ)
                routing(sl, 6)
                reduce(sl, 6)
                routing(sl, 7)
                residual(sl)
                routing(sl, 8)
                reduce(sl, 7)
                routing(sl, 9)
                routing(sl, 10)

            def mix(i):
                ntl, E, F = ((NTILE0, E0, F0), (NTILE1, E1, F1))[i]
                m = {k: v[i] for k, v in M.items()}
                made = [0]

                def link(ins):
                    made[0] += 1
                    ins.then_inc(m["dve"], 1)
                    dve.wait_ge(m["dve"], made[0])

                R = Fc("region")[:, 0:E]
                dve.wait_ge(m["count"], 1)
                link(dve.tensor_copy(cntf[:, 0:E], psT[1][:, 0:E]))
                link(ts(padi[:, 0:E], cntf[:, 0:E], float(P - 1), None, ALU.add))
                link(ts(padi2[:, 0:E], padi[:, 0:E], 7, 7, ALU.logical_shift_right, ALU.logical_shift_left))
                link(dve.tensor_copy(padf[:, 0:E], padi2[:, 0:E]))
                q = [fill[:, a, 0:E] for a in range(4)]
                link(ts(q[0], cntf[:, 0:E], Fc("row"), None, ALU.add))
                link(tt(q[1], q[0], padf[:, 0:E], ALU.is_ge))
                link(ts(q[2], q[1], float(NOWHERE), None, ALU.mult))
                link(tt(q[3], q[0], q[2], ALU.add))
                tt(filld[i][:, :], q[3], R, ALU.add).then_inc(m["fill"], 1)
                link(dve.memset(acc[:, :], 0.0))
                link(dve.memset(base[:, 0:1], 0.0))
                for e in range(E):
                    link(tt(base[:, e + 1:e + 2], base[:, e:e + 1], padf[:, e:e + 1], ALU.add))
                start = cf[0:1, CF["start"][0]:CF["start"][0] + ntl]
                wide = [1, ntl, E - 1]
                g1 = ge[:, 0:ntl, 0:E - 1]
                link(tt(g1, start.unsqueeze(2).to_broadcast(wide), base[0:1, 1:E].unsqueeze(1).to_broadcast(wide), ALU.is_ge))
                link(dve.tensor_reduce(tef[:, 0:ntl], g1, op=ALU.add, axis=AX.X))
                dve.tensor_copy(tei[i][:, :], tef[:, 0:ntl]).then_inc(m["te"], 1)
                link(ts(short[:, 0:E - 1], padf[0:1, 0:E - 1], -1.0, float(REGION), ALU.mult, ALU.add))
                link(tt(g1, g1, short[:, 0:E - 1].unsqueeze(1).to_broadcast(wide), ALU.mult))
                w = [rowf[:, a, 0:ntl] for a in range(4)]
                link(dve.tensor_reduce(w[0], g1, op=ALU.add, axis=AX.X))
                link(tt(w[1], w[0], start, ALU.add))
                link(ts(w[0], w[1], -1.0, float(E * REGION), ALU.mult, ALU.add))
                link(ts(w[2], start, base[0:1, E:E + 1], None, ALU.is_ge))
                link(tt(w[3], w[0], w[2], ALU.mult))
                tt(rowi[i][:, :], w[1], w[3], ALU.add).then_inc(m["rows"], 1)
                if i == 1:
                    dve.wait_ge(m["te"], 1)
                    dve.wait_ge(m["bias"], 32)
                def where_to(j, it, n):
                    jx = j + 4 * it
                    where = hx[:, bass.ds(jx, 1), 2 * C]
                    if n == 0:
                        dve.wait_ge(MD["load"][i][j % 4], 16 * (j // 4 + 1 + it))
                        ts(idt[:, 0, bass.ds(jx, 1)], where, 0.0, Fc("row"), ALU.is_equal, ALU.mult).then_inc(m["idt"], 1)
                        return
                    dve.wait_ge(m["idt"], 2 * jx + n)
                    if n == 1:
                        tt(idt[:, 1, bass.ds(jx, 1)], idt[:, 0, bass.ds(jx, 1)], where, ALU.add).then_inc(m["idt"], 1)
                    else:
                        ts(ids[i][:, bass.ds(jx, 1)], idt[:, 1, bass.ds(jx, 1)], float(OUTSIDE), None,
                           ALU.add).then_inc(m["ids"], 1)

                def hidden(j, it):
                    jx = j + 4 * it
                    if i == 0:
                        dve.wait_ge(m["actg"], jx + 1)
                        if j >= 2:
                            dve.wait_ge(m["at"], jx - 1)
                        tt(mixact[:, j % 2, 0:F], gate[:, j % 2, 0:F], psT[j % 2][:, 512:512 + F],
                           ALU.mult).then_inc(m["act"], 1)
                    else:
                        e = dve.value_load(tei[i][0:1, bass.ds(jx, 1)], min_val=0, max_val=E - 1)
                        dve.wait_ge(m["up"], jx + 1)
                        if j >= 2:
                            dve.wait_ge(m["act"], jx - 1)
                        tt(gate[:, j % 2, 0:F], psT[j % 2][:, 0:F], b1r[:, bass.ds(e * F, F)],
                           ALU.add).then_inc(m["actg"], 1)
                    where_to(j, it, 0)
                    if j >= 4:
                        dve.wait_ge(MD["store"][i][j % 4], 16 * (j // 4 + it))
                    if i == 1:
                        tt(yt[:, j % 4, :], hx[:, bass.ds(jx, 1), C:2 * C].rearrange("p t c -> p (t c)"),
                           b2r[:, bass.ds(e * C, C)], ALU.add).then_inc(m["ready"], 1)

                def turned(j, it):
                    jx = j + 4 * it
                    dve.wait_ge(m["at"], jx + 1)
                    if j >= 2:
                        dve.wait_ge(m["prod"], jx - 1)
                    dve.tensor_copy(actT[:, j % 2, 0:F], psS[:, 512 * (j % 2):512 * (j % 2) + F]).then_inc(m["atev"], 1)

                def result(j, it):
                    jx = j + 4 * it
                    if i == 0:
                        r = hx[:, bass.ds(jx, 1), C:2 * C].rearrange("p t c -> p (t c)")
                    else:
                        r = yt[:, j % 4, :]
                        dve.wait_ge(m["ready"], jx + 1)
                    dve.wait_ge(m["prod"], jx + 1)
                    tt(yt[:, j % 4, :], psO[:, 0:C], r, ALU.add).then_inc(m["yev"], 1)

                def tile(j, it):
                    if j < ntl:
                        hidden(j, it)
                    if 1 <= j <= ntl:
                        turned(j - 1, it)
                    if j < ntl:
                        where_to(j, it, 1)
                    if j >= 2:
                        result(j - 2, it)
                    if j < ntl:
                        where_to(j, it, 2)

                tile(0, 0)
                tile(1, 0)
                tile(2, 0)
                tile(3, 0)
                with dve.Fori(0, (ntl - 8) // 4) as it:
                    for j in range(4):
                        tile(4 + j, it)
                for j in range(ntl - 4, ntl + 2):
                    tile(j, 0)

            dve.memset(vv[:, :, :], 0.0).then_inc(S["setup"], 1)
            dve.memset(acc[:, :], 0.0).then_inc(S["setup"], 1)
            dve.wait_ge(S["setup"], 2)
            dve.memset(vv[:, :, 0:TPS * H * 32].rearrange("p b (h c) -> p b h c", c=32)[:, :, :, HALF + D:HALF + D + 1], 1.0).then_inc(S["setup"], 1)
            dve.wait_ge(S["const"], NCONST)
            ts(cols[:, BQ2S:BQ2S + 1], cols[:, BQ2:BQ2 + 1], float(D) ** -0.5, None, ALU.mult).then_inc(S["setup"], 1)
            dve.wait_ge(S["setup"], 4)
            made = [0]

            def link(ins):
                made[0] += 1
                ins.then_inc(S["pos"], 1)
                dve.wait_ge(S["pos"], made[0])

            link(dve.tensor_reduce(posc[:, 0, :], posr[:, :, :], op=ALU.add, axis=AX.X))
            for a in range(PARTS):
                link(dve.tensor_copy(poscp[:, a, :], posc[:, a, :]))
                if a + 1 < PARTS:
                    link(tt(posc[:, a + 1, :], posc[:, a, :], poscp[:, a, :], ALU.subtract))
            slots(dve, step, 0, 2 * NSEQ)
            mix(0)
            dve.wait_ge(S["pv"], 2 * NSEQ * GROUPS)
            dve.tensor_copy(poscb.rearrange("o a (h t) -> o a h t", h=8),
                            poscp[:, :, :].unsqueeze(3).to_broadcast([1, PARTS, 8, SEQ])).then_inc(S["posb"], 1)
            dve.wait_ge(S["posb"], 1)
            slots(dve, step, 2 * NSEQ, 3 * NSEQ)
            mix(1)

        @block.gpsimd
        def _(pool):
            tt, ts, cp = pool.tensor_tensor, pool.tensor_scalar, pool.tensor_copy

            def rstds(u, first, m, v, r, need, mid, done, shift):
                wait(pool, need, at(2, u, 2, first))
                tt(v[:, :, 1:2], m[:, :, 1:2], eps[:, :].unsqueeze(2), ALU.add).then_inc(S[mid], 1)
                wait(pool, mid, at(1, u, 1, first))
                tt(v[:, :, 0:1], nil[:, :].unsqueeze(2), m[:, :, 0:1], ALU.subtract)
                tt(r[:, :, 0:1], v[:, :, 1:2], half[:, :].unsqueeze(2), ALU.pow).then_inc(S[done], 1)
                wait(pool, done, at(1, u, 1, first))
                tt(r[:, :, 1:2], v[:, :, 0:1], r[:, :, 0:1], ALU.mult).then_inc(S[shift], 1)

            def xz(sl):
                u = sl.unit(OFF_ROUTE, (1, 2))
                if not u:
                    return
                b = u.b % 2
                moved(pool, "scat", u, 2, NSEQ, n=TPS)
                tt(hrow[:, b, :, 2 * C], Fc("tokid")[:, bass.ds(u.s * TPS, TPS)], nil[:, :], ALU.add)
                wait(pool, "zout", at(1, u, 1))
                if u.layer == 1:
                    moved(pool, "resdma", u)
                y = xres[:, b] if u.layer == 1 else nil[:, :].unsqueeze(2).to_broadcast([P, TPS, C])
                tt(hrow[:, b, :, C:2 * C], zb[:, b], y, ALU.add).then_inc(S["xz"], 1)

            def scatter(sl):
                u = sl.unit(OFF_LOGIT, (1, 2))
                if not u:
                    return
                b, d = u.b % 2, hs_d[u.layer - 1]
                wait(pool, "hfin", at(1, u, 1, NSEQ))
                wait(pool, "xz", at(1, u, 1, NSEQ))
                wait(pool, "routing", at(NROUTE, u, NROUTE, NSEQ))
                wait(pool, "tick", at(1, u, 0, NSEQ))
                tt(tick[:, 0:1], nil[:, 0:1], nil[:, 0:1], ALU.add).then_inc(S["tick"], 1)
                for i in range(TPS):
                    pool.indirect_dma_start(d[:, :], bass.IndirectOffsetOnAxis(ap=dest[:, b, i:i + 1], axis=0),
                                            hrow[:, b, i, :], None).then_inc(D_["scat"][b], 16)

            def split_max(sl):
                u = sl.unit(OFF_MAX)
                if not u:
                    return
                b = u.b % 2
                zero_m = nil[:, :].unsqueeze(2).to_broadcast([P, TPS, H])
                wait(pool, "nmax", at(2, u, 2))
                wait(pool, "mt", at(1, u, 0))
                tt(mparts[:, :, 0, :], nmax[:, b], zero_m, ALU.add).then_inc(S["mhi"], 1)
                wait(pool, "mhi", at(1, u, 1))
                tt(mres[:, b], nmax[:, b], mparts[:, :, 0, :], ALU.subtract).then_inc(S["mres"], 1)
                wait(pool, "mres", at(1, u, 1))
                tt(mparts[:, :, 1, :], mres[:, b], zero_m, ALU.add).then_inc(S["mmid"], 1)
                wait(pool, "mmid", at(1, u, 1))
                tt(mparts[:, :, 2, :], mres[:, b], mparts[:, :, 1, :], ALU.subtract).then_inc(S["mlo"], 1)

            def rope_add(sl):
                u = sl.unit(OFF_PROJ, (1,))
                if not u:
                    return
                wait(pool, "rotev", at(1, u, 1, NSEQ))
                wait(pool, "qkev", at(2, u, 2))
                tt(qkf[:, :, :], qkf[:, :, :], qks[:, :, :], ALU.add).then_inc(S["ropeadd"], 1)

            def split(sl):
                u = sl.unit(OFF_PROJ)
                if not u:
                    return
                if u.layer == 1:
                    wait(pool, "ropeadd", at(1, u, 1, NSEQ))
                else:
                    wait(pool, "qkev", at(2, u, 2))
                if u.layer == 0:
                    wait(pool, "sp", at(1, u, 1))
                wait(pool, "hi", at(1, u, 1))
                tt(qkf[:, :, :], qkf[:, :, :], parts[:, 0], ALU.subtract).then_inc(S["resid"], 1)

            def split_rest(sl):
                u = sl.unit(OFF_SPREAD)
                if not u:
                    return
                wait(pool, "mid", at(1, u, 1))
                tt(parts[:, 2], qkf[:, :, :], parts[:, 1], ALU.subtract).then_inc(S["lo"], 1)

            def conv(sl):
                u = sl.unit(OFF_PROJ, (1,))
                if not u:
                    return
                b = u.b % 2
                x, o = xT[:, b, :], cT[:, b, :]
                wait(pool, "xtev", at(1, u, 1))
                wait(pool, "v", at(1, u, -1))
                tt(o, x, convw[:, 2:3].to_broadcast([P, SEQ]), ALU.mult).then_inc(S["tap0"], 1)
                tt(tap[:, 0, :], x, convw[:, 1:2].to_broadcast([P, SEQ]), ALU.mult).then_inc(S["tap1"], 1)
                tt(tap[:, 1, :], x, convw[:, 0:1].to_broadcast([P, SEQ]), ALU.mult).then_inc(S["tap2"], 1)
                wait(pool, "tap0", at(1, u, 1, NSEQ))
                wait(pool, "tap1", at(1, u, 1, NSEQ))
                tt(o[:, 1:SEQ], o[:, 1:SEQ], tap[:, 0, 0:SEQ - 1], ALU.add).then_inc(S["tap3"], 1)
                wait(pool, "tap2", at(1, u, 1, NSEQ))
                wait(pool, "tap3", at(1, u, 1, NSEQ))
                tt(o[:, 2:SEQ], o[:, 2:SEQ], tap[:, 1, 0:SEQ - 2], ALU.add).then_inc(S["conv"], 1)

            def res_bias(sl):
                u = sl.unit(OFF_OUT, (0, 2))
                if not u:
                    return
                moved(pool, "resdma", u)
                x, b = xres[:, u.b % 2], rows[:, BO0 if u.layer == 0 else BO2, :]
                tt(x, x, b.unsqueeze(1).to_broadcast([P, TPS, C]), ALU.add).then_inc(S["rbias"], 1)

            def affine(sl):
                u = sl.unit(OFF_ROUTE, (1,))
                if not u:
                    return
                x = hrow[:, u.b % 2, :, 0:C]
                wait(pool, "hout", at(2, u, 2, NSEQ))
                for name, r, s_ in (("hw", LN2W, ALU.mult), ("hfin", LN2B, ALU.add)):
                    tt(x, x, rows[:, r, :].unsqueeze(1).to_broadcast([P, TPS, C]), s_).then_inc(S[name], 1)
                    if name == "hw":
                        wait(pool, "hw", at(1, u, 1, NSEQ))

            def pads(sl):
                u = sl.unit(OFF_MAX, (0,))
                if not u:
                    return
                wait(pool, "epad", at(1, u, 1))
                e = epad[:, u.b]
                tt(e, e, Fc("pad64").unsqueeze(2).to_broadcast([P, TPS, H]), ALU.mult).then_inc(S["epad64"], 1)

            def step(sl):
                ur, ul = sl.unit(OFF_ROUTE, (1, 2)), sl.unit(OFF_LOAD)
                conv(sl)
                split_rest(sl)
                if ur:
                    b = ur.b % 2
                    rstds(ur, NSEQ, mv3[:, b], rstd3v[:, b], rstd3[:, b], "mvs3", "veps3", "rstds3", "shifts3")
                split_max(sl)
                if ul:
                    rstds(ul, 0, mv[:, ul.b], rstdv[:, ul.b], rstd[:, ul.b], "mvs", "veps", "rstds", "shifts")
                xz(sl)
                pads(sl)
                res_bias(sl)
                affine(sl)
                rope_add(sl)
                if ul and ul.layer == 1:
                    rstds(ul, NSEQ, mv2[:, ul.b], rstd2v[:, ul.b], rstd2[:, ul.b], "mvs2", "veps2", "rstds2", "shifts2")
                split(sl)
                scatter(sl)

            def mix(i):
                m = {k: v[i] for k, v in M.items()}
                ntl = (NTILE0, NTILE1)[i]
                pool.wait_ge(m["fill"], 1)
                for e in range((E0, E1)[i]):
                    pool.indirect_dma_start(hs_d[i][:, :], bass.IndirectOffsetOnAxis(ap=filld[i][:, e:e + 1], axis=0),
                                            zrow[:, :], None, bounds_check=(E0, E1)[i] * REGION + P - 1,
                                            oob_is_err=False).then_inc(m["filled"], 16)
                for j in range(ntl):
                    pool.wait_ge(m["ids"], j + 1)
                    pool.wait_ge(m["yev"], j + 1)
                    pool.indirect_dma_start((x2_d, out)[i][:, :], bass.IndirectOffsetOnAxis(ap=ids[i][:, j:j + 1], axis=0),
                                            yt[:, j % 4, :], None, bounds_check=NSEQ * SEQ - 1,
                                            oob_is_err=False).then_inc(MD["store"][i][j % 4], 16)

            pool.memset(zrow[:, :], 0.0).then_inc(S["zero"], 1)
            pool.memset(half[:, :], -0.5).then_inc(S["half"], 1)
            pool.memset(mparts[:, :, :, :], 0.0).then_inc(S["half"], 1)
            pool.memset(nil[:, :], 0.0).then_inc(S["half"], 1)
            pool.memset(eps[:, :], EPS).then_inc(S["half"], 1)
            pool.wait_ge(S["half"], 4)
            pool.wait_ge(S["zero"], 1)
            for q, (n, d) in enumerate(zip((E0, E1), hs_d)):
                for r in range(0, P, P // TPS):
                    pool.dma_start(d[n * REGION + r:n * REGION + r + P // TPS, :],
                                   zrow[r:r + P // TPS, :]).then_inc(D_["scat"][q], 16)
            pool.wait_ge(S["const"], NCONST)
            slots(pool, step, 0, 2 * NSEQ)
            mix(0)
            slots(pool, step, 2 * NSEQ, 3 * NSEQ)
            mix(1)




def _constants():
    import numpy as np
    bf = mybir.dt.np(mybir.dt.bfloat16)
    far = -1e30
    i, j = np.arange(P)[:, None], np.arange(P)[None, :]
    cf = np.zeros((P, CF["all"]), np.float32)

    def put(dst, where, name, a):
        dst[:, where[name][0]:where[name][1]] = a

    inv = (np.float32(1.0) / np.float32(10000.0) ** (np.arange(0, D, 2, dtype=np.float32) / np.float32(D))).astype(np.float32)
    freqs = (np.arange(SEQ, dtype=np.float32)[:, None] * inv[None, :]).astype(np.float32)
    emb = np.concatenate([freqs, freqs], axis=-1).T
    cos, sin = np.cos(emb), np.sin(emb) * np.where(np.arange(D) < D // 2, 1, -1)[:, None]
    cos, sin = np.repeat(cos, H, axis=0), np.repeat(sin, H, axis=0)
    scale = float(D) ** -0.5
    put(cf, CF, "ident", np.eye(P))
    put(cf, CF, "cosq", cos * scale)
    put(cf, CF, "cosk", cos)
    put(cf, CF, "sinq", sin * scale)
    put(cf, CF, "sink", sin)
    put(cf, CF, "heads", np.arange(P)[:, None] % H == np.arange(H)[None, :])
    tok = np.arange(SEQ).reshape(TPS, P).T
    put(cf, CF, "padfar", np.where((tok < WS) | (tok >= SEQ - WS), 0.0, 1e30))
    put(cf, CF, "pad64", float(WS))
    put(cf, CF, "ones", 1.0)
    put(cf, CF, "eid", np.arange(8)[None, :] - 64.0)
    put(cf, CF, "start", P * np.arange(64)[None, :])
    put(cf, CF, "tokid", P * j[:, 0:NT] + i - OUTSIDE)
    put(cf, CF, "row", i)
    put(cf, CF, "region", REGION * np.arange(8)[None, :])
    cb = np.zeros((P, CB["all"]), bf)
    jb = np.arange(BAND)[None, :]
    band = np.concatenate([np.where(np.abs(jb - i) <= WS, 0, far), np.where((jb >= i) & (jb <= i + 2 * WS), 0, far)], 1)
    put(cb, CB, "ident", np.eye(P))
    put(cb, CB, "band", band)
    put(cb, CB, "causal_q", np.where(j > i, far, 0))
    put(cb, CB, "causal_k", np.where(j < i, far, 0))
    put(cb, CB, "before", i < j)
    put(cb, CB, "ones", 1.0)
    f = (1.0 / 1250.0 ** (np.arange(C // 2, dtype=np.float64) / (C // 2)))[:C // 4].astype(np.float32).astype(np.float64)
    th = np.arange(SEQ)[None, :] * f[:, None]
    ti, tj = np.empty((8, D, SEQ)), np.empty((8, D, SEQ))
    for h in range(8):
        for a in range(4):
            x = th[4 * h + a]
            ti[h, 2 * a], ti[h, 2 * a + 1] = np.cos(x), np.sin(x)
            tj[h, 2 * a], tj[h, 2 * a + 1] = np.cos(x) - np.sin(x), np.cos(x) + np.sin(x)

    def split(a):
        out, r = [], a.astype(np.float32)
        for _ in range(PARTS):
            out.append(r.astype(bf))
            r = r - out[-1].astype(np.float32)
        return out
    pi, pj = split(ti), split(tj)
    trig = np.zeros((2, ROWS, H, SEQ), bf)
    for n, (a, b) in enumerate(PAIRS):
        trig[0, D * n:D * n + D, 0:8] = pi[a].transpose(1, 0, 2)
        trig[1, D * n:D * n + D, 0:8] = pj[b].transpose(1, 0, 2)
    trig[0, 0:PARTS, 8:H] = 1.0
    return cf, cb, trig, np.ones((PARTS, H, SEQ), bf)


def kernel(**inputs):
    import numpy as np
    import concourse.bacc as bacc
    from concourse.bass_utils import run_bass_kernel_spmd

    g = {k: np.asarray(v) for k, v in inputs.items()}
    hd = np.arange(P).reshape(H, D).T.reshape(P)
    oh = np.arange(P).reshape(2, PACK, 4, D).transpose(0, 2, 1, 3).reshape(P)
    wqkv, aw = g["L1_attn_w_qkv"], g["L0_ffn_attn_w"]
    bqkv = g["L1_attn_b_qkv"]
    cf, cb, trig, ones = _constants()
    A, F_ = "L0_attn_", "L0_ffn_"
    ws = [g[A + "wq"].T[:, hd], g[A + "wk"].T[:, hd], g[A + "wv"].T, g[A + "wo"].T[oh],
          aw[:, 0:C][:, hd], aw[:, C:2 * C][:, hd], aw[:, 2 * C:], g[F_ + "proj_w"][oh],
          wqkv[0:C].T[:, hd], wqkv[C:2 * C].T[:, hd], wqkv[2 * C:].T, g["L1_attn_w_proj"].T[oh]]
    arrays = {
        "x": g["L0_attn_x"].reshape(NSEQ * SEQ, C), "cf": cf, "cb": cb, "trig": trig, "onesb": ones,
        "wt": np.stack(ws, axis=1),
        "cols": np.stack([g[A + "bq"][hd], g[A + "bk"][hd], g[F_ + "ln1_w"], g[F_ + "ln1_b"],
                          bqkv[0:C][hd], bqkv[C:2 * C][hd]], axis=1),
        "convw": g[F_ + "conv_w"].reshape(C, 3),
        "rows": np.stack([g[A + "bv"], g[A + "bo"], g[F_ + "ln2_w"], g[F_ + "ln2_b"], bqkv[2 * C:],
                          g["L1_attn_b_proj"]]),
        "wr": np.concatenate([g[F_ + "router_w"], g["L1_ffn_Wr"]], axis=1), "br": g["L1_ffn_br"],
        "up0": g[F_ + "expert_wv"], "dn0": g[F_ + "expert_proj"],
        "up1": g["L1_ffn_W1"], "dn1": g["L1_ffn_W2"], "b1": g["L1_ffn_b1"].reshape(E1 * F1),
        "b2": g["L1_ffn_b2"].reshape(E1 * C), "pos": g["L1_attn_pos_independent"].reshape(1, 8, 8),
    }
    nc = bacc.Bacc("TRN2", target_bir_lowering=False, num_devices=1)
    arrays = {f"in_{k}": np.ascontiguousarray(v) for k, v in arrays.items()}
    t = {k[3:]: nc.dram_tensor(k, v.shape, mybir.dt.from_np(v.dtype), kind="ExternalInput").ap() for k, v in arrays.items()}
    out = nc.dram_tensor("out", (NSEQ * SEQ, C), mybir.dt.float32, kind="ExternalOutput").ap()
    build(nc, t, out)
    r = run_bass_kernel_spmd(nc, [arrays], core_ids=[0])
    return r.results[0]["out"].reshape(NSEQ, SEQ, C)
```
